# Optimizing a Trainium2 kernel written in Bass

```python
import numpy as np
import jax
import jax.numpy as jnp

def _softmax(x, axis=-1):
    return jax.nn.softmax(x, axis=axis)

def _gelu(x):
    return jax.nn.gelu(x, approximate=True)

def _silu(x):
    return jax.nn.silu(x)

def _sigmoid(x):
    return jax.nn.sigmoid(x)

def _layernorm(x, axis=-1, eps=1e-05):
    m = jnp.mean(x, axis=axis, keepdims=True)
    v = jnp.var(x, axis=axis, keepdims=True)
    return (x - m) / jnp.sqrt(v + eps)

def _scatter_add(tgt, idx, src, axis=0):
    return tgt.at[idx].add(src)

def _segment_sum(src, seg, n):
    return jax.ops.segment_sum(src, seg, n)
kernel_name = 'mk_decoder_postln_d2_seqx_r8_d9cfad'

def setup_inputs(seed: int=0):
    np.random.seed(seed)
    _w = jnp.asarray

    def _rec_inputs():
        import jax
        import jax.numpy as jnp
        _rk = jax.random.key(seed)
        x = -0.0005207 + 1.001 * jax.random.normal(jax.random.fold_in(_rk, 1), (8, 128, 128), jnp.float32)
        _lenS = 128 - jax.random.randint(jax.random.fold_in(_rk, 7), (8,), 0, max(1, 128 // 4) + 1, jnp.int32)
        _lenS2 = 120 - jax.random.randint(jax.random.fold_in(_rk, 8), (8,), 0, max(1, 120 // 4) + 1, jnp.int32)
        _ctx_1024P = jax.random.normal(jax.random.fold_in(_rk, 11), (8, 16, 128), jnp.float32)
        _ctx_1024c = jax.random.dirichlet(jax.random.fold_in(_rk, 511), 0.3 * jnp.ones((16,), jnp.float32), (8, 120))
        _ctx_1024t = jnp.einsum('bsk,bkd->bsd', _ctx_1024c, _ctx_1024P)
        _ctx_1024t = _ctx_1024t * jax.lax.rsqrt(jnp.mean(jnp.square(_ctx_1024t)) + 1e-12) * 0.953939
        ctx_1024 = 2.81802e-05 + 1.00001 * (_ctx_1024t + 0.3 * jax.random.normal(jax.random.fold_in(_rk, 611), (8, 120, 128), jnp.float32))
        return (x, ctx_1024)
    x, ctx_1024 = _rec_inputs()

    def _L0_attn_setup():
        import jax, jax.numpy as jnp
        import numpy as np
        DIM = 128
        H = 16
        DH = DIM // H

        def _l2norm(a):
            n = jnp.linalg.norm(a, axis=-1, keepdims=True)
            return a / jnp.maximum(n, 1e-12)
        key = jax.random.key(seed)
        ks = jax.random.split(key, 6)
        B, T = (4, 512)
        s = 0.02
        return {'x': jax.random.normal(ks[0], (B, T, DIM), jnp.float32), 'Wqkv': jax.random.normal(ks[1], (3 * DIM, DIM), jnp.float32) * s, 'Wg': jax.random.normal(ks[2], (H, DIM), jnp.float32) * s, 'bg': jnp.zeros((H,), jnp.float32), 'Wb': jax.random.normal(ks[3], (H, DIM), jnp.float32) * s, 'bb': jnp.zeros((H,), jnp.float32), 'Wout': jax.random.normal(ks[4], (DIM, DIM), jnp.float32) * s}
    _L0_attn_all = _L0_attn_setup()
    _L0_attn_in = {k: v for k, v in _L0_attn_all.items() if k in ('Wqkv', 'Wg', 'bg', 'Wb', 'bb', 'Wout')}
    del _L0_attn_all

    def _L0_xattn_setup():
        import jax, jax.numpy as jnp
        import numpy as np
        E = 128
        H = 16
        D = E // H
        key = jax.random.key(seed)
        ks = jax.random.split(key, 12)
        B, Tq, Tk = (2, 128, 1024)
        s = 0.02
        return {'hidden_states': jax.random.normal(ks[0], (B, Tq, E), jnp.float32), 'key_value_states': jax.random.normal(ks[1], (B, Tk, E), jnp.float32), 'Wq': jax.random.normal(ks[2], (E, E), jnp.float32) * s, 'bq': jnp.zeros((E,), jnp.float32), 'Wk': jax.random.normal(ks[3], (E, E), jnp.float32) * s, 'bk': jnp.zeros((E,), jnp.float32), 'Wv': jax.random.normal(ks[4], (E, E), jnp.float32) * s, 'bv': jnp.zeros((E,), jnp.float32), 'Wo': jax.random.normal(ks[5], (E, E), jnp.float32) * s, 'bo': jnp.zeros((E,), jnp.float32), 'stride': 16}
    _L0_xattn_all = _L0_xattn_setup()
    _L0_xattn_in = {k: v for k, v in _L0_xattn_all.items() if k in ('Wq', 'bq', 'Wk', 'bk', 'Wv', 'bv', 'Wo', 'bo')}
    del _L0_xattn_all

    def _L0_ffn_setup():
        import jax, jax.numpy as jnp
        import numpy as np
        B, S, D_MODEL, D_FF = (4, 256, 128, 512)

        def _quantum_transform(hidden, theta, w_real, w_imag):
            imag = w_imag * jnp.sin(theta + hidden * 0.1)
            quantum_phase = jnp.cos(theta) * w_real + jnp.sin(theta) * w_imag
            return hidden + quantum_phase * imag * 0.1
        key = jax.random.key(seed)
        ks = jax.random.split(key, 8)
        return {'x': jax.random.normal(ks[0], (B, S, D_MODEL), dtype=jnp.float32), 'W1': jax.random.normal(ks[1], (D_MODEL, D_FF), dtype=jnp.float32) * (1.0 / np.sqrt(D_MODEL)), 'b1': jnp.zeros((D_FF,), dtype=jnp.float32), 'quantum_phases': jax.random.normal(ks[2], (D_FF,), dtype=jnp.float32) * (2.0 * np.pi), 'quantum_weights_real': jax.random.normal(ks[3], (D_FF,), dtype=jnp.float32) * 0.1, 'quantum_weights_imag': jax.random.normal(ks[4], (D_FF,), dtype=jnp.float32) * 0.1, 'W2': jax.random.normal(ks[5], (D_FF, D_MODEL), dtype=jnp.float32) * (1.0 / np.sqrt(D_FF)), 'b2': jnp.zeros((D_MODEL,), dtype=jnp.float32)}
    _L0_ffn_all = _L0_ffn_setup()
    _L0_ffn_in = {k: v for k, v in _L0_ffn_all.items() if k in ('W1', 'b1', 'quantum_phases', 'quantum_weights_real', 'quantum_weights_imag', 'W2', 'b2')}
    del _L0_ffn_all

    def _L1_attn_setup():
        import jax, jax.numpy as jnp
        import numpy as np
        D_MODEL = 128
        D_STATE = 16
        EXPAND = 2
        D_INNER = EXPAND * D_MODEL
        BATCH = 8
        SEQ = 256

        def _linear_init(key, fan_in, shape):
            bound = 1.0 / np.sqrt(fan_in)
            return jax.random.uniform(key, shape, jnp.float32, -bound, bound)

        def _silu(v):
            return v * jax.nn.sigmoid(v)
        key = jax.random.key(seed)
        ks = jax.random.split(key, 9)
        x = jax.random.normal(ks[0], (BATCH, SEQ, D_MODEL), jnp.float32)
        W_in = _linear_init(ks[1], D_MODEL, (D_MODEL, 2 * D_INNER))
        b_in = _linear_init(ks[2], D_MODEL, (2 * D_INNER,))
        W_x = _linear_init(ks[3], D_INNER, (D_INNER, 2 * D_STATE))
        b_x = _linear_init(ks[4], D_INNER, (2 * D_STATE,))
        W_dt = _linear_init(ks[5], D_INNER, (D_INNER, D_INNER))
        b_dt = _linear_init(ks[6], D_INNER, (D_INNER,))
        W_out = _linear_init(ks[7], D_INNER, (D_INNER, D_MODEL))
        b_out = _linear_init(ks[8], D_INNER, (D_MODEL,))
        A = jnp.tile(jnp.arange(1, D_STATE + 1, dtype=jnp.float32), (D_INNER, 1))
        A_log = jnp.log(A)
        D_param = jnp.ones((D_INNER,), jnp.float32)
        return dict(x=x, W_in=W_in, b_in=b_in, W_x=W_x, b_x=b_x, W_dt=W_dt, b_dt=b_dt, W_out=W_out, b_out=b_out, A_log=A_log, D_param=D_param)
    _L1_attn_all = _L1_attn_setup()
    _L1_attn_in = {k: v for k, v in _L1_attn_all.items() if k in ('W_in', 'b_in', 'W_x', 'b_x', 'W_dt', 'b_dt', 'W_out', 'b_out', 'A_log', 'D_param')}
    del _L1_attn_all

    def _L1_xattn_setup():
        import jax, jax.numpy as jnp
        import numpy as np
        B, M, N, DIM, DH, H = (8, 512, 64, 128, 128, 8)
        INNER = DH * H
        EPS = 1e-05

        def _layernorm(x, g, b):
            mu = jnp.mean(x, axis=-1, keepdims=True)
            var = jnp.var(x, axis=-1, keepdims=True)
            return (x - mu) * jax.lax.rsqrt(var + EPS) * g + b
        key = jax.random.key(seed)
        ks = jax.random.split(key, 8)
        sd = 0.02
        return {'x': jax.random.normal(ks[0], (B, M, DIM), jnp.float32), 'latents': jax.random.normal(ks[1], (B, N, DIM), jnp.float32), 'gamma_media': jnp.ones((DIM,), jnp.float32), 'beta_media': jnp.zeros((DIM,), jnp.float32), 'gamma_lat': jnp.ones((DIM,), jnp.float32), 'beta_lat': jnp.zeros((DIM,), jnp.float32), 'Wq': jax.random.normal(ks[2], (DIM, INNER), jnp.float32) * sd, 'bq': jnp.zeros((INNER,), jnp.float32), 'Wkv': jax.random.normal(ks[3], (DIM, 2 * INNER), jnp.float32) * sd, 'bkv': jnp.zeros((2 * INNER,), jnp.float32), 'Wo': jax.random.normal(ks[4], (INNER, DIM), jnp.float32) * sd, 'bo': jnp.zeros((DIM,), jnp.float32)}
    _L1_xattn_all = _L1_xattn_setup()
    _L1_xattn_in = {k: v for k, v in _L1_xattn_all.items() if k in ('gamma_media', 'beta_media', 'gamma_lat', 'beta_lat', 'Wq', 'bq', 'Wkv', 'bkv', 'Wo', 'bo')}
    del _L1_xattn_all

    def _L1_ffn_setup():
        import jax, jax.numpy as jnp
        import numpy as np
        DIM = 128

        def _reference_tuple_inner(x, W_r, W_k, W_v, mu_r, mu_k):
            B, T, C = x.shape
            x_prev = jnp.concatenate([jnp.zeros((B, 1, C), x.dtype), x[:, :-1, :]], axis=1)
            xr = mu_r * x + (1.0 - mu_r) * x_prev
            xk = mu_k * x + (1.0 - mu_k) * x_prev
            r = jax.nn.sigmoid(jnp.einsum('btc,dc->btd', xr, W_r))
            k = jnp.einsum('btc,dc->btd', xk, W_k)
            k_act = jnp.square(jax.nn.relu(k))
            out = r * jnp.einsum('btc,dc->btd', k_act, W_v)
            new_state = x[:, -1, :]
            return (out, new_state)
        key = jax.random.key(seed)
        ks = jax.random.split(key, 6)
        B, T, C = (8, 256, DIM)
        x = jax.random.normal(ks[0], (B, T, C), dtype=jnp.float32)
        s = 1.0 / np.sqrt(C)
        W_r = jax.random.uniform(ks[1], (C, C), jnp.float32, -s, s)
        W_k = jax.random.uniform(ks[2], (C, C), jnp.float32, -s, s)
        W_v = jax.random.uniform(ks[3], (C, C), jnp.float32, -s, s)
        mu_r = jax.random.uniform(ks[4], (C,), jnp.float32)
        mu_k = jax.random.uniform(ks[5], (C,), jnp.float32)
        return {'x': x, 'W_r': W_r, 'W_k': W_k, 'W_v': W_v, 'mu_r': mu_r, 'mu_k': mu_k}
    _L1_ffn_all = _L1_ffn_setup()
    _L1_ffn_in = {k: v for k, v in _L1_ffn_all.items() if k in ('W_r', 'W_k', 'W_v', 'mu_r', 'mu_k')}
    del _L1_ffn_all
    return {'x': x, 'ctx_1024': ctx_1024, 'L0_attn_Wqkv': _L0_attn_in['Wqkv'], 'L0_attn_Wg': _L0_attn_in['Wg'], 'L0_attn_bg': _L0_attn_in['bg'], 'L0_attn_Wb': _L0_attn_in['Wb'], 'L0_attn_bb': _L0_attn_in['bb'], 'L0_attn_Wout': _L0_attn_in['Wout'], 'L0_xattn_Wq': _L0_xattn_in['Wq'], 'L0_xattn_bq': _L0_xattn_in['bq'], 'L0_xattn_Wk': _L0_xattn_in['Wk'], 'L0_xattn_bk': _L0_xattn_in['bk'], 'L0_xattn_Wv': _L0_xattn_in['Wv'], 'L0_xattn_bv': _L0_xattn_in['bv'], 'L0_xattn_Wo': _L0_xattn_in['Wo'], 'L0_xattn_bo': _L0_xattn_in['bo'], 'L0_ffn_W1': _L0_ffn_in['W1'], 'L0_ffn_b1': _L0_ffn_in['b1'], 'L0_ffn_quantum_phases': _L0_ffn_in['quantum_phases'], 'L0_ffn_quantum_weights_real': _L0_ffn_in['quantum_weights_real'], 'L0_ffn_quantum_weights_imag': _L0_ffn_in['quantum_weights_imag'], 'L0_ffn_W2': _L0_ffn_in['W2'], 'L0_ffn_b2': _L0_ffn_in['b2'], 'L1_attn_W_in': _L1_attn_in['W_in'], 'L1_attn_b_in': _L1_attn_in['b_in'], 'L1_attn_W_x': _L1_attn_in['W_x'], 'L1_attn_b_x': _L1_attn_in['b_x'], 'L1_attn_W_dt': _L1_attn_in['W_dt'], 'L1_attn_b_dt': _L1_attn_in['b_dt'], 'L1_attn_W_out': _L1_attn_in['W_out'], 'L1_attn_b_out': _L1_attn_in['b_out'], 'L1_attn_A_log': _L1_attn_in['A_log'], 'L1_attn_D_param': _L1_attn_in['D_param'], 'L1_xattn_gamma_media': _L1_xattn_in['gamma_media'], 'L1_xattn_beta_media': _L1_xattn_in['beta_media'], 'L1_xattn_gamma_lat': _L1_xattn_in['gamma_lat'], 'L1_xattn_beta_lat': _L1_xattn_in['beta_lat'], 'L1_xattn_Wq': _L1_xattn_in['Wq'], 'L1_xattn_bq': _L1_xattn_in['bq'], 'L1_xattn_Wkv': _L1_xattn_in['Wkv'], 'L1_xattn_bkv': _L1_xattn_in['bkv'], 'L1_xattn_Wo': _L1_xattn_in['Wo'], 'L1_xattn_bo': _L1_xattn_in['bo'], 'L1_ffn_W_r': _L1_ffn_in['W_r'], 'L1_ffn_W_k': _L1_ffn_in['W_k'], 'L1_ffn_W_v': _L1_ffn_in['W_v'], 'L1_ffn_mu_r': _L1_ffn_in['mu_r'], 'L1_ffn_mu_k': _L1_ffn_in['mu_k']}

def reference(x, ctx_1024, L0_attn_Wqkv, L0_attn_Wg, L0_attn_bg, L0_attn_Wb, L0_attn_bb, L0_attn_Wout, L0_xattn_Wq, L0_xattn_bq, L0_xattn_Wk, L0_xattn_bk, L0_xattn_Wv, L0_xattn_bv, L0_xattn_Wo, L0_xattn_bo, L0_ffn_W1, L0_ffn_b1, L0_ffn_quantum_phases, L0_ffn_quantum_weights_real, L0_ffn_quantum_weights_imag, L0_ffn_W2, L0_ffn_b2, L1_attn_W_in, L1_attn_b_in, L1_attn_W_x, L1_attn_b_x, L1_attn_W_dt, L1_attn_b_dt, L1_attn_W_out, L1_attn_b_out, L1_attn_A_log, L1_attn_D_param, L1_xattn_gamma_media, L1_xattn_beta_media, L1_xattn_gamma_lat, L1_xattn_beta_lat, L1_xattn_Wq, L1_xattn_bq, L1_xattn_Wkv, L1_xattn_bkv, L1_xattn_Wo, L1_xattn_bo, L1_ffn_W_r, L1_ffn_W_k, L1_ffn_W_v, L1_ffn_mu_r, L1_ffn_mu_k):
    import jax
    import jax.numpy as jnp

    def _L0_attn_ref(x, Wqkv, Wg, bg, Wb, bb, Wout):
        import jax, jax.numpy as jnp
        import numpy as np
        DIM = 128
        H = 16
        DH = DIM // H

        def _l2norm(a):
            n = jnp.linalg.norm(a, axis=-1, keepdims=True)
            return a / jnp.maximum(n, 1e-12)
        B, T, D = x.shape
        qkv = (x @ Wqkv.T).reshape(B, T, 3, H, DH)
        q = _l2norm(qkv[:, :, 0])
        k = _l2norm(qkv[:, :, 1])
        v = qkv[:, :, 2]
        alpha = jax.nn.sigmoid(x @ Wg.T + bg)
        beta = jax.nn.sigmoid(x @ Wb.T + bb)
        qT = jnp.moveaxis(q, 1, 0)
        kT = jnp.moveaxis(k, 1, 0)
        vT = jnp.moveaxis(v, 1, 0)
        aT = jnp.moveaxis(alpha, 1, 0)
        bT = jnp.moveaxis(beta, 1, 0)
        S0 = jnp.zeros((B, H, DH, DH), jnp.float32)

        def step(S, inp):
            q_t, k_t, v_t, a_t, b_t = inp
            Sk = jnp.einsum('bhij,bhj->bhi', S, k_t)
            a = a_t[..., None, None]
            b = b_t[..., None, None]
            S = a * (S - b * Sk[..., :, None] * k_t[..., None, :]) + b * v_t[..., :, None] * k_t[..., None, :]
            o = jnp.einsum('bhij,bhj->bhi', S, q_t)
            return (S, o)
        _, outs = jax.lax.scan(step, S0, (qT, kT, vT, aT, bT))
        out = jnp.moveaxis(outs, 0, 1).reshape(B, T, D)
        return out @ Wout.T

    def _L0_xattn_ref(hidden_states, key_value_states, Wq, bq, Wk, bk, Wv, bv, Wo, bo, stride):
        import jax, jax.numpy as jnp
        import numpy as np
        E = 128
        H = 16
        D = E // H
        B, Tq, _ = hidden_states.shape
        Tk = key_value_states.shape[1]
        scaling = D ** (-0.5)
        Q = (hidden_states @ Wq.T + bq).reshape(B, Tq, H, D).transpose(0, 2, 1, 3)
        K = (key_value_states @ Wk.T + bk).reshape(B, Tk, H, D).transpose(0, 2, 1, 3)
        V = (key_value_states @ Wv.T + bv).reshape(B, Tk, H, D).transpose(0, 2, 1, 3)
        m = Tk // stride
        idx = jnp.arange(H)[:, None] + stride * jnp.arange(m)[None, :]
        gather = idx[None, :, :, None]
        Kg = jnp.take_along_axis(K, gather, axis=2)
        Vg = jnp.take_along_axis(V, gather, axis=2)
        scores = jnp.einsum('bhqd,bhkd->bhqk', Q, Kg) * scaling
        attn = jax.nn.softmax(scores, axis=-1)
        out = jnp.einsum('bhqk,bhkd->bhqd', attn, Vg)
        out = out.transpose(0, 2, 1, 3).reshape(B, Tq, E)
        return out @ Wo.T + bo

    def _L0_ffn_ref(x, W1, b1, quantum_phases, quantum_weights_real, quantum_weights_imag, W2, b2):
        import jax, jax.numpy as jnp
        import numpy as np
        B, S, D_MODEL, D_FF = (4, 256, 128, 512)

        def _quantum_transform(hidden, theta, w_real, w_imag):
            imag = w_imag * jnp.sin(theta + hidden * 0.1)
            quantum_phase = jnp.cos(theta) * w_real + jnp.sin(theta) * w_imag
            return hidden + quantum_phase * imag * 0.1
        hidden = jnp.einsum('bsd,df->bsf', x, W1) + b1
        q = _quantum_transform(hidden, quantum_phases, quantum_weights_real, quantum_weights_imag)
        act = jax.nn.relu(q)
        return jnp.einsum('bsf,fd->bsd', act, W2) + b2

    def _L1_attn_ref(x, W_in, b_in, W_x, b_x, W_dt, b_dt, W_out, b_out, A_log, D_param):
        import jax, jax.numpy as jnp
        import numpy as np
        D_MODEL = 128
        D_STATE = 16
        EXPAND = 2
        D_INNER = EXPAND * D_MODEL
        BATCH = 8
        SEQ = 256

        def _linear_init(key, fan_in, shape):
            bound = 1.0 / np.sqrt(fan_in)
            return jax.random.uniform(key, shape, jnp.float32, -bound, bound)

        def _silu(v):
            return v * jax.nn.sigmoid(v)
        xz = x @ W_in + b_in
        x_proj, z = jnp.split(xz, 2, axis=-1)
        u = _silu(x_proj)
        A = -jnp.exp(A_log)
        x_dbl = u @ W_x + b_x
        Bm, Cm = jnp.split(x_dbl, 2, axis=-1)
        dt = jax.nn.softplus(u @ W_dt + b_dt)
        uT = jnp.swapaxes(u, 0, 1)
        dtT = jnp.swapaxes(dt, 0, 1)
        BT = jnp.swapaxes(Bm, 0, 1)
        CT = jnp.swapaxes(Cm, 0, 1)

        def step(h, inp):
            u_t, dt_t, B_t, C_t = inp
            dA = jnp.exp(dt_t[..., None] * A)
            h = h * dA + (dt_t * u_t)[..., None] * B_t[:, None, :]
            y_t = jnp.einsum('bds,bs->bd', h, C_t) + D_param * u_t
            return (h, y_t)
        h0 = jnp.zeros((x.shape[0], D_INNER, D_STATE), x.dtype)
        _, yT = jax.lax.scan(step, h0, (uT, dtT, BT, CT))
        y = jnp.swapaxes(yT, 0, 1)
        y = y * _silu(z)
        return y @ W_out + b_out

    def _L1_xattn_ref(x, latents, gamma_media, beta_media, gamma_lat, beta_lat, Wq, bq, Wkv, bkv, Wo, bo):
        import jax, jax.numpy as jnp
        import numpy as np
        B, M, N, DIM, DH, H = (8, 512, 64, 128, 128, 8)
        INNER = DH * H
        EPS = 1e-05

        def _layernorm(x, g, b):
            mu = jnp.mean(x, axis=-1, keepdims=True)
            var = jnp.var(x, axis=-1, keepdims=True)
            return (x - mu) * jax.lax.rsqrt(var + EPS) * g + b
        b = x.shape[0]
        xn = _layernorm(x, gamma_media, beta_media)
        ln = _layernorm(latents, gamma_lat, beta_lat)
        q = ln @ Wq + bq
        kv_input = jnp.concatenate([xn, ln], axis=1)
        kv = kv_input @ Wkv + bkv
        k, v = jnp.split(kv, 2, axis=-1)

        def to_heads(t):
            return t.reshape(b, t.shape[1], H, DH).transpose(0, 2, 1, 3)
        q, k, v = (to_heads(q), to_heads(k), to_heads(v))
        q = q * DH ** (-0.5)
        sim = jnp.einsum('bhid,bhjd->bhij', q, k)
        attn = jax.nn.softmax(sim, axis=-1)
        out = jnp.einsum('bhij,bhjd->bhid', attn, v)
        out = out.transpose(0, 2, 1, 3).reshape(b, -1, INNER)
        return out @ Wo + bo

    def _L1_ffn_ref(x, W_r, W_k, W_v, mu_r, mu_k):
        import jax, jax.numpy as jnp
        import numpy as np
        DIM = 128

        def _reference_tuple_inner(x, W_r, W_k, W_v, mu_r, mu_k):
            B, T, C = x.shape
            x_prev = jnp.concatenate([jnp.zeros((B, 1, C), x.dtype), x[:, :-1, :]], axis=1)
            xr = mu_r * x + (1.0 - mu_r) * x_prev
            xk = mu_k * x + (1.0 - mu_k) * x_prev
            r = jax.nn.sigmoid(jnp.einsum('btc,dc->btd', xr, W_r))
            k = jnp.einsum('btc,dc->btd', xk, W_k)
            k_act = jnp.square(jax.nn.relu(k))
            out = r * jnp.einsum('btc,dc->btd', k_act, W_v)
            new_state = x[:, -1, :]
            return (out, new_state)
        return _reference_tuple_inner(x, W_r, W_k, W_v, mu_r, mu_k)[0]
    x = _layernorm(x + _L0_attn_ref(x, L0_attn_Wqkv, L0_attn_Wg, L0_attn_bg, L0_attn_Wb, L0_attn_bb, L0_attn_Wout), axis=-1)
    x = _layernorm(x + _L0_xattn_ref(x, ctx_1024, L0_xattn_Wq, L0_xattn_bq, L0_xattn_Wk, L0_xattn_bk, L0_xattn_Wv, L0_xattn_bv, L0_xattn_Wo, L0_xattn_bo, 16), axis=-1)
    x = _layernorm(x + _L0_ffn_ref(x, L0_ffn_W1, L0_ffn_b1, L0_ffn_quantum_phases, L0_ffn_quantum_weights_real, L0_ffn_quantum_weights_imag, L0_ffn_W2, L0_ffn_b2), axis=-1)
    x = _layernorm(x + _L1_attn_ref(x, L1_attn_W_in, L1_attn_b_in, L1_attn_W_x, L1_attn_b_x, L1_attn_W_dt, L1_attn_b_dt, L1_attn_W_out, L1_attn_b_out, L1_attn_A_log, L1_attn_D_param), axis=-1)
    x = _layernorm(x + _L1_xattn_ref(ctx_1024, x, L1_xattn_gamma_media, L1_xattn_beta_media, L1_xattn_gamma_lat, L1_xattn_beta_lat, L1_xattn_Wq, L1_xattn_bq, L1_xattn_Wkv, L1_xattn_bkv, L1_xattn_Wo, L1_xattn_bo), axis=-1)
    x = _layernorm(x + _L1_ffn_ref(x, L1_ffn_W_r, L1_ffn_W_k, L1_ffn_W_v, L1_ffn_mu_r, L1_ffn_mu_k), axis=-1)
    return x

_drawn_inputs = setup_inputs


def setup_inputs(seed=0):
    import zlib

    import numpy as np

    out = dict(_drawn_inputs(seed))
    spreads = {'L0_attn_bg': (0.0, 0.8),
     'L0_attn_bb': (0.0, 0.8),
     'L0_xattn_bq': (0.0, 2.0),
     'L0_xattn_bk': (0.0, 2.0),
     'L0_xattn_bv': (0.0, 0.38),
     'L0_xattn_bo': (0.0, 0.1),
     'L0_ffn_b1': (0.0, 0.1),
     'L0_ffn_b2': (0.0, 0.1),
     'L1_attn_D_param': (1.0, 0.6),
     'L1_xattn_gamma_media': (1.0, 0.6),
     'L1_xattn_beta_media': (0.0, 0.8),
     'L1_xattn_gamma_lat': (1.0, 0.6),
     'L1_xattn_beta_lat': (0.0, 0.8),
     'L1_xattn_bq': (0.0, 2.0),
     'L1_xattn_bkv': (0.0, 0.1),
     'L1_xattn_bo': (0.0, 0.1)}
    factors = {'L0_attn_Wqkv': 5.388,
     'L0_attn_Wg': 8.0,
     'L0_attn_Wb': 8.0,
     'L0_attn_Wout': 5.246,
     'L0_xattn_Wq': 8.0,
     'L0_xattn_Wk': 8.0,
     'L0_ffn_quantum_phases': 8.0,
     'L0_ffn_quantum_weights_real': 8.0,
     'L0_ffn_quantum_weights_imag': 8.0,
     'L1_attn_b_in': 7.072,
     'L1_attn_W_x': 8.0,
     'L1_attn_b_x': 8.0,
     'L1_attn_W_dt': 8.0,
     'L1_attn_b_dt': 8.0,
     'L1_attn_A_log': 8.0,
     'L1_xattn_Wq': 8.0,
     'L1_ffn_W_r': 2.871,
     'L1_ffn_mu_r': 6.47}
    for name, (base, spread) in spreads.items():
        noise = np.random.default_rng([zlib.crc32(name.encode()), seed]).standard_normal(out[name].shape)
        drawn = base * np.exp(spread * noise) if base else spread * noise
        out[name] = jnp.asarray(drawn.astype(out[name].dtype))
    for name, factor in factors.items():
        out[name] = (out[name] * factor).astype(out[name].dtype)
    return out
```

```python
from contextlib import ExitStack

import numpy as np
import concourse.bass as bass
from concourse import mybir

F32 = mybir.dt.float32
BF16 = mybir.dt.bfloat16
I32 = mybir.dt.int32
ALU = mybir.AluOpType
ACT = mybir.ActivationFunctionType
AX = mybir.AxisListType

P = 128
B, T, D = 8, 128, 128
BT = B * T
HB = B // 2
BANK = 512
H, DH = 16, 8
C = 8
NC = T // C
TC = 120
NM = TC // 16
NK = NM * 16
FF = 512
NF = FF // P
DI = 256
NH = DI // P
NS = 16
XH = 8
KV = TC + T
EPS = 1e-5
TWO_PI = float(2 * np.pi)
PI_F = float(np.nextafter(np.float32(np.pi), np.float32(0)))
ROUND = 1.5 * 2.0 ** 23
LOG1P_SERIES = 2.0 ** -7

PACKS = {
    "first": [("xT", BT), ("w_qkvgb", 3 * D + 2 * H), ("gate_bias", 2), ("ident", P)],
    "early": [("w_out0", D), ("wq0", D), ("wk0", D), ("wv0", D), ("wo0", D), ("bq0", 1), ("bk0", 1),
              ("bv0", 1), ("mask_k", NK), ("mask_v", D), ("ctxT", B * TC)],
    "fold": [("wq1T", XH * D), ("wk1T", XH * D), ("wv1T", XH * D), ("wo1", XH * D), ("bq1", XH), ("bv1", XH)],
    "late": [("w1", FF), ("b1", NF), ("theta", NF), ("w_re", NF), ("w_im", NF), ("w2", NF * D), ("w_in", 2 * DI),
             ("b_in", 2 * NH), ("w_x", NH * 2 * NS), ("w_dt", NH * DI), ("b_dt", NH), ("w_out", NH * D),
             ("a_log", NH * NS), ("d_skip", NH), ("b_x", 1), ("g_med", 1), ("be_med", 1), ("g_lat", 1), ("be_lat", 1),
             ("w_r", D), ("w_k", D), ("w_v", D), ("mu_r", 1), ("mu_k", 1),
             ("pick", 2 * NS)],
}
ROWS = ["bo0", "b2", "b_out", "bo1", "g_med", "be_med", "g_lat", "be_lat"]


def columns(pack):
    at, out = 0, {}
    for name, n in PACKS[pack]:
        out[name] = (at, n)
        at += n
    return out, at


def decoder(nc, first, x, early, context, fold, late, rows, out):
    with ExitStack() as ctx:
        sems = {}

        def S(name):
            if name not in sems:
                sems[name] = ctx.enter_context(nc.semaphore(name))
            return sems[name]

        def sb(name, shape, dt=F32):
            return ctx.enter_context(nc.sbuf_tensor(name, shape, dt))

        where, tiles = {}, {}
        for pack in PACKS:
            cols, n = columns(pack)
            tiles[pack] = sb(f"{pack}_in", [P, n])
            for name, (at, w) in cols.items():
                where[name] = (pack, at, w)

        def W(name):
            pack, at, w = where[name]
            return tiles[pack][:, at:at + w]

        row_in = sb("rows_in", [P, len(ROWS), D])
        pick = sb("pick_wide", [3 * 2 * NS, 2 * NS, P], BF16)
        ident = W("ident")

        xrow = sb("xrow", [P, 2, B, D])
        xres = sb("xres", [P, B, D])
        xcol = sb("xcol", [P, B, T])
        key0 = sb("key0", [P, B, NK])
        val0 = sb("val0", [P, B, D])
        kvT = sb("kvT", [P, B, KV])
        kv_ctx = sb("kv_ctx", [P, B, D])
        kv_lat = sb("kv_lat", [P, B, D])
        fold_qk = sb("fold_qk", [P, XH, D])
        fold_vo = sb("fold_vo", [P, XH, D])
        fold_bq = sb("fold_bq", [P, XH])
        fold_bo = sb("fold_bo", [P, D])
        stats = sb("stats", [P, B, 6])
        mv = sb("mv", [P, B, 2])
        veps = sb("veps", [P, B])
        rstd = sb("rstd", [P, B])
        cstats = sb("cstats", [P, B, 6])
        cmv = sb("cmv", [P, B, 2])
        cveps = sb("cveps", [P, B])
        crstd = sb("crstd", [P, B])
        mhalf = sb("mhalf", [P, B])
        arena = sb("arena", [P, 27000])
        ps = ctx.enter_context(nc.psum_tensor("ps", [P, 8 * BANK], F32))

        NORMS = [1, 2, 3, 4, 7, 5, 6]

        def normed(n, k=B):
            return NORMS.index(n) * B + k

        def nth(n):
            return NORMS.index(n) + 1

        class Arena:
            def __init__(self):
                self.at = 0

            def __call__(self, n):
                self.at += n
                assert self.at <= arena.shape[1], self.at
                return arena[:, self.at - n:self.at]

        def bank(k, n=1):
            return ps[:, k * BANK:(k + n) * BANK]

        def rows_of(ap):
            return ap.rearrange("p (b c) -> p b c", b=B)

        A = Arena()
        qkvt = A(B * (3 * D + 2 * H)).rearrange("p (n b h) -> p n b h", b=B, h=H)
        square = A(2 * T * DH)
        end = A.at
        A.at = 0
        sub_t = A(NC * 2 * DH * C)
        sub_r = A(NC * 2 * DH).rearrange("p (c n) -> p c n", n=2 * DH)
        ch_t = A(2 * C * DH * DH)
        ch_r = A(C * DH)
        ch_r2 = A(DH * DH)
        Kend = A(T * DH).rearrange("p (c t j) -> p c t j", t=C, j=DH)
        assert A.at <= end
        A.at = end
        norm2 = A(2 * T)
        inv = A(2 * T)
        K = A(T * DH).rearrange("p (t j) -> p t j", j=DH)
        Q = A(T * DH).rearrange("p (t j) -> p t j", j=DH)
        gates = A(2 * T)
        decay = A(T * C).rearrange("p (c t i) -> p c t i", t=C, i=C)
        bdecay = A(T * C).rearrange("p (c t i) -> p c t i", t=C, i=C)
        gcum = A(T).rearrange("p (c t) -> p c t", t=C)
        bgcum = A(T).rearrange("p (c t) -> p c t", t=C)
        low = A(T * C).rearrange("p (c t i) -> p c t i", t=C, i=C)
        att = A(T * C).rearrange("p (c t i) -> p c t i", t=C, i=C)
        X = A(T * 2 * DH).rearrange("p (c t n) -> p c t n", t=C, n=2 * DH)
        U = A(T * DH).rearrange("p (c t i) -> p c t i", t=C, i=DH)
        state = A(NC * DH * DH).rearrange("p (c i j) -> p c i j", i=DH, j=DH)
        Qg = A(T * DH).rearrange("p (c t j) -> p c t j", t=C, j=DH)
        NR = NC // 2
        NQ = NC // 4
        gram = A.at
        prod_o = A(2 * NR * DH * C * DH)
        gram_k = arena[:, gram:gram + NC * DH * C * (C - 1) // 2]
        gram_q = arena[:, gram + NC * DH * C * (C - 1) // 2:gram + NC * DH * C * C]
        osb, ot = K.rearrange("p t j -> p (t j)"), Q.rearrange("p t j -> p (t j)")
        otT = low.rearrange("p c t i -> p (c t i)")

        alpha = gates[:, 0:T].rearrange("p (c t) -> p c t", t=C)
        beta = gates[:, T:2 * T].rearrange("p (c t) -> p c t", t=C)
        prods = prod_o.rearrange("p (n j c t i) -> p n j c t i", n=2, j=DH, c=NR, t=C)
        prod_s, prod_a = prods[:, 0], prods[:, 1]

        A = Arena()
        s2_q = A(BT)
        s2_max, s2_den, s2_rden = A(B * H), A(B * H), A(B * H)
        s2_e, s2_p = A(B * NK), A(B * NK)
        s2_pT, s2_oT = A(BT), A(BT)
        s3_hid = A(2 * BT).rearrange("p (n t) -> p n t", n=2)
        s3_ang = A(2 * BT).rearrange("p (n t) -> p n t", n=2)
        s3_t = A(BT)
        s3_act = A(NF * BT).rearrange("p (n t) -> p n t", n=NF)
        s3_th, s3_n, s3_sin, s3_cf, s3_bias = A(2 * NF), A(2 * NF), A(2 * NF), A(NF), A(NF)
        A = Arena()
        u4 = A(NH * BT).rearrange("p (n t) -> p n t", n=NH)
        gz = A(NH * BT).rearrange("p (n t) -> p n t", n=NH)
        dt = A(NH * BT).rearrange("p (n t) -> p n t", n=NH)
        dtu = A(NH * BT).rearrange("p (n t) -> p n t", n=NH)
        neg_a = A(NH * NS).rearrange("p (n s) -> p n s", n=NH)
        bc_f = A(BT)
        bc_r = A(BT)
        bc_mid = A(BT // 2).bitcast(BF16)
        bc_parts = A(BT // 2).bitcast(BF16)
        at = A.at
        fade = A(4 * BT).rearrange("p (n t) -> p n t", n=4)
        drive = A(2 * BT).rearrange("p (n t) -> p n t", n=2)
        hist = A(2 * BT).rearrange("p (n t) -> p n t", n=2)
        seen = A(2 * BT).rearrange("p (n t) -> p n t", n=2)
        c_wide = A(2 * BT).rearrange("p (n t) -> p n t", n=2)
        yg = A(NH * BT).rearrange("p (n t) -> p n t", n=NH)
        A.at = at
        dt_e, dt_l, dt_ser = A(NH * BT), A(NH * BT), A(NH * BT)
        dt_mask = A(NH * BT).bitcast(I32)
        A = Arena()
        s5_q = A(XH * BT).rearrange("p (h t) -> p h t", h=XH)
        s5_p = A(2 * 4 * KV).rearrange("p (n h k) -> p n h k", n=2, h=4)
        s5_pT = A(2 * 2 * 512).rearrange("p (n k i) -> p n k i", n=2, k=2)
        s5_z = A(2 * 512).rearrange("p (n i) -> p n i", n=2)
        s5_max = A(8).rearrange("p (n h) -> p n h", n=2)
        s5_den = A(8).rearrange("p (n h) -> p n h", n=2)
        s5_rden = A(8).rearrange("p (n h) -> p n h", n=2)
        xpad = A(B * (T + 1)).rearrange("p (b t) -> p b t", b=B)
        mixed = A(2 * BT).rearrange("p (n b t) -> p n b t", n=2, b=B)
        kact = A(BT)
        gate6 = A(BT)
        omm = A(2)

        block = ctx.enter_context(nc.Block())

        @block.sync
        def _(sp):
            sp.dma_start(tiles["first"][:], first).then_inc(S("first_in"), 16)
            sp.dma_start(xres[:], x).then_inc(S("x_in"), 16)
            sp.dma_start(tiles["early"][:], early).then_inc(S("early_in"), 16)
            sp.dma_start(kv_ctx[0:TC], context).then_inc(S("ctx_in"), 16)
            sp.dma_start(tiles["fold"][:], fold).then_inc(S("fold_in"), 16)
            sp.dma_start(row_in[:], rows.partition_broadcast(P)).then_inc(S("rows_in"), 16)
            sp.dma_start(tiles["late"][:], late).then_inc(S("late_in"), 16)
            sp.wait_ge(S("normed"), normed(6))
            sp.dma_start(out.rearrange("b t c -> t b c"), xrow[:, 0]).then_inc(S("stored"), 16)
            sp.wait_ge(S("stored"), 16)

        @block.vector
        def _(ve):
            count = [0]

            def step(ins):
                count[0] += 1
                ins.then_inc(S("vector_step"), 1)

            def join():
                ve.wait_ge(S("vector_step"), count[0])

            def then(ins):
                step(ins)
                join()

            tt, stt, ts = nc.vector.tensor_tensor, nc.vector.scalar_tensor_tensor, nc.vector.tensor_scalar

            def norm(n, acc, sem, need):
                dst = xrow[:, n % 2]
                if n == 1:
                    ve.wait_ge(S("x_in"), 16)
                else:
                    ve.wait_ge(S("residual"), n - 1)
                ve.wait_ge(S(sem), need)
                then(tt(dst, rows_of(acc), xres[:], ALU.add))
                norm_rows(n, dst, dst)

            def norm_rows(n, src, dst):
                for b in range(B):
                    step(nc.vector.bn_stats(stats[:, b], src[:, b]))
                join()
                for b in range(B):
                    step(nc.vector.bn_aggr(mv[:, b], stats[:, b]))
                join()
                ts(veps[:], mv[:, :, 1], EPS, None, ALU.add).then_inc(S("var"), 1)
                ve.wait_ge(S("rstd"), nth(n))
                for b in range(B):
                    ts(dst[:, b], src[:, b], mv[:, b, 0:1], rstd[:, b:b + 1],
                       ALU.subtract, ALU.mult).then_inc(S("normed"), 1)
                ve.wait_ge(S("normed"), normed(n))

            for b in range(1, B, 2):
                ve.wait_ge(S("qkv_mm"), b + 1)
                nc.vector.tensor_copy(qkvt[:, :, b], bank(b)[:, 0:3 * D + 2 * H].rearrange("p (n h) -> p n h", h=H)).then_inc(S("qkv_odd"), 1)
            for n in range(2):
                ve.wait_ge(S("square"), n + 1)
                nc.vector.tensor_reduce(norm2[:, n * T:(n + 1) * T],
                                        square[:, n * T * DH:(n + 1) * T * DH].rearrange("p (t j) -> p t j", j=DH),
                                        AX.X, ALU.add).then_inc(S("square_sum"), 1)
            ve.wait_ge(S("square_sum"), 2)
            ts(norm2, norm2, 1e-24, None, ALU.max).then_inc(S("square_sum"), 1)
            ve.wait_ge(S("gates"), 2)
            ve.wait_ge(S("v_turned"), 1)
            step(tt(X[:, :, :, 0:DH], bank(4, 2).rearrange("p (j c t) -> p c t j", j=DH, t=C),
                    beta.unsqueeze(3).to_broadcast([P, NC, C, DH]), ALU.mult))
            ve.wait_ge(S("norm_root"), 1)
            then(nc.vector.reciprocal(inv, norm2))
            for n, dst in ((0, K), (1, Q)):
                tt(dst, bank(2 * n, 2).rearrange("p (j t) -> p t j", j=DH),
                   inv[:, n * T:(n + 1) * T].unsqueeze(2).to_broadcast([P, T, DH]), ALU.mult).then_inc(S("unit"), 1)
            ve.wait_ge(S("unit"), 2)
            Kc = K.rearrange("p (c t) j -> p c t j", t=C)
            at, rows_k = 0, []
            for t in range(1, C):
                n = NC * t * DH
                rows_k.append(gram_k[:, at:at + n].rearrange("p (c i j) -> p c i j", i=t, j=DH))
                at += n
                step(tt(rows_k[-1], Kc[:, :, t:t + 1, :].to_broadcast([P, NC, t, DH]), Kc[:, :, 0:t, :], ALU.mult))
            join()
            ve.wait_ge(S("cleared"), 4)
            for t in range(1, C):
                step(nc.vector.tensor_reduce(low[:, :, t, 0:t], rows_k[t - 1], AX.X, ALU.add))
            ve.wait_ge(S("decayed"), 4)
            step(tt(X[:, :, :, DH:], Kc, bgcum.unsqueeze(3).to_broadcast([P, NC, C, DH]), ALU.mult))
            step(tt(Kend, Kc, decay[:, :, C - 1, :].unsqueeze(3).to_broadcast([P, NC, C, DH]), ALU.mult))
            join()
            then(tt(low, low, bdecay, ALU.mult))
            at = 0
            for t in range(C):
                if t:
                    tmp = sub_t[:, 0:NC * 2 * DH * t].rearrange("p (c n i) -> p c n i", n=2 * DH, i=t)
                    step(tt(tmp, low[:, :, t, 0:t].unsqueeze(2).to_broadcast([P, NC, 2 * DH, t]),
                            X[:, :, 0:t, :].rearrange("p c i n -> p c n i"), ALU.mult))
                    need = count[0]
                n = NC * (t + 1) * DH
                ve.wait_ge(S("gram_q"), t + 1)
                nc.vector.tensor_reduce(att[:, :, t, 0:t + 1],
                                        gram_q[:, at:at + n].rearrange("p (c i j) -> p c i j", i=t + 1, j=DH),
                                        AX.X, ALU.add).then_inc(S("att_raw"), 1)
                at += n
                if t:
                    ve.wait_ge(S("vector_step"), need)
                    then(nc.vector.tensor_reduce(sub_r, tmp, AX.X, ALU.add))
                    then(tt(X[:, :, t, :], X[:, :, t, :], sub_r, ALU.subtract))
            ve.wait_ge(S("state_zero"), 1)
            for c in range(NC):
                if c:
                    tmp = ch_t[:, 0:512].rearrange("p (t i j) -> p t i j", t=C, i=DH)
                    then(tt(tmp, X[:, c, :, DH:].unsqueeze(2).to_broadcast([P, C, DH, DH]),
                            state[:, c].unsqueeze(1).to_broadcast([P, C, DH, DH]), ALU.mult))
                    then(nc.vector.tensor_reduce(ch_r.rearrange("p (t i) -> p t i", t=C), tmp, AX.X, ALU.add))
                    tt(U[:, c], X[:, c, :, 0:DH], ch_r.rearrange("p (t i) -> p t i", t=C),
                       ALU.subtract).then_inc(S("u_ready"), 1)
                else:
                    nc.vector.tensor_copy(U[:, c], X[:, c, :, 0:DH]).then_inc(S("u_ready"), 1)
                ve.wait_ge(S("u_ready"), c + 1)
                if c + 1 < NC:
                    tmp = ch_t[:, 512:1024].rearrange("p (i j t) -> p i j t", i=DH, j=DH)
                    then(tt(tmp, U[:, c].rearrange("p t i -> p i t").unsqueeze(2).to_broadcast([P, DH, DH, C]),
                            Kend[:, c].rearrange("p t j -> p j t").unsqueeze(1).to_broadcast([P, DH, DH, C]),
                            ALU.mult))
                    then(nc.vector.tensor_reduce(ch_r2.rearrange("p (i j) -> p i j", i=DH), tmp, AX.X, ALU.add))
                    stt(state[:, c + 1], state[:, c], gcum[:, c, C - 1:C], ch_r2.rearrange("p (i j) -> p i j", i=DH),
                        ALU.mult, ALU.add).then_inc(S("state_ready"), 1)
                    ve.wait_ge(S("state_ready"), c + 1)
            ve.wait_ge(S("ctx_in"), 16)
            cr = kv_ctx
            for b in range(B):
                step(nc.vector.bn_stats(cstats[0:TC, b], cr[0:TC, b]))
            join()
            for b in range(B):
                step(nc.vector.bn_aggr(cmv[0:TC, b], cstats[0:TC, b]))
            join()
            ts(cveps[0:TC], cmv[0:TC, :, 1], EPS, None, ALU.add).then_inc(S("ctx_var"), 1)
            ve.wait_ge(S("ctx_rstd"), 1)
            for b in range(B):
                ts(kv_ctx[0:TC, b], cr[0:TC, b], cmv[0:TC, b, 0:1], crstd[0:TC, b:b + 1],
                   ALU.subtract, ALU.mult).then_inc(S("ctx_norm"), 1)
            for n in range(2):
                ve.wait_ge(S("key0_mm"), n + 1)
                stt(key0[:, n * HB:(n + 1) * HB],
                    bank(n)[:, 0:HB * TC].rearrange("p (b t) -> p b t", b=HB)[:, :, 0:NK], W("bk0"),
                    W("mask_k").unsqueeze(1).to_broadcast([P, HB, NK]), ALU.add, ALU.mult).then_inc(S("key0"), 1)
            for n in range(2):
                ve.wait_ge(S("val0_mm"), n + 1)
                tt(val0[0:NK, n * HB:(n + 1) * HB], bank(2 + n)[0:NK].rearrange("p (b c) -> p b c", b=HB),
                   W("mask_v")[0:NK].unsqueeze(1).to_broadcast([NK, HB, D]), ALU.mult).then_inc(S("val0"), 1)
            ve.wait_ge(S("rows_in"), 16)
            ve.wait_ge(S("fold_bo_mm"), 1)
            tt(fold_bo[:], bank(5)[:, 0:D], row_in[:, ROWS.index("bo1")], ALU.add).then_inc(S("fold_bo"), 1)

            norm(1, bank(4, 2), "projected", 1 * B)

            ve.wait_ge(S("score0"), B)
            sc = bank(2, 2).rearrange("p (b n) -> p b n", b=B)[:, :, 0:NK]
            then(nc.vector.tensor_reduce(s2_max, sc.rearrange("p b (m h) -> p b h m", h=H), AX.X, ALU.max))
            s2_m = s2_max.rearrange("p (b h) -> p b h", h=H).unsqueeze(2).to_broadcast([P, B, NM, H])
            tt(s2_e.rearrange("p (b m h) -> p b m h", b=B, h=H), sc.rearrange("p b (m h) -> p b m h", h=H), s2_m,
               ALU.subtract).then_inc(S("score0_shift"), 1)
            ve.wait_ge(S("exp0"), 1)
            then(nc.vector.tensor_reduce(s2_den, s2_e.rearrange("p (b m h) -> p b h m", b=B, h=H), AX.X, ALU.add))
            then(nc.vector.reciprocal(s2_rden, s2_den))
            tt(s2_p.rearrange("p (b m h) -> p b m h", b=B, h=H), s2_e.rearrange("p (b m h) -> p b m h", b=B, h=H),
               s2_rden.rearrange("p (b h) -> p b h", h=H).unsqueeze(2).to_broadcast([P, B, NM, H]),
               ALU.mult).then_inc(S("prob0"), 1)
            ve.wait_ge(S("probT0_mm"), B)
            nc.vector.tensor_copy(s2_pT[0:NK, BT // 2:], bank(5)[0:NK]).then_inc(S("probT0_b"), 1)

            norm(2, bank(2, 2), "projected", 2 * B)

            for f in range(NF):
                hid, ang = s3_hid[:, f % 2], s3_ang[:, f % 2]
                ve.wait_ge(S("angle"), f + 1)
                then(ts(s3_t[:], ang, 1 / TWO_PI, ROUND, ALU.mult, ALU.add))
                then(ts(s3_t[:], s3_t[:], ROUND, TWO_PI, ALU.subtract, ALU.mult))
                then(tt(ang, ang, s3_t[:], ALU.subtract))
                ts(ang, ang, PI_F, -PI_F, ALU.min, ALU.max).then_inc(S("reduced"), 1)
                ve.wait_ge(S("sine"), f + 1)
                stt(ang, ang, s3_cf[:, f:f + 1], hid, ALU.mult, ALU.add).then_inc(S("gated"), 1)

            norm(3, bank(4, 2), "projected", 3 * B)

            ve.wait_ge(S("xdbl"), 2)
            then(nc.vector.tensor_copy(bc_parts[0:32], bc_f[0:32]))
            then(tt(bc_r[0:32], bc_f[0:32], bc_parts[0:32], ALU.subtract))
            then(nc.vector.tensor_copy(bc_mid[0:32], bc_r[0:32]))
            step(nc.vector.tensor_copy(bc_parts[32:64], bc_mid[0:32]))
            then(tt(bc_r[0:32], bc_r[0:32], bc_mid[0:32], ALU.subtract))
            nc.vector.tensor_copy(bc_parts[64:96], bc_r[0:32]).then_inc(S("bc_parts"), 1)
            ve.wait_ge(S("dt_exp"), 1)
            step(ts(dt_ser, dt_e, 1 / 3, -0.5, ALU.mult, ALU.add))
            step(ts(dt_mask, dt_e, LOG1P_SERIES, None, ALU.is_lt))
            join()
            then(tt(dt_ser, dt_ser, dt_e, ALU.mult))
            then(stt(dt_ser, dt_ser, 1.0, dt_e, ALU.add, ALU.mult))
            ve.wait_ge(S("dt_log"), 1)
            then(nc.vector.copy_predicated(dt_l, dt_mask, dt_ser))
            ve.wait_ge(S("dt_relu"), 2)
            for n in range(NH):
                tt(dt[:, n], dt[:, n], dt_l.rearrange("p (n t) -> p n t", n=NH)[:, n], ALU.add).then_inc(S("dt"), 1)
            ve.wait_ge(S("dt"), NH)
            ve.wait_ge(S("u_in"), NH)
            then(tt(dtu, dt, u4, ALU.mult))
            for s in range(NS):
                ve.wait_ge(S("b_wide"), s + 1)
                for n in range(NH):
                    k = s * NH + n
                    tt(drive[:, k % 2], dtu[:, n], bank(4, 2), ALU.mult).then_inc(S("drive"), 1)
                for n in range(NH):
                    k = s * NH + n
                    ve.wait_ge(S("fade"), k + 1)
                    ve.wait_ge(S("drive"), k + 1)
                    if k >= 2:
                        ve.wait_ge(S("read_out"), k - 1)
                    nc.vector.tensor_tensor_scan(hist[:, k % 2], fade[:, k % 4], drive[:, k % 2], 0.0,
                                                 ALU.mult, ALU.add).then_inc(S("scan"), 1)
                ve.wait_ge(S("scan"), NH * (s + 1))
            for n in range(NH):
                ve.wait_ge(S("y_mm"), n + 1)
                then(stt(yg[:, n], u4[:, n], W("d_skip")[:, n:n + 1], bank(2 * n, 2), ALU.mult, ALU.add))
                tt(yg[:, n], yg[:, n], gz[:, n], ALU.mult).then_inc(S("y_gated"), 1)

            norm(4, bank(4, 2), "projected", 4 * B)

            norm_rows(7, xrow[:, 0], kv_lat[:])
            for b in range(B):
                for g in range(2):
                    k = 2 * b + g
                    sim = bank(2 * (k % 2), 2).rearrange("p (h n) -> p h n", h=4)[:, :, 0:KV]
                    ve.wait_ge(S("sim"), 4 * (k + 1))
                    mx = s5_max[:, k % 2]
                    then(nc.vector.tensor_reduce(mx, sim, AX.X, ALU.max))
                    ts(mx, mx, -float(D) ** -0.5, None, ALU.mult).then_inc(S("sim_max"), 1)
                    ve.wait_ge(S("exp5"), 4 * (k + 1))
                    then(nc.vector.reciprocal(s5_rden[:, k % 2], s5_den[:, k % 2]))
                    pr = s5_p[:, k % 2]
                    tt(pr, pr, s5_rden[:, k % 2].unsqueeze(2).to_broadcast([P, 4, KV]), ALU.mult).then_inc(S("prob5"), 1)
                    ve.wait_ge(S("probT5_mm"), 8 * (k + 1))
                    nc.vector.tensor_copy(s5_pT[:, k % 2, 1], bank(5)).then_inc(S("probT5_lat"), 1)
                ve.wait_ge(S("y5_mm"), b + 1)
                if b == 0:
                    ve.wait_ge(S("residual"), 4)
                step(tt(xrow[:, 1, b], bank(7)[:, (b % 4) * D:(b % 4 + 1) * D], xres[:, b], ALU.add))
                join()
                then(nc.vector.bn_stats(stats[:, b], xrow[:, 1, b]))
                nc.vector.bn_aggr(mv[:, b], stats[:, b]).then_inc(S("stat5"), 1)
            ve.wait_ge(S("stat5"), B)
            ts(veps[:], mv[:, :, 1], EPS, None, ALU.add).then_inc(S("var"), 1)
            ve.wait_ge(S("rstd"), nth(5))
            for b in range(B):
                ts(xrow[:, 1, b], xrow[:, 1, b], mv[:, b, 0:1], rstd[:, b:b + 1],
                   ALU.subtract, ALU.mult).then_inc(S("normed"), 1)

            prev = xpad[:, :, 0:T]
            ve.wait_ge(S("one_minus_mu"), 2)
            ve.wait_ge(S("xpad"), 3)
            for n, mu in enumerate(("mu_k", "mu_r")):
                then(ts(mixed[:, n], prev, omm[:, n:n + 1], None, ALU.mult))
                stt(mixed[:, n], xpad[:, :, 1:], W(mu), mixed[:, n], ALU.mult, ALU.add).then_inc(S("mixed"), 1)
            for n in range(2):
                ve.wait_ge(S("k_relu"), n + 1)
                tt(kact[:, n * BT // 2:(n + 1) * BT // 2], kact[:, n * BT // 2:(n + 1) * BT // 2],
                   kact[:, n * BT // 2:(n + 1) * BT // 2], ALU.mult).then_inc(S("k_act"), 1)
            ve.wait_ge(S("recept"), 1)
            ve.wait_ge(S("kv_mm"), B)
            then(tt(gate6, gate6, bank(4, 2), ALU.mult))
            then(tt(xrow[:, 0], xrow[:, 1], rows_of(gate6), ALU.add))
            norm_rows(6, xrow[:, 0], xrow[:, 0])

        @block.gpsimd
        def _(po):
            count = [0]

            def step(ins):
                count[0] += 1
                ins.then_inc(S("pool_step"), 1)

            def join():
                po.wait_ge(S("pool_step"), count[0])

            def then(ins):
                step(ins)
                join()

            tt, ts = nc.gpsimd.tensor_tensor, nc.gpsimd.tensor_scalar
            nc.gpsimd.memset(low, 0.0).then_inc(S("cleared"), 1)
            nc.gpsimd.memset(att, 0.0).then_inc(S("cleared"), 1)
            nc.gpsimd.memset(mhalf[:], -0.5).then_inc(S("cleared"), 1)
            nc.gpsimd.memset(decay, 0.0).then_inc(S("cleared"), 1)
            po.wait_ge(S("cleared"), 4)
            step(nc.gpsimd.memset(decay.rearrange("p c t i -> p c (t i)")[:, :, 0::C + 1], 1.0))
            nc.gpsimd.memset(state[:, 0], 0.0).then_inc(S("state_zero"), 1)
            join()
            po.wait_ge(S("gates"), 2)
            for t in range(1, C):
                ins = tt(decay[:, :, t, 0:t], decay[:, :, t - 1, 0:t],
                         alpha[:, :, t:t + 1].to_broadcast([P, NC, t]), ALU.mult)
                if t < C - 1:
                    then(ins)
            ins.then_inc(S("decayed"), 1)
            po.wait_ge(S("decayed"), 1)
            tt(gcum, decay[:, :, :, 0], alpha[:, :, 0:1].to_broadcast([P, NC, C]), ALU.mult).then_inc(S("decayed"), 1)
            po.wait_ge(S("decayed"), 2)
            tt(bgcum, gcum, beta, ALU.mult).then_inc(S("decayed"), 1)
            tt(bdecay, decay, beta.unsqueeze(3).to_broadcast([P, NC, C, C]), ALU.mult).then_inc(S("decayed"), 1)
            po.wait_ge(S("unit"), 2)
            Kc = K.rearrange("p (c t) j -> p c t j", t=C)
            Qc = Q.rearrange("p (c t) j -> p c t j", t=C)
            at = 0
            for t in range(C):
                n = NC * (t + 1) * DH
                tt(gram_q[:, at:at + n].rearrange("p (c i j) -> p c i j", i=t + 1, j=DH),
                   Qc[:, :, t:t + 1, :].to_broadcast([P, NC, t + 1, DH]), Kc[:, :, 0:t + 1, :],
                   ALU.mult).then_inc(S("gram_q"), 1)
                at += n
            step(tt(Qg, Qc, gcum.unsqueeze(3).to_broadcast([P, NC, C, DH]), ALU.mult))
            po.wait_ge(S("att_raw"), C)
            step(tt(att, att, decay, ALU.mult))
            join()
            po.wait_ge(S("unit"), 2)
            for c in range(NC):
                if c:
                    po.wait_ge(S("state_ready"), c)
                if c >= NR and c % NQ == 0:
                    po.wait_ge(S("o_mm"), (c - NR) // NQ + 1)
                tt(prod_s[:, :, c % NR].rearrange("p j t i -> p t i j"), Qg[:, c].unsqueeze(2).to_broadcast([P, C, DH, DH]),
                   state[:, c].unsqueeze(1).to_broadcast([P, C, DH, DH]), ALU.mult).then_inc(S("prods"), 1)
                po.wait_ge(S("u_ready"), c + 1)
                tt(prod_a[:, :, c % NR].rearrange("p j t i -> p t i j"), att[:, c].unsqueeze(2).to_broadcast([P, C, DH, C]),
                   U[:, c].rearrange("p j i -> p i j").unsqueeze(1).to_broadcast([P, C, DH, C]),
                   ALU.mult).then_inc(S("prods"), 1)

            def power(n):
                po.wait_ge(S("var"), nth(n))
                tt(rstd[:], veps[:], mhalf[:], ALU.pow).then_inc(S("rstd"), 1)

            po.wait_ge(S("ctx_var"), 1)
            tt(crstd[0:TC], cveps[0:TC], mhalf[0:TC], ALU.pow).then_inc(S("ctx_rstd"), 1)
            po.wait_ge(S("ctx_norm"), B)
            po.wait_ge(S("ctxT5_mm"), B)
            po.wait_ge(S("rows_in"), 16)
            then(tt(kv_ctx[0:TC], kv_ctx[0:TC],
                    row_in[0:TC, ROWS.index("g_med")].unsqueeze(1).to_broadcast([TC, B, D]), ALU.mult))
            tt(kv_ctx[0:TC], kv_ctx[0:TC], row_in[0:TC, ROWS.index("be_med")].unsqueeze(1).to_broadcast([TC, B, D]),
               ALU.add).then_inc(S("kv_ctx"), 1)
            power(1)

            def residual(n, bias):
                po.wait_ge(S("normed"), normed(n - 1))
                tt(xres[:], xrow[:, (n - 1) % 2], bias.unsqueeze(1).to_broadcast([P, B, D]),
                   ALU.add).then_inc(S("residual"), 1)

            residual(2, row_in[:, ROWS.index("bo0")])
            po.wait_ge(S("late_in"), 16)
            step(ts(s3_th[:, 0:NF], W("theta"), 1.0, None, ALU.mult))
            step(ts(s3_th[:, NF:], W("theta"), TWO_PI / 4, None, ALU.add))
            join()
            then(ts(s3_n, s3_th, 1 / TWO_PI, ROUND, ALU.mult, ALU.add))
            then(ts(s3_n, s3_n, ROUND, None, ALU.subtract))
            then(ts(s3_sin, s3_n, 6.28125, None, ALU.mult))
            then(tt(s3_th, s3_th, s3_sin, ALU.subtract))
            then(ts(s3_sin, s3_n, TWO_PI - 6.28125, None, ALU.mult))
            then(tt(s3_th, s3_th, s3_sin, ALU.subtract))
            ts(s3_th, s3_th, PI_F, -PI_F, ALU.min, ALU.max).then_inc(S("theta"), 1)
            po.wait_ge(S("theta"), 1)
            then(ts(s3_bias, W("b1"), 0.1, None, ALU.mult))
            tt(s3_bias, s3_bias, s3_th[:, 0:NF], ALU.add).then_inc(S("theta"), 1)
            po.wait_ge(S("theta_sin"), 1)
            step(tt(s3_n[:, 0:NF], s3_sin[:, NF:], W("w_re"), ALU.mult))
            step(tt(s3_n[:, NF:], s3_sin[:, 0:NF], W("w_im"), ALU.mult))
            join()
            then(tt(s3_cf, s3_n[:, 0:NF], s3_n[:, NF:], ALU.add))
            then(tt(s3_cf, s3_cf, W("w_im"), ALU.mult))
            ts(s3_cf, s3_cf, 0.1, None, ALU.mult).then_inc(S("gate_factor"), 1)
            power(2)
            residual(3, row_in[:, ROWS.index("b2")])
            for f in range(NF):
                po.wait_ge(S("gated"), f + 1)
                ts(s3_act[:, f], s3_ang[:, f % 2], 0.0, None, ALU.max).then_inc(S("act3"), 1)
            power(3)
            residual(4, row_in[:, ROWS.index("b_out")])
            po.wait_ge(S("a_exp"), 1)
            ts(neg_a, neg_a, -1.0, None, ALU.mult).then_inc(S("neg_a"), 1)
            po.wait_ge(S("dt"), NH)
            nc.gpsimd.memset(fade.rearrange("p n (b t) -> p (n b) t", t=T)[:, :, 0:1], 0.0).then_inc(S("fade_zero"), 1)
            for k in range(NS * NH):
                s = k // NH
                po.wait_ge(S("scan"), k + 1)
                po.wait_ge(S("c_wide"), s + 1)
                if k >= 2:
                    po.wait_ge(S("seen_used"), k - 1)
                tt(seen[:, k % 2], hist[:, k % 2], c_wide[:, s % 2], ALU.mult).then_inc(S("read_out"), 1)
            power(4)
            residual(5, fold_bo[:])
            power(7)
            po.wait_ge(S("turned"), 4 * B)
            po.wait_ge(S("normed"), normed(7))
            then(tt(kv_lat[:], kv_lat[:], row_in[:, ROWS.index("g_lat")].unsqueeze(1).to_broadcast([P, B, D]), ALU.mult))
            tt(kv_lat[:], kv_lat[:], row_in[:, ROWS.index("be_lat")].unsqueeze(1).to_broadcast([P, B, D]),
               ALU.add).then_inc(S("kv_lat"), 1)
            po.wait_ge(S("normed"), normed(4))
            ts(omm[:, 0:1], W("mu_k"), -1.0, 1.0, ALU.mult, ALU.add).then_inc(S("one_minus_mu"), 1)
            ts(omm[:, 1:2], W("mu_r"), -1.0, 1.0, ALU.mult, ALU.add).then_inc(S("one_minus_mu"), 1)
            nc.gpsimd.memset(xpad[:, :, 0:1], 0.0).then_inc(S("xpad"), 1)
            power(5)
            power(6)

        @block.scalar
        def _(ac):
            act = nc.scalar.activation

            def columns_out(n):
                for g in range(2):
                    ac.wait_ge(S("turned"), (n - 1) * B + HB * (g + 1))
                    act(xcol[:, g * HB:(g + 1) * HB], bank(6 + g).rearrange("p (b t) -> p b t", b=HB),
                        ACT.Copy).then_inc(S("xcol"), 1)

            for b in range(0, B, 2):
                ac.wait_ge(S("qkv_mm"), b + 1)
                act(qkvt[:, :, b], bank(b)[:, 0:3 * D + 2 * H].rearrange("p (n h) -> p n h", h=H), ACT.Copy).then_inc(S("qkv_even"), 1)
            ac.wait_ge(S("gates_turned"), 1)
            for n, dst in enumerate((gates[:, 0:T], gates[:, T:])):
                act(dst, bank(6)[:, n * T:(n + 1) * T], ACT.Sigmoid, bias=W("gate_bias")[:, n:n + 1]).then_inc(S("gates"), 1)
            for n in range(2):
                ac.wait_ge(S("kq_turned"), n + 1)
                act(square[:, n * T * DH:(n + 1) * T * DH].rearrange("p (t j) -> p j t", j=DH),
                    bank(2 * n, 2).rearrange("p (j t) -> p j t", j=DH), ACT.Square).then_inc(S("square"), 1)
            ac.wait_ge(S("square_sum"), 3)
            act(norm2, norm2, ACT.Sqrt).then_inc(S("norm_root"), 1)
            for dst, sem, k in ((fold_qk, "fold_qk", 0), (fold_vo, "fold_vo", 2)):
                for g in range(2):
                    ac.wait_ge(S(sem + "_mm"), 4 * (g + 1))
                    act(dst[:, 4 * g:4 * g + 4], bank(k + g).rearrange("p (h c) -> p h c", h=4), ACT.Copy).then_inc(S(sem), 1)
            ac.wait_ge(S("fold_bq_mm"), 1)
            act(fold_bq[:], bank(4)[:, 0:XH], ACT.Copy).then_inc(S("fold_bq"), 1)
            ac.wait_ge(S("late_in"), 16)
            act(pick[:], W("pick")[0:96].unsqueeze(2).to_broadcast([96, 2 * NS, P]), ACT.Copy).then_inc(S("pick"), 1)
            for g in range(2):
                ac.wait_ge(S("ctxT5_mm"), HB * (g + 1))
                act(kvT[:, g * HB:(g + 1) * HB, 0:TC], bank(g).rearrange("p (b t) -> p b t", b=HB)[:, :, 0:TC],
                    ACT.Identity, bias=W("be_med"), scale=W("g_med")).then_inc(S("kvT_ctx"), 1)
            for g in range(2):
                ac.wait_ge(S("o_mm"), 2 * (g + 1))
                act(osb.rearrange("p (i t) -> p i t", i=DH)[:, :, g * 64:(g + 1) * 64],
                    bank(6 + g).rearrange("p (t i) -> p i t", i=DH), ACT.Copy).then_inc(S("osb"), 1)
            for g in range(2):
                ac.wait_ge(S("o_rows_mm"), 4 * (g + 1))
                act(ot.rearrange("p (n i) -> p i n", i=DH)[:, 4 * g:4 * g + 4],
                    bank(g).rearrange("p (i n) -> p i n", i=4), ACT.Copy).then_inc(S("o_rows"), 1)
            for g in range(2):
                ac.wait_ge(S("o_cols_mm"), HB * (g + 1))
                act(otT[:, g * 512:(g + 1) * 512], bank(2 + g), ACT.Copy).then_inc(S("o_cols"), 1)
            columns_out(1)
            for g in range(2):
                ac.wait_ge(S("q0_mm"), g + 1)
                act(s2_q[:, g * 512:(g + 1) * 512], bank(g), ACT.Identity, bias=W("bq0")).then_inc(S("q0"), 1)
            ac.wait_ge(S("score0_shift"), 1)
            act(s2_e, s2_e, ACT.Exp, scale=float(DH) ** -0.5).then_inc(S("exp0"), 1)
            ac.wait_ge(S("probT0_mm"), HB)
            act(s2_pT[0:NK, 0:512], bank(4)[0:NK], ACT.Copy).then_inc(S("probT0_a"), 1)
            for g in range(2):
                ac.wait_ge(S("o0_mm"), HB * (g + 1))
                act(s2_oT[:, g * 512:(g + 1) * 512], bank(g), ACT.Identity, bias=W("bv0")).then_inc(S("o0"), 1)
            ac.wait_ge(S("theta"), 1)
            act(s3_sin, s3_th, ACT.Sin).then_inc(S("theta_sin"), 1)
            columns_out(2)
            ac.wait_ge(S("theta"), 2)

            def sine(f):
                ac.wait_ge(S("reduced"), f + 1)
                if f == 0:
                    ac.wait_ge(S("gate_factor"), 1)
                act(s3_ang[:, f % 2], s3_ang[:, f % 2], ACT.Sin).then_inc(S("sine"), 1)

            for f in range(NF):
                ac.wait_ge(S("hid_mm"), f + 1)
                if f >= 2:
                    ac.wait_ge(S("act3"), f - 1)
                act(s3_ang[:, f % 2], bank(2 * (f % 2), 2), ACT.Identity, bias=s3_bias[:, f:f + 1],
                    scale=0.1).then_inc(S("angle"), 1)
                act(s3_hid[:, f % 2], bank(2 * (f % 2), 2), ACT.Identity, bias=W("b1")[:, f:f + 1]).then_inc(S("hid"), 1)
                if f:
                    sine(f - 1)
            sine(NF - 1)
            columns_out(3)
            for n in range(2 * NH):
                ac.wait_ge(S("xz_mm"), n + 1)
                act(u4[:, n] if n < NH else gz[:, n - NH], bank(2 * (n % 2), 2), ACT.Silu,
                    bias=W("b_in")[:, n:n + 1]).then_inc(S("u_in") if n < NH else S("gz"), 1)
            for g in range(2):
                ac.wait_ge(S("xdbl_mm"), g + 1)
                act(bc_f[0:32, g * 512:(g + 1) * 512], bank(4 + g)[0:32], ACT.Identity,
                    bias=W("b_x")[0:32]).then_inc(S("xdbl"), 1)
            for n in range(NH):
                ac.wait_ge(S("dt_mm"), n + 1)
                act(dt_e[:, n * BT:(n + 1) * BT], bank(2 * n, 2), ACT.Abs, bias=W("b_dt")[:, n:n + 1]).then_inc(S("dt_abs"), 1)
                act(dt[:, n], bank(2 * n, 2), ACT.Relu, bias=W("b_dt")[:, n:n + 1]).then_inc(S("dt_relu"), 1)
            ac.wait_ge(S("dt_abs"), NH)
            act(dt_e, dt_e, ACT.Exp, scale=-1.0).then_inc(S("dt_exp"), 1)
            act(neg_a.rearrange("p n s -> p (n s)"), W("a_log"), ACT.Exp).then_inc(S("a_exp"), 1)
            ac.wait_ge(S("dt_exp"), 1)
            act(dt_l, dt_e, ACT.Ln, bias=1.0).then_inc(S("dt_log"), 1)
            ac.wait_ge(S("fade_zero"), 1)
            ac.wait_ge(S("neg_a"), 1)
            for s in range(NS):
                for n in range(NH):
                    k = s * NH + n
                    if k >= 4:
                        ac.wait_ge(S("scan"), k - 3)
                    act(fade[:, k % 4].rearrange("p (b t) -> p b t", t=T)[:, :, 1:],
                        dt[:, n].rearrange("p (b t) -> p b t", t=T)[:, :, 1:], ACT.Exp,
                        scale=neg_a[:, n, s:s + 1]).then_inc(S("fade"), 1)
                ac.wait_ge(S("c_wide_mm"), s + 1)
                if s >= 2:
                    ac.wait_ge(S("read_out"), NH * (s - 1))
                act(c_wide[:, s % 2], bank(6, 2), ACT.Copy).then_inc(S("c_wide"), 1)
            for g in range(2):
                ac.wait_ge(S("turned"), 3 * B + HB * (g + 1))
                act(kvT[:, g * HB:(g + 1) * HB, TC:], bank(6 + g).rearrange("p (b t) -> p b t", b=HB), ACT.Identity,
                    bias=W("be_lat"), scale=W("g_lat")).then_inc(S("kvT_lat"), 1)
            for h in range(XH):
                ac.wait_ge(S("q5_mm"), h + 1)
                act(s5_q[:, h], bank(2 * (h % 2), 2), ACT.Identity, bias=fold_bq[:, h:h + 1]).then_inc(S("q5"), 1)
            for k in range(2 * B):
                ac.wait_ge(S("sim_max"), k + 1)
                if k >= 2:
                    ac.wait_ge(S("probT5_mm"), 8 * (k - 1))
                for h in range(4):
                    act(s5_p[:, k % 2, h], bank(2 * (k % 2), 2).rearrange("p (h n) -> p h n", h=4)[:, h, 0:KV], ACT.Exp,
                        bias=s5_max[:, k % 2, h:h + 1], scale=float(D) ** -0.5,
                        accum_out=s5_den[:, k % 2, h:h + 1]).then_inc(S("exp5"), 1)
                ac.wait_ge(S("probT5_mm"), 8 * (k + 1))
                act(s5_pT[0:TC, k % 2, 0], bank(4)[0:TC], ACT.Copy).then_inc(S("probT5_ctx"), 1)
                ac.wait_ge(S("z5_mm"), k + 1)
                if k >= 2:
                    ac.wait_ge(S("y5_part"), k - 1)
                act(s5_z[:, k % 2], bank(6), ACT.Copy).then_inc(S("z5"), 1)
            for g in range(2):
                ac.wait_ge(S("turned"), 4 * B + HB * (g + 1))
                act(xpad[:, g * HB:(g + 1) * HB, 1:], bank(4 + g).rearrange("p (b t) -> p b t", b=HB),
                    ACT.Copy).then_inc(S("xpad"), 1)
            for g in range(2):
                ac.wait_ge(S("k6_mm"), g + 1)
                act(kact[:, g * 512:(g + 1) * 512], bank(2 + g), ACT.Relu).then_inc(S("k_relu"), 1)
            ac.wait_ge(S("r6_mm"), B)
            act(gate6, bank(0, 2), ACT.Sigmoid).then_inc(S("recept"), 1)

        @block.tensor
        def _(pe):
            mm, turn = nc.tensor.matmul, nc.tensor.transpose
            xT = W("xT").rearrange("p (b t) -> p b t", b=B)

            def turn_rows(n, src, k=6):
                for b in range(B):
                    pe.wait_ge(S("normed"), normed(n, b + 1))
                    turn(bank(k, 2)[:, b * T:(b + 1) * T], src[:, b], ident).then_inc(S("turned"), 1)

            pe.wait_ge(S("first_in"), 16)
            for b in range(B):
                mm(bank(b)[:, 0:3 * D + 2 * H], xT[:, b], W("w_qkvgb"), start=True, stop=True).then_inc(S("qkv_mm"), 1)
            pe.wait_ge(S("qkv_even"), B // 2)
            pe.wait_ge(S("qkv_odd"), B // 2)
            for n in range(2):
                ins = turn(bank(6)[:, n * T:(n + 1) * T], qkvt[:, 3 * DH + n].rearrange("p b h -> p (b h)"), ident)
            ins.then_inc(S("gates_turned"), 1)
            for n, (k, sem) in enumerate(((1, "kq_turned"), (0, "kq_turned"), (2, "v_turned"))):
                for j in range(DH):
                    ins = turn(bank(2 * n, 2)[:, j * T:(j + 1) * T],
                               qkvt[:, k * DH + j].rearrange("p b h -> p (b h)"), ident)
                ins.then_inc(S(sem), 1)
            pe.wait_ge(S("fold_in"), 16)
            pe.wait_ge(S("unit"), 2)
            fq, fk = (W(n).rearrange("p (h c) -> p h c", h=XH) for n in ("wq1T", "wk1T"))
            fv, fo = (W(n).rearrange("p (h c) -> p h c", h=XH) for n in ("wv1T", "wo1"))
            for h in range(XH):
                mm(bank(0, 2)[:, h * D:(h + 1) * D], fq[:, h], fk[:, h], start=True, stop=True).then_inc(S("fold_qk_mm"), 1)
            for h in range(XH):
                mm(bank(2, 2)[:, h * D:(h + 1) * D], fv[:, h], fo[:, h], start=True, stop=True).then_inc(S("fold_vo_mm"), 1)
            pe.wait_ge(S("vector_step"), 1)
            for h in range(XH):
                ins = mm(bank(4)[:, h:h + 1], fk[:, h], W("bq1")[:, h:h + 1], start=True, stop=True)
            ins.then_inc(S("fold_bq_mm"), 1)
            for h in range(XH):
                ins = mm(bank(5)[:, 0:D], W("bv1")[:, h:h + 1].to_broadcast([P, P]), fo[:, h],
                         start=(h == 0), stop=(h == XH - 1))
            ins.then_inc(S("fold_bo_mm"), 1)
            for g in range(NC // NQ):
                pe.wait_ge(S("prods"), 2 * NQ * (g + 1))
                at = g % 2 * NQ * C * DH
                for n, pr in enumerate((prod_s, prod_a)):
                    for j in range(C):
                        ins = mm(bank(6 + g // 2)[:, at:at + NQ * C * DH], ident,
                                 pr[:, j, g % 2 * NQ:(g % 2 + 1) * NQ].rearrange("p c t i -> p (c t i)"),
                                 start=(n == 0 and j == 0), stop=(n == 1 and j == C - 1))
                ins.then_inc(S("o_mm"), 1)
            pe.wait_ge(S("fold_qk"), 2)
            for b in range(B):
                pe.wait_ge(S("ctx_norm"), b + 1)
                turn(bank(0, 2)[:, b * T:b * T + TC], kv_ctx[0:TC, b], ident[0:TC, 0:TC]).then_inc(S("ctxT5_mm"), 1)
            pe.wait_ge(S("kvT_ctx"), 2)
            pe.wait_ge(S("early_in"), 16)
            cT = W("ctxT").rearrange("p (b t) -> p b t", b=B)
            for g in range(2):
                mm(bank(g)[:, 0:HB * TC], W("wk0"), W("ctxT")[:, g * HB * TC:(g + 1) * HB * TC],
                   start=True, stop=True).then_inc(S("key0_mm"), 1)
            pe.wait_ge(S("fold_vo"), 2)
            for g in range(2):
                for b in range(g * HB, (g + 1) * HB):
                    ins = mm(bank(2, 2)[0:NK, b * D:(b + 1) * D], cT[:, b, 0:NK], W("wv0"), start=True, stop=True)
                ins.then_inc(S("val0_mm"), 1)
            pe.wait_ge(S("osb"), 2)
            pe.wait_ge(S("key0"), 2)
            for i in range(DH):
                turn(bank(0, 2)[:, i * P:(i + 1) * P], osb[:, i * T:(i + 1) * T], ident).then_inc(S("o_rows_mm"), 1)
            pe.wait_ge(S("o_rows"), 2)
            pe.wait_ge(S("val0"), 2)
            for b in range(B):
                turn(bank(2, 2)[:, b * T:(b + 1) * T], ot[:, b * D:(b + 1) * D], ident).then_inc(S("o_cols_mm"), 1)
            pe.wait_ge(S("fold_bq"), 1)
            pe.wait_ge(S("fold_bo"), 1)
            for b in range(B):
                if b % HB == 0:
                    pe.wait_ge(S("o_cols"), b // HB + 1)
                mm(bank(4, 2)[:, b * D:(b + 1) * D], otT[:, b * T:(b + 1) * T], W("w_out0"),
                   start=True, stop=True).then_inc(S("projected"), 1)
            turn_rows(1, xrow[:, 1])
            for g in range(2):
                pe.wait_ge(S("xcol"), 0 + g + 1)
                mm(bank(g), W("wq0"), xcol[:, g * HB:(g + 1) * HB], start=True, stop=True).then_inc(S("q0_mm"), 1)
            for b in range(B):
                if b % HB == 0:
                    pe.wait_ge(S("q0"), b // HB + 1)
                mm(bank(2, 2)[:, b * T:b * T + NK], s2_q[:, b * T:(b + 1) * T], key0[:, b],
                   start=True, stop=True).then_inc(S("score0"), 1)
            pe.wait_ge(S("prob0"), 1)
            for b in range(B):
                turn(bank(4, 2)[0:NK, b * T:(b + 1) * T], s2_p[:, b * NK:(b + 1) * NK], ident).then_inc(S("probT0_mm"), 1)
            for b in range(B):
                if b % HB == 0:
                    pe.wait_ge(S("probT0_a" if b == 0 else "probT0_b"), 1)
                mm(bank(0, 2)[:, b * T:(b + 1) * T], val0[0:NK, b], s2_pT[0:NK, b * T:(b + 1) * T],
                   start=True, stop=True).then_inc(S("o0_mm"), 1)
            for b in range(B):
                if b % HB == 0:
                    pe.wait_ge(S("o0"), b // HB + 1)
                mm(bank(2, 2)[:, b * D:(b + 1) * D], s2_oT[:, b * T:(b + 1) * T], W("wo0"),
                   start=True, stop=True).then_inc(S("projected"), 1)
            turn_rows(2, xrow[:, 0])
            w2 = W("w2").rearrange("p (f c) -> p f c", f=NF)
            for f in range(NF):
                if f >= 2:
                    pe.wait_ge(S("hid"), f - 1)
                for g in range(2):
                    pe.wait_ge(S("xcol"), 2 + g + 1)
                    ins = mm(bank(2 * (f % 2) + g), W("w1")[:, f * P:(f + 1) * P], xcol[:, g * HB:(g + 1) * HB],
                             start=True, stop=True)
                ins.then_inc(S("hid_mm"), 1)
            pe.wait_ge(S("act3"), NF)
            for b in range(B):
                for f in range(NF):
                    ins = mm(bank(4, 2)[:, b * D:(b + 1) * D], s3_act[:, f, b * T:(b + 1) * T], w2[:, f],
                             start=(f == 0), stop=(f == NF - 1))
                ins.then_inc(S("projected"), 1)
            turn_rows(3, xrow[:, 1])
            for n in range(2 * NH):
                if n >= 2:
                    pe.wait_ge(S("u_in"), n - 1)
                for g in range(2):
                    pe.wait_ge(S("xcol"), 4 + g + 1)
                    ins = mm(bank(2 * (n % 2) + g), W("w_in")[:, n * P:(n + 1) * P], xcol[:, g * HB:(g + 1) * HB],
                             start=True, stop=True)
                ins.then_inc(S("xz_mm"), 1)
            wx = W("w_x").rearrange("p (n s) -> p n s", n=NH)
            for g in range(2):
                for n in range(NH):
                    ins = mm(bank(4 + g)[0:32], wx[:, n], u4[:, n, g * 512:(g + 1) * 512], start=(n == 0), stop=(n == NH - 1))
                ins.then_inc(S("xdbl_mm"), 1)
            wdt = W("w_dt").rearrange("p (n d) -> p n d", n=NH)
            for m in range(NH):
                pe.wait_ge(S("gz"), m + 1)
                for g in range(2):
                    for n in range(NH):
                        ins = mm(bank(2 * m + g), wdt[:, n, m * P:(m + 1) * P], u4[:, n, g * 512:(g + 1) * 512],
                                 start=(n == 0), stop=(n == NH - 1))
                ins.then_inc(S("dt_mm"), 1)

            def widen(s):
                if s:
                    pe.wait_ge(S("drive"), NH * s)
                for g in range(2):
                    ins = mm(bank(4 + g), pick[:, s], bc_parts[0:96, g * 512:(g + 1) * 512], start=True, stop=True)
                ins.then_inc(S("b_wide"), 1)
                if s:
                    pe.wait_ge(S("c_wide"), s)
                for g in range(2):
                    ins = mm(bank(6 + g), pick[:, NS + s], bc_parts[0:96, g * 512:(g + 1) * 512], start=True, stop=True)
                ins.then_inc(S("c_wide_mm"), 1)

            pe.wait_ge(S("bc_parts"), 1)
            pe.wait_ge(S("pick"), 1)
            widen(0)
            pe.wait_ge(S("dt_relu"), NH)
            for s in range(NS):
                if s + 1 < NS:
                    widen(s + 1)
                for n in range(NH):
                    k = s * NH + n
                    pe.wait_ge(S("read_out"), k + 1)
                    for g in range(2):
                        ins = mm(bank(2 * n + g), ident, seen[:, k % 2, g * 512:(g + 1) * 512],
                                 start=(s == 0), stop=(s == NS - 1))
                    ins.then_inc(S("seen_used"), 1)
                    if s == NS - 1:
                        pass
            pe.wait_ge(S("seen_used"), NS * NH)
            pe.sem_inc(S("y_mm"), NH)
            wo = W("w_out").rearrange("p (n c) -> p n c", n=NH)
            pe.wait_ge(S("y_gated"), NH)
            for b in range(B):
                for n in range(NH):
                    ins = mm(bank(4, 2)[:, b * D:(b + 1) * D], yg[:, n, b * T:(b + 1) * T], wo[:, n],
                             start=(n == 0), stop=(n == NH - 1))
                ins.then_inc(S("projected"), 1)
            turn_rows(7, kv_lat)
            for h in range(XH):
                if h >= 2:
                    pe.wait_ge(S("q5"), h - 1)
                for g in range(2):
                    pe.wait_ge(S("kvT_lat"), g + 1)
                    ins = mm(bank(2 * (h % 2) + g), fold_qk[:, h], kvT[:, g * HB:(g + 1) * HB, TC:], start=True, stop=True)
                ins.then_inc(S("q5_mm"), 1)
            pe.wait_ge(S("q5"), XH)

            def similar(k):
                b, g = k // 2, k % 2
                if k >= 2:
                    pe.wait_ge(S("exp5"), 4 * (k - 1))
                for h in range(4):
                    mm(bank(2 * (k % 2), 2)[:, h * 256:h * 256 + KV], s5_q[:, 4 * g + h, b * T:(b + 1) * T], kvT[:, b],
                       start=True, stop=True).then_inc(S("sim"), 1)

            similar(0)
            pe.wait_ge(S("kv_lat"), 1)
            pe.wait_ge(S("kv_ctx"), 1)
            for k in range(2 * B):
                b, g = k // 2, k % 2
                if k + 1 < 2 * B:
                    similar(k + 1)
                pe.wait_ge(S("prob5"), k + 1)
                if k:
                    pe.wait_ge(S("probT5_ctx"), k)
                    pe.wait_ge(S("probT5_lat"), k)
                for h in range(4):
                    turn(bank(4)[0:TC, h * T:(h + 1) * T], s5_p[:, k % 2, h, 0:TC], ident).then_inc(S("probT5_mm"), 1)
                    turn(bank(5)[:, h * T:(h + 1) * T], s5_p[:, k % 2, h, TC:], ident).then_inc(S("probT5_mm"), 1)
                pe.wait_ge(S("probT5_ctx"), k + 1)
                if k:
                    pe.wait_ge(S("z5"), k)
                mm(bank(6), kv_ctx[0:TC, b], s5_pT[0:TC, k % 2, 0], start=True, stop=False)
                pe.wait_ge(S("probT5_lat"), k + 1)
                mm(bank(6), kv_lat[:, b], s5_pT[:, k % 2, 1], start=False, stop=True).then_inc(S("z5_mm"), 1)
                pe.wait_ge(S("z5"), k + 1)
                if b >= 1:
                    pe.wait_ge(S("stat5"), b)
                for h in range(4):
                    ins = mm(bank(7)[:, (b % 4) * D:(b % 4 + 1) * D], s5_z[:, k % 2, h * T:(h + 1) * T],
                             fold_vo[:, 4 * g + h], start=(g == 0 and h == 0), stop=(g == 1 and h == 3))
                ins.then_inc(S("y5_part"), 1)
                if g:
                    pe.wait_ge(S("y5_part"), k + 1)
                    pe.sem_inc(S("y5_mm"), 1)
            turn_rows(5, xrow[:, 1], 4)
            for g in range(2):
                pe.wait_ge(S("mixed"), 1)
                mm(bank(2 + g), W("w_k"), mixed[:, 0, g * HB:(g + 1) * HB], start=True, stop=True).then_inc(S("k6_mm"), 1)
            pe.wait_ge(S("mixed"), 2)
            for b in range(B):
                mm(bank(0, 2)[:, b * D:(b + 1) * D], mixed[:, 1, b], W("w_r"), start=True, stop=True).then_inc(S("r6_mm"), 1)
            for b in range(B):
                if b % HB == 0:
                    pe.wait_ge(S("k_act"), b // HB + 1)
                mm(bank(4, 2)[:, b * D:(b + 1) * D], kact[:, b * T:(b + 1) * T], W("w_v"),
                   start=True, stop=True).then_inc(S("kv_mm"), 1)


_INS = ["first", "x", "early", "context", "fold", "late", "rows"]


def layout(i):
    i = {k: np.asarray(v) for k, v in i.items()}

    def col(v):
        return v.reshape(-1, P).T

    def blocks(w):
        return w.reshape(-1, P, w.shape[-1]).transpose(1, 0, 2).reshape(P, -1)

    def tall(w):
        out = np.zeros((P,) + w.shape[1:], w.dtype)
        out[:w.shape[0]] = w
        return out

    def heads_t(w):
        return w.reshape(D, XH, D).transpose(2, 1, 0).reshape(D, -1)

    ch, tok = np.arange(P), np.arange(P)
    mask = (ch[:, None] // DH == tok[None, :] % H).astype(np.float32)
    v = {
        "xT": i["x"].transpose(2, 0, 1).reshape(P, BT),
        "w_qkvgb": np.concatenate([i["L0_attn_Wqkv"].reshape(3, H, DH, D).transpose(3, 0, 2, 1).reshape(D, 3 * D), i["L0_attn_Wg"].T, i["L0_attn_Wb"].T], 1),
        "gate_bias": np.stack([np.tile(i["L0_attn_bg"], B), np.tile(i["L0_attn_bb"], B)], 1),
        "ident": np.eye(P, dtype=np.float32),
        "w_out0": i["L0_attn_Wout"].T,
        "wq0": i["L0_xattn_Wq"].T, "wk0": i["L0_xattn_Wk"].T, "wv0": i["L0_xattn_Wv"].T, "wo0": i["L0_xattn_Wo"].T,
        "bq0": col(i["L0_xattn_bq"]), "bk0": col(i["L0_xattn_bk"]), "bv0": col(i["L0_xattn_bv"]),
        "mask_k": mask[:, :NK], "mask_v": mask.T,
        "ctxT": i["ctx_1024"].transpose(2, 0, 1).reshape(P, B * TC),
        "wq1T": heads_t(i["L1_xattn_Wq"]),
        "wk1T": heads_t(i["L1_xattn_Wkv"][:, :XH * D]), "wv1T": heads_t(i["L1_xattn_Wkv"][:, XH * D:]),
        "wo1": blocks(i["L1_xattn_Wo"]), "bq1": col(i["L1_xattn_bq"]), "bv1": col(i["L1_xattn_bkv"][XH * D:]),
        "w1": i["L0_ffn_W1"], "b1": col(i["L0_ffn_b1"]), "theta": col(i["L0_ffn_quantum_phases"]),
        "w_re": col(i["L0_ffn_quantum_weights_real"]), "w_im": col(i["L0_ffn_quantum_weights_imag"]),
        "w2": blocks(i["L0_ffn_W2"]),
        "w_in": i["L1_attn_W_in"], "b_in": col(i["L1_attn_b_in"]), "w_x": blocks(i["L1_attn_W_x"]),
        "w_dt": blocks(i["L1_attn_W_dt"]), "b_dt": col(i["L1_attn_b_dt"]), "w_out": blocks(i["L1_attn_W_out"]),
        "a_log": blocks(i["L1_attn_A_log"]), "d_skip": col(i["L1_attn_D_param"]),
        "b_x": tall(i["L1_attn_b_x"][:, None]),
        "g_med": col(i["L1_xattn_gamma_media"]), "be_med": col(i["L1_xattn_beta_media"]),
        "g_lat": col(i["L1_xattn_gamma_lat"]), "be_lat": col(i["L1_xattn_beta_lat"]),
        "w_r": i["L1_ffn_W_r"].T, "w_k": i["L1_ffn_W_k"].T, "w_v": i["L1_ffn_W_v"].T,
        "mu_r": col(i["L1_ffn_mu_r"]), "mu_k": col(i["L1_ffn_mu_k"]),
        "pick": tall(np.tile(np.eye(2 * NS, dtype=np.float32), (3, 1))),
    }
    packs = {p: np.ascontiguousarray(np.concatenate([v[n] for n, _ in cols], 1)) for p, cols in PACKS.items()}
    packs["x"] = i["x"].transpose(1, 0, 2)
    packs["context"] = i["ctx_1024"].transpose(1, 0, 2)
    packs["rows"] = np.stack([i["L0_xattn_bo"], i["L0_ffn_b2"], i["L1_attn_b_out"], i["L1_xattn_bo"],
                              i["L1_xattn_gamma_media"], i["L1_xattn_beta_media"],
                              i["L1_xattn_gamma_lat"], i["L1_xattn_beta_lat"]])
    return packs


def kernel(**inputs):
    import concourse.bacc as bacc
    from concourse.bass_utils import run_bass_kernel_spmd

    nc = bacc.Bacc("TRN2", target_bir_lowering=False, num_devices=1)
    packs = layout(inputs)
    arrays, args = {}, []
    for name in _INS:
        a = np.ascontiguousarray(packs[name])
        arrays[f"in_{name}_dram"] = a
        args.append(nc.dram_tensor(f"in_{name}_dram", a.shape, mybir.dt.from_np(a.dtype), kind="ExternalInput").ap())
    args.append(nc.dram_tensor("out_0_dram", (B, T, D), F32, kind="ExternalOutput").ap())
    decoder(nc, *args)
    r = run_bass_kernel_spmd(nc, [arrays], core_ids=[0])
    return r.results[0]["out_0_dram"]
```

```python
from contextlib import ExitStack

import numpy as np
import concourse.bass as bass
from concourse import mybir

F32 = mybir.dt.float32
BF16 = mybir.dt.bfloat16
ALU = mybir.AluOpType
ACT = mybir.ActivationFunctionType
AX = mybir.AxisListType

P = 128
B, T, D = 8, 128, 128
BT = B * T
HB = B // 2
BANK = 512
H, DH = 16, 8
C = 8
NC = T // C
TC = 120
NM = TC // 16
NK = NM * 16
FF = 512
NF = FF // P
DI = 256
NH = DI // P
NS = 16
XH = 8
KV = TC + T
EPS = 1e-5
TWO_PI = float(2 * np.pi)
PI_F = float(np.nextafter(np.float32(np.pi), np.float32(0)))
ROUND = 1.5 * 2.0 ** 23

PACKS = {
    "first": [("xT", BT), ("w_qkvgb", 3 * D + 2 * H), ("gate_bias", 2), ("ident", P)],
    "early": [("w_out0", D), ("wq0", D), ("wk0", D), ("wv0", D), ("wo0", D), ("bq0", 1), ("bk0", 1),
              ("bv0", 1), ("mask_k", NK), ("mask_v", D), ("ctxT", B * TC)],
    "fold": [("wq1T", XH * D), ("wk1T", XH * D), ("wv1T", XH * D), ("wo1", XH * D), ("bq1", XH), ("bv1", XH)],
    "late": [("w1", FF), ("b1", NF), ("theta", NF), ("w_re", NF), ("w_im", NF), ("w2", NF * D), ("w_in", 2 * DI),
             ("b_in", 2 * NH), ("w_x", NH * 2 * NS), ("w_dt", NH * DI), ("b_dt", NH), ("w_out", NH * D),
             ("a_log", NH * NS), ("d_skip", NH), ("b_x", 1), ("g_med", 1), ("be_med", 1), ("g_lat", 1), ("be_lat", 1),
             ("w_r", D), ("w_k", D), ("w_v", D), ("mu_r", 1), ("mu_k", 1),
             ("pick", 2 * NS)],
}
ROWS = ["bo0", "b2", "b_out", "bo1", "g_med", "be_med", "g_lat", "be_lat"]


def columns(pack):
    at, out = 0, {}
    for name, n in PACKS[pack]:
        out[name] = (at, n)
        at += n
    return out, at


def decoder(nc, first, x, early, context, fold, late, rows, out):
    with ExitStack() as ctx:
        sems = {}

        def S(name):
            if name not in sems:
                sems[name] = ctx.enter_context(nc.semaphore(name))
            return sems[name]

        def sb(name, shape, dt=F32):
            return ctx.enter_context(nc.sbuf_tensor(name, shape, dt))

        where, tiles = {}, {}
        for pack in PACKS:
            cols, n = columns(pack)
            tiles[pack] = sb(f"{pack}_in", [P, n])
            for name, (at, w) in cols.items():
                where[name] = (pack, at, w)

        def W(name):
            pack, at, w = where[name]
            return tiles[pack][:, at:at + w]

        row_in = sb("rows_in", [P, len(ROWS), D])
        pick = sb("pick_wide", [3 * 2 * NS, 2 * NS, P], BF16)
        ident = W("ident")

        xrow = sb("xrow", [P, 2, B, D])
        xres = sb("xres", [P, B, D])
        xcol = sb("xcol", [P, B, T])
        key0 = sb("key0", [P, B, NK])
        val0 = sb("val0", [P, B, D])
        kvT = sb("kvT", [P, B, KV])
        kv_ctx = sb("kv_ctx", [P, B, D])
        kv_lat = sb("kv_lat", [P, B, D])
        fold_qk = sb("fold_qk", [P, XH, D])
        fold_vo = sb("fold_vo", [P, XH, D])
        fold_bq = sb("fold_bq", [P, XH])
        fold_bo = sb("fold_bo", [P, D])
        stats = sb("stats", [P, B, 6])
        mv = sb("mv", [P, B, 2])
        veps = sb("veps", [P, B])
        rstd = sb("rstd", [P, B])
        cstats = sb("cstats", [P, B, 6])
        cmv = sb("cmv", [P, B, 2])
        cveps = sb("cveps", [P, B])
        crstd = sb("crstd", [P, B])
        mhalf = sb("mhalf", [P, B])
        arena = sb("arena", [P, 27000])
        ps = ctx.enter_context(nc.psum_tensor("ps", [P, 8 * BANK], F32))

        NORMS = [1, 2, 3, 4, 7, 5, 6]

        def normed(n, k=B):
            return NORMS.index(n) * B + k

        def half(n, g):
            return NORMS.index(n) * 2 + g + 1

        class Arena:
            def __init__(self):
                self.at = 0

            def __call__(self, n):
                self.at += n
                assert self.at <= arena.shape[1], self.at
                return arena[:, self.at - n:self.at]

        def bank(k, n=1):
            return ps[:, k * BANK:(k + n) * BANK]

        def rows_of(ap):
            return ap.rearrange("p (b c) -> p b c", b=B)

        A = Arena()
        qkvt = A(B * (3 * D + 2 * H)).rearrange("p (n b h) -> p n b h", b=B, h=H)
        square = A(2 * T * DH)
        end = A.at
        A.at = 0
        sub_t = A(NC * 2 * DH * C)
        sub_r = A(NC * 2 * DH).rearrange("p (c n) -> p c n", n=2 * DH)
        ch_t = A(2 * C * DH * DH)
        ch_r = A(C * DH)
        ch_r2 = A(DH * DH)
        Kend = A(T * DH).rearrange("p (c t j) -> p c t j", t=C, j=DH)
        assert A.at <= end
        A.at = end
        norm2 = A(2 * T)
        inv = A(2 * T)
        K = A(T * DH).rearrange("p (t j) -> p t j", j=DH)
        Q = A(T * DH).rearrange("p (t j) -> p t j", j=DH)
        gates = A(2 * T)
        decay = A(T * C).rearrange("p (c t i) -> p c t i", t=C, i=C)
        bdecay = A(T * C).rearrange("p (c t i) -> p c t i", t=C, i=C)
        gcum = A(T).rearrange("p (c t) -> p c t", t=C)
        bgcum = A(T).rearrange("p (c t) -> p c t", t=C)
        low = A(T * C).rearrange("p (c t i) -> p c t i", t=C, i=C)
        att = A(T * C).rearrange("p (c t i) -> p c t i", t=C, i=C)
        X = A(T * 2 * DH).rearrange("p (c t n) -> p c t n", t=C, n=2 * DH)
        U = A(T * DH).rearrange("p (c t i) -> p c t i", t=C, i=DH)
        state = A(NC * DH * DH).rearrange("p (c i j) -> p c i j", i=DH, j=DH)
        Qg = A(T * DH).rearrange("p (c t j) -> p c t j", t=C, j=DH)
        NR = NC // 2
        gram = A.at
        prod_o = A(2 * NR * DH * C * DH)
        gram_k = arena[:, gram:gram + NC * DH * C * (C - 1) // 2]
        gram_q = arena[:, gram + NC * DH * C * (C - 1) // 2:gram + NC * DH * C * C]
        osb, ot = K.rearrange("p t j -> p (t j)"), Q.rearrange("p t j -> p (t j)")
        otT = low.rearrange("p c t i -> p (c t i)")

        alpha = gates[:, 0:T].rearrange("p (c t) -> p c t", t=C)
        beta = gates[:, T:2 * T].rearrange("p (c t) -> p c t", t=C)
        prods = prod_o.rearrange("p (n j c t i) -> p n j c t i", n=2, j=DH, c=NR, t=C)
        prod_s, prod_a = prods[:, 0], prods[:, 1]

        A = Arena()
        s2_q = A(BT)
        s2_max, s2_den, s2_rden = A(B * H), A(B * H), A(B * H)
        s2_e, s2_p = A(B * NK), A(B * NK)
        s2_pT, s2_oT = A(BT), A(BT)
        s3_hid = A(2 * BT).rearrange("p (n t) -> p n t", n=2)
        s3_ang = A(2 * BT).rearrange("p (n t) -> p n t", n=2)
        s3_t = A(BT)
        s3_act = A(NF * BT).rearrange("p (n t) -> p n t", n=NF)
        s3_th, s3_n, s3_sin, s3_cf, s3_bias = A(2 * NF), A(2 * NF), A(2 * NF), A(NF), A(NF)
        A = Arena()
        u4 = A(NH * BT).rearrange("p (n t) -> p n t", n=NH)
        gz = A(NH * BT).rearrange("p (n t) -> p n t", n=NH)
        dt = A(NH * BT).rearrange("p (n t) -> p n t", n=NH)
        dtu = A(NH * BT).rearrange("p (n t) -> p n t", n=NH)
        neg_a = A(NH * NS).rearrange("p (n s) -> p n s", n=NH)
        bc_f = A(BT)
        bc_r = A(BT)
        bc_mid = A(BT // 2).bitcast(BF16)
        bc_parts = A(BT // 2).bitcast(BF16)
        diag_d = A(NH * P).rearrange("p (n c) -> p n c", n=NH)
        fade = A(3 * BT).rearrange("p (n t) -> p n t", n=3)
        drive = A(3 * BT).rearrange("p (n t) -> p n t", n=3)
        hist = A(2 * BT).rearrange("p (n t) -> p n t", n=2)
        seen = A(2 * BT).rearrange("p (n t) -> p n t", n=2)
        c_wide = A(2 * BT).rearrange("p (n t) -> p n t", n=2)
        b_wide = A(2 * BT).rearrange("p (n t) -> p n t", n=2)
        yg = fade[:, 0:2]
        dt_e, dt_l = hist, seen
        A = Arena()
        s5_q = A(XH * BT).rearrange("p (h t) -> p h t", h=XH)
        s5_p = A(2 * 4 * KV).rearrange("p (n h k) -> p n h k", n=2, h=4)
        s5_pT = A(2 * 2 * 512).rearrange("p (n k i) -> p n k i", n=2, k=2)
        s5_z = A(2 * 512).rearrange("p (n i) -> p n i", n=2)
        s5_max = A(8).rearrange("p (n h) -> p n h", n=2)
        s5_den = A(8).rearrange("p (n h) -> p n h", n=2)
        s5_rden = A(8).rearrange("p (n h) -> p n h", n=2)
        xpad = A(B * (T + 1)).rearrange("p (b t) -> p b t", b=B)
        mixed = A(2 * BT).rearrange("p (n b t) -> p n b t", n=2, b=B)
        kact = A(BT)
        gate6 = A(BT)
        omm = A(2)

        block = ctx.enter_context(nc.Block())

        @block.sync
        def _(sp):
            sp.dma_start(tiles["first"][:], first).then_inc(S("first_in"), 16)
            sp.dma_start(xres[:], x).then_inc(S("x_in"), 16)
            sp.dma_start(tiles["early"][:], early).then_inc(S("early_in"), 16)
            sp.dma_start(kv_ctx[0:TC], context).then_inc(S("ctx_in"), 16)
            sp.dma_start(tiles["fold"][:], fold).then_inc(S("fold_in"), 16)
            sp.dma_start(row_in[:], rows.partition_broadcast(P)).then_inc(S("rows_in"), 16)
            sp.dma_start(tiles["late"][:], late).then_inc(S("late_in"), 16)
            sp.wait_ge(S("normed"), normed(6))
            sp.dma_start(out.rearrange("b t c -> t b c"), xrow[:, 0]).then_inc(S("stored"), 16)
            sp.wait_ge(S("stored"), 16)

        @block.vector
        def _(ve):
            count = [0]

            def step(ins):
                count[0] += 1
                ins.then_inc(S("vector_step"), 1)

            def join():
                ve.wait_ge(S("vector_step"), count[0])

            def then(ins):
                step(ins)
                join()

            tt, stt, ts = nc.vector.tensor_tensor, nc.vector.scalar_tensor_tensor, nc.vector.tensor_scalar

            def add_residual(n, g, acc):
                h = slice(g * HB, (g + 1) * HB)
                if n == 1:
                    ve.wait_ge(S("x_in"), 16)
                else:
                    ve.wait_ge(S("residual"), 2 * (n - 2) + g + 1)
                ve.wait_ge(S("projected"), (n - 1) * B + (g + 1) * HB)
                then(tt(xrow[:, n % 2, h], acc.rearrange("p (b c) -> p b c", b=HB), xres[:, h], ALU.add))

            def norms(halves):
                last = None
                for n, g, src, dst, make in halves:
                    if make is not None:
                        make()
                    statistics(g, src)
                    if last:
                        norm_finish(*last)
                    ts(veps[:, g * HB:(g + 1) * HB], mv[:, g * HB:(g + 1) * HB, 1], EPS, None, ALU.add).then_inc(S("var"), 1)
                    last = (n, g, src, dst)
                norm_finish(*last)

            def stage_norms(n, k):
                return [(n, g, xrow[:, n % 2], xrow[:, n % 2], lambda g=g: add_residual(n, g, bank(k + g)))
                        for g in range(2)]

            def statistics(g, src):
                for b in range(g * HB, (g + 1) * HB):
                    step(nc.vector.bn_stats(stats[:, b], src[:, b]))
                join()
                for b in range(g * HB, (g + 1) * HB):
                    step(nc.vector.bn_aggr(mv[:, b], stats[:, b]))
                join()

            def norm_finish(n, g, src, dst):
                ve.wait_ge(S("rstd"), half(n, g))
                for b in range(g * HB, (g + 1) * HB):
                    ts(dst[:, b], src[:, b], mv[:, b, 0:1], rstd[:, b:b + 1],
                       ALU.subtract, ALU.mult).then_inc(S("normed"), 1)
                ve.wait_ge(S("normed"), normed(n, (g + 1) * HB))

            for b in range(1, B, 2):
                ve.wait_ge(S("qkv_mm"), b + 1)
                nc.vector.tensor_copy(qkvt[:, :, b], bank(b)[:, 0:3 * D + 2 * H].rearrange("p (n h) -> p n h", h=H)).then_inc(S("qkv_odd"), 1)
            ve.wait_ge(S("ctx_in"), 16)
            cr = kv_ctx
            for b in range(B):
                step(nc.vector.bn_stats(cstats[0:TC, b], cr[0:TC, b]))
            join()
            for b in range(B):
                step(nc.vector.bn_aggr(cmv[0:TC, b], cstats[0:TC, b]))
            join()
            ts(cveps[0:TC], cmv[0:TC, :, 1], EPS, None, ALU.add).then_inc(S("ctx_var"), 1)
            ve.wait_ge(S("ctx_rstd"), 1)
            for b in range(B):
                ts(kv_ctx[0:TC, b], cr[0:TC, b], cmv[0:TC, b, 0:1], crstd[0:TC, b:b + 1],
                   ALU.subtract, ALU.mult).then_inc(S("ctx_norm"), 1)
            for n in range(2):
                ve.wait_ge(S("square"), n + 1)
                nc.vector.tensor_reduce(norm2[:, n * T:(n + 1) * T],
                                        square[:, n * T * DH:(n + 1) * T * DH].rearrange("p (t j) -> p t j", j=DH),
                                        AX.X, ALU.add).then_inc(S("square_sum"), 1)
            ve.wait_ge(S("square_sum"), 2)
            ts(norm2, norm2, 1e-24, None, ALU.max).then_inc(S("square_sum"), 1)
            ve.wait_ge(S("gates"), 2)
            ve.wait_ge(S("v_turned"), 1)
            step(tt(X[:, :, :, 0:DH], bank(4, 2).rearrange("p (j c t) -> p c t j", j=DH, t=C),
                    beta.unsqueeze(3).to_broadcast([P, NC, C, DH]), ALU.mult))
            ve.wait_ge(S("norm_root"), 1)
            then(nc.vector.reciprocal(inv, norm2))
            for n, dst in ((0, K), (1, Q)):
                tt(dst, bank(2 * n, 2).rearrange("p (j t) -> p t j", j=DH),
                   inv[:, n * T:(n + 1) * T].unsqueeze(2).to_broadcast([P, T, DH]), ALU.mult).then_inc(S("unit"), 1)
            ve.wait_ge(S("unit"), 2)
            Kc = K.rearrange("p (c t) j -> p c t j", t=C)
            at, rows_k = 0, []
            for t in range(1, C):
                n = NC * t * DH
                rows_k.append(gram_k[:, at:at + n].rearrange("p (c i j) -> p c i j", i=t, j=DH))
                at += n
                step(tt(rows_k[-1], Kc[:, :, t:t + 1, :].to_broadcast([P, NC, t, DH]), Kc[:, :, 0:t, :], ALU.mult))
            join()
            ve.wait_ge(S("cleared"), 4)
            for t in range(1, C):
                step(nc.vector.tensor_reduce(low[:, :, t, 0:t], rows_k[t - 1], AX.X, ALU.add))
            ve.wait_ge(S("decayed"), 4)
            step(tt(X[:, :, :, DH:], Kc, bgcum.unsqueeze(3).to_broadcast([P, NC, C, DH]), ALU.mult))
            step(tt(Kend, Kc, decay[:, :, C - 1, :].unsqueeze(3).to_broadcast([P, NC, C, DH]), ALU.mult))
            join()
            then(tt(low, low, bdecay, ALU.mult))
            at = 0
            for t in range(C):
                if t:
                    tmp = sub_t[:, 0:NC * 2 * DH * t].rearrange("p (c n i) -> p c n i", n=2 * DH, i=t)
                    step(tt(tmp, low[:, :, t, 0:t].unsqueeze(2).to_broadcast([P, NC, 2 * DH, t]),
                            X[:, :, 0:t, :].rearrange("p c i n -> p c n i"), ALU.mult))
                    need = count[0]
                n = NC * (t + 1) * DH
                ve.wait_ge(S("gram_q"), t + 1)
                nc.vector.tensor_reduce(att[:, :, t, 0:t + 1],
                                        gram_q[:, at:at + n].rearrange("p (c i j) -> p c i j", i=t + 1, j=DH),
                                        AX.X, ALU.add).then_inc(S("att_raw"), 1)
                at += n
                if t:
                    ve.wait_ge(S("vector_step"), need)
                    then(nc.vector.tensor_reduce(sub_r, tmp, AX.X, ALU.add))
                    then(tt(X[:, :, t, :], X[:, :, t, :], sub_r, ALU.subtract))
            for n in range(2):
                ve.wait_ge(S("key0_mm"), n + 1)
                stt(key0[:, n * HB:(n + 1) * HB],
                    bank(n)[:, 0:HB * TC].rearrange("p (b t) -> p b t", b=HB)[:, :, 0:NK], W("bk0"),
                    W("mask_k").unsqueeze(1).to_broadcast([P, HB, NK]), ALU.add, ALU.mult).then_inc(S("key0"), 1)
            for n in range(2):
                ve.wait_ge(S("val0_mm"), n + 1)
                tt(val0[0:NK, n * HB:(n + 1) * HB], bank(2 + n)[0:NK].rearrange("p (b c) -> p b c", b=HB),
                   W("mask_v")[0:NK].unsqueeze(1).to_broadcast([NK, HB, D]), ALU.mult).then_inc(S("val0"), 1)
            ve.wait_ge(S("rows_in"), 16)
            ve.wait_ge(S("fold_bo_mm"), 1)
            tt(fold_bo[:], bank(5)[:, 0:D], row_in[:, ROWS.index("bo1")], ALU.add).then_inc(S("fold_bo"), 1)

            ve.wait_ge(S("state_zero"), 1)
            for c in range(NC):
                if c:
                    tmp = ch_t[:, 0:512].rearrange("p (t i j) -> p t i j", t=C, i=DH)
                    then(tt(tmp, X[:, c, :, DH:].unsqueeze(2).to_broadcast([P, C, DH, DH]),
                            state[:, c].unsqueeze(1).to_broadcast([P, C, DH, DH]), ALU.mult))
                    then(nc.vector.tensor_reduce(ch_r.rearrange("p (t i) -> p t i", t=C), tmp, AX.X, ALU.add))
                    tt(U[:, c], X[:, c, :, 0:DH], ch_r.rearrange("p (t i) -> p t i", t=C),
                       ALU.subtract).then_inc(S("u_ready"), 1)
                else:
                    nc.vector.tensor_copy(U[:, c], X[:, c, :, 0:DH]).then_inc(S("u_ready"), 1)
                ve.wait_ge(S("u_ready"), c + 1)
                if c + 1 < NC:
                    tmp = ch_t[:, 512:1024].rearrange("p (i j t) -> p i j t", i=DH, j=DH)
                    then(tt(tmp, U[:, c].rearrange("p t i -> p i t").unsqueeze(2).to_broadcast([P, DH, DH, C]),
                            Kend[:, c].rearrange("p t j -> p j t").unsqueeze(1).to_broadcast([P, DH, DH, C]),
                            ALU.mult))
                    then(nc.vector.tensor_reduce(ch_r2.rearrange("p (i j) -> p i j", i=DH), tmp, AX.X, ALU.add))
                    stt(state[:, c + 1], state[:, c], gcum[:, c, C - 1:C], ch_r2.rearrange("p (i j) -> p i j", i=DH),
                        ALU.mult, ALU.add).then_inc(S("state_ready"), 1)
                    ve.wait_ge(S("state_ready"), c + 1)
            norms(stage_norms(1, 4))

            def by_head(ap, g):
                return ap[:, g * HB:(g + 1) * HB].unsqueeze(2).to_broadcast([P, HB, NM, H])

            s2m, s2d, s2r = (ap.rearrange("p (b h) -> p b h", h=H) for ap in (s2_max, s2_den, s2_rden))
            s2e, s2p = (ap.rearrange("p (b m h) -> p b m h", b=B, h=H) for ap in (s2_e, s2_p))
            for g in range(2):
                h = slice(g * HB, (g + 1) * HB)
                ve.wait_ge(S("score0"), (g + 1) * HB)
                sc = bank(2 + g).rearrange("p (b n) -> p b n", b=HB)[:, :, 0:NK]
                then(nc.vector.tensor_reduce(s2m[:, h], sc.rearrange("p b (m h) -> p b h m", h=H), AX.X, ALU.max))
                tt(s2e[:, h], sc.rearrange("p b (m h) -> p b m h", h=H), by_head(s2m, g),
                   ALU.subtract).then_inc(S("score0_shift"), 1)
            for g in range(2):
                h = slice(g * HB, (g + 1) * HB)
                ve.wait_ge(S("exp0"), g + 1)
                then(nc.vector.tensor_reduce(s2d[:, h], s2e[:, h].rearrange("p b m h -> p b h m"), AX.X, ALU.add))
                then(nc.vector.reciprocal(s2r[:, h], s2d[:, h]))
                tt(s2p[:, h], s2e[:, h], by_head(s2r, g), ALU.mult).then_inc(S("prob0"), 1)
            norms(stage_norms(2, 2))

            def turns_of(k):
                ve.wait_ge(S("angle"), 2 * (k + 1))
                if k:
                    ve.wait_ge(S("reduced"), k)
                then(ts(s3_t, s3_ang[:, k % 2], 1 / TWO_PI, ROUND, ALU.mult, ALU.add))
                ts(s3_t, s3_t, ROUND, TWO_PI, ALU.subtract, ALU.mult).then_inc(S("turns"), 1)

            turns_of(0)
            for k in range(NF):
                g, hid, ang = k // 2, s3_hid[:, k % 2], s3_ang[:, k % 2]
                ve.wait_ge(S("reduced"), k + 1)
                ts(ang, ang, PI_F, -PI_F, ALU.min, ALU.max).then_inc(S("clamped"), 1)
                if k + 1 < NF:
                    turns_of(k + 1)
                ve.wait_ge(S("sine"), k + 1)
                for m in range(2):
                    f = 2 * (k % 2) + m
                    stt(ang[:, m * 512:(m + 1) * 512], ang[:, m * 512:(m + 1) * 512], s3_cf[:, f:f + 1],
                        hid[:, m * 512:(m + 1) * 512], ALU.mult, ALU.add).then_inc(S("gated"), 1)
                ve.wait_ge(S("gated"), 2 * (k + 1))
                ts(s3_act[:, 2 * (k % 2):2 * (k % 2) + 2, g * 512:(g + 1) * 512],
                   ang.rearrange("p (m t) -> p m t", m=2), 0.0, None, ALU.max).then_inc(S("act3"), 1)
            norms(stage_norms(3, 4))

            for g in range(2):
                h = slice(g * 512, (g + 1) * 512)
                ve.wait_ge(S("xdbl"), g + 1)
                then(nc.vector.tensor_copy(bc_parts[0:32, h], bc_f[0:32, h]))
                then(tt(bc_r[0:32, h], bc_f[0:32, h], bc_parts[0:32, h], ALU.subtract))
                then(nc.vector.tensor_copy(bc_mid[0:32, h], bc_r[0:32, h]))
                step(nc.vector.tensor_copy(bc_parts[32:64, h], bc_mid[0:32, h]))
                then(tt(bc_r[0:32, h], bc_r[0:32, h], bc_mid[0:32, h], ALU.subtract))
                nc.vector.tensor_copy(bc_parts[64:96, h], bc_r[0:32, h]).then_inc(S("bc_parts"), 1)
            ve.wait_ge(S("dt_exp"), 1)
            then(ts(dtu[:, 0], dt_e[:, 0], 1.0, None, ALU.add))
            then(ts(dtu[:, 0], dtu[:, 0], 1.0, None, ALU.subtract))
            then(tt(dtu[:, 0], dt_e[:, 0], dtu[:, 0], ALU.subtract))
            ve.wait_ge(S("dt_relu"), 1)
            tt(dt[:, 0], dt[:, 0], dtu[:, 0], ALU.add).then_inc(S("dt_part"), 1)
            for n in range(NH):
                for g in range(2):
                    ve.wait_ge(S("z_mm"), 2 * n + g + 1)
                    ts(gz[:, n, g * 512:(g + 1) * 512], bank(2 + 2 * n + g), W("b_in")[:, NH + n:NH + n + 1], None,
                       ALU.add).then_inc(S("gz_in"), 1)
            for n in range(NH):
                ve.wait_ge(S("dt_log"), n + 1)
                ve.wait_ge(S("dt_part"), n + 1)
                tt(dt[:, n], dt[:, n], dt_l[:, n], ALU.add).then_inc(S("dt"), 1)
                ve.wait_ge(S("dt"), n + 1)
                tt(dtu[:, n], dt[:, n], u4[:, n], ALU.mult).then_inc(S("dtu"), 1)
            def drive_of(k):
                s, n = k // NH, k % NH
                ve.wait_ge(S("b_wide"), s + 1)
                if k >= 3:
                    ve.wait_ge(S("scan"), k - 2)
                tt(drive[:, k % 3], dtu[:, n], b_wide[:, s % 2], ALU.mult).then_inc(S("drive"), 1)

            ve.wait_ge(S("dtu"), NH)
            drive_of(0)
            drive_of(1)
            for k in range(NS * NH):
                ve.wait_ge(S("fade"), k + 1)
                ve.wait_ge(S("drive"), k + 1)
                if k >= 2:
                    ve.wait_ge(S("read_out"), k - 1)
                elif k == 0:
                    ve.wait_ge(S("dtu"), NH)
                nc.vector.tensor_tensor_scan(hist[:, k % 2], fade[:, k % 3], drive[:, k % 3], 0.0,
                                             ALU.mult, ALU.add).then_inc(S("scan"), 1)
                if k + 2 < NS * NH:
                    drive_of(k + 2)
            ve.wait_ge(S("scan"), NS * NH)
            ve.wait_ge(S("seen_used"), NS * NH - 2)
            for g in range(2):
                h = slice(g * 512, (g + 1) * 512)
                tt(seen[:, 1, h], hist[:, 1, h], c_wide[:, (NS - 1) % 2, h], ALU.mult).then_inc(S("read_last"), 1)
            for g in range(2):
                for n in range(NH):
                    ve.wait_ge(S("y_mm"), NH * g + n + 1)
                    ve.wait_ge(S("gz"), n + 1)
                    y, z = (ap[:, n, g * 512:(g + 1) * 512] for ap in (yg, gz))
                    tt(y, bank(2 * n + g), z, ALU.mult).then_inc(S("y_gated"), 1)

            norms(stage_norms(4, 4) + [(7, g, xrow[:, 0], kv_lat[:], None) for g in range(2)])

            def shift(k):
                sim = bank(2 * (k % 2), 2).rearrange("p (h n) -> p h n", h=4)[:, :, 0:KV]
                ve.wait_ge(S("sim"), 4 * (k + 1))
                mx = s5_max[:, k % 2]
                then(nc.vector.tensor_reduce(mx, sim, AX.X, ALU.max))
                ts(mx, mx, -float(D) ** -0.5, None, ALU.mult).then_inc(S("sim_max"), 1)

            def add5(b):
                ve.wait_ge(S("y5_part"), 2 * (b + 1))
                if b == 0:
                    ve.wait_ge(S("residual"), 8)
                tt(xrow[:, 1, b], bank(7)[:, (b % 4) * D:(b % 4 + 1) * D], xres[:, b], ALU.add).then_inc(S("y5_out"), 1)

            def stat5(b):
                ve.wait_ge(S("y5_out"), b + 1)
                then(nc.vector.bn_stats(stats[:, b], xrow[:, 1, b]))
                then(nc.vector.bn_aggr(mv[:, b], stats[:, b]))

            shift(0)
            for k in range(2 * B):
                ve.wait_ge(S("exp5"), 4 * (k + 1))
                then(nc.vector.reciprocal(s5_rden[:, k % 2], s5_den[:, k % 2]))
                pr = s5_p[:, k % 2]
                tt(pr, pr, s5_rden[:, k % 2].unsqueeze(2).to_broadcast([P, 4, KV]), ALU.mult).then_inc(S("prob5"), 1)
                if k >= 4 and k % 2 == 0:
                    add5(k // 2 - 2)
                if k + 1 < 2 * B:
                    shift(k + 1)
                if k >= 4 and k % 2 == 0:
                    stat5(k // 2 - 2)
                ve.wait_ge(S("probT5_mm"), 8 * (k + 1))
                if k >= 2:
                    ve.wait_ge(S("z5_mm"), k - 1)
                nc.vector.tensor_copy(s5_pT[:, k % 2, 1], bank(5)).then_inc(S("probT5_lat"), 1)
            add5(B - 2)
            stat5(B - 2)
            ts(veps[:, 0:HB], mv[:, 0:HB, 1], EPS, None, ALU.add).then_inc(S("var"), 1)
            norm_finish(5, 0, xrow[:, 1], xrow[:, 1])
            add5(B - 1)
            stat5(B - 1)
            ts(veps[:, HB:], mv[:, HB:, 1], EPS, None, ALU.add).then_inc(S("var"), 1)
            norm_finish(5, 1, xrow[:, 1], xrow[:, 1])

            ve.wait_ge(S("one_minus_mu"), 2)
            for g in range(2):
                h = slice(g * HB, (g + 1) * HB)
                ve.wait_ge(S("xpad"), g + 2)
                for n in range(2):
                    step(ts(mixed[:, n, h], xpad[:, h, 0:T], omm[:, n:n + 1], None, ALU.mult))
                join()
                for n, mu in enumerate(("mu_k", "mu_r")):
                    stt(mixed[:, n, h], xpad[:, h, 1:], W(mu), mixed[:, n, h], ALU.mult, ALU.add).then_inc(S("mixed"), 1)
            for g in range(2):
                h = slice(g * 512, (g + 1) * 512)
                ve.wait_ge(S("k_relu"), g + 1)
                tt(kact[:, h], kact[:, h], kact[:, h], ALU.mult).then_inc(S("k_act"), 1)

            def gated_residual(g):
                h = slice(g * 512, (g + 1) * 512)
                ve.wait_ge(S("recept"), g + 1)
                ve.wait_ge(S("kv_mm"), (g + 1) * HB)
                then(tt(gate6[:, h], gate6[:, h], bank(4 + g), ALU.mult))
                then(tt(xrow[:, 0, g * HB:(g + 1) * HB], xrow[:, 1, g * HB:(g + 1) * HB],
                        gate6[:, h].rearrange("p (b c) -> p b c", b=HB), ALU.add))

            norms([(6, g, xrow[:, 0], xrow[:, 0], lambda g=g: gated_residual(g)) for g in range(2)])

        @block.gpsimd
        def _(po):
            count = [0]

            def step(ins):
                count[0] += 1
                ins.then_inc(S("pool_step"), 1)

            def join():
                po.wait_ge(S("pool_step"), count[0])

            def then(ins):
                step(ins)
                join()

            tt, ts = nc.gpsimd.tensor_tensor, nc.gpsimd.tensor_scalar
            nc.gpsimd.memset(low, 0.0).then_inc(S("cleared"), 1)
            nc.gpsimd.memset(att, 0.0).then_inc(S("cleared"), 1)
            nc.gpsimd.memset(mhalf[:], -0.5).then_inc(S("cleared"), 1)
            nc.gpsimd.memset(decay, 0.0).then_inc(S("cleared"), 1)
            po.wait_ge(S("cleared"), 4)
            step(nc.gpsimd.memset(decay.rearrange("p c t i -> p c (t i)")[:, :, 0::C + 1], 1.0))
            nc.gpsimd.memset(state[:, 0], 0.0).then_inc(S("state_zero"), 1)
            join()
            po.wait_ge(S("cleared"), 4)
            po.wait_ge(S("ctx_var"), 1)
            tt(crstd[0:TC], cveps[0:TC], mhalf[0:TC], ALU.pow).then_inc(S("ctx_rstd"), 1)
            po.wait_ge(S("gates"), 2)
            for t in range(1, C):
                ins = tt(decay[:, :, t, 0:t], decay[:, :, t - 1, 0:t],
                         alpha[:, :, t:t + 1].to_broadcast([P, NC, t]), ALU.mult)
                if t < C - 1:
                    then(ins)
            ins.then_inc(S("decayed"), 1)
            po.wait_ge(S("decayed"), 1)
            tt(gcum, decay[:, :, :, 0], alpha[:, :, 0:1].to_broadcast([P, NC, C]), ALU.mult).then_inc(S("decayed"), 1)
            po.wait_ge(S("decayed"), 2)
            tt(bgcum, gcum, beta, ALU.mult).then_inc(S("decayed"), 1)
            tt(bdecay, decay, beta.unsqueeze(3).to_broadcast([P, NC, C, C]), ALU.mult).then_inc(S("decayed"), 1)
            po.wait_ge(S("unit"), 2)
            Kc = K.rearrange("p (c t) j -> p c t j", t=C)
            Qc = Q.rearrange("p (c t) j -> p c t j", t=C)
            at = 0
            for t in range(C):
                n = NC * (t + 1) * DH
                tt(gram_q[:, at:at + n].rearrange("p (c i j) -> p c i j", i=t + 1, j=DH),
                   Qc[:, :, t:t + 1, :].to_broadcast([P, NC, t + 1, DH]), Kc[:, :, 0:t + 1, :],
                   ALU.mult).then_inc(S("gram_q"), 1)
                at += n
            po.wait_ge(S("ctx_norm"), B)
            po.wait_ge(S("ctxT5_mm"), B)
            po.wait_ge(S("rows_in"), 16)
            then(tt(kv_ctx[0:TC], kv_ctx[0:TC],
                    row_in[0:TC, ROWS.index("g_med")].unsqueeze(1).to_broadcast([TC, B, D]), ALU.mult))
            tt(kv_ctx[0:TC], kv_ctx[0:TC], row_in[0:TC, ROWS.index("be_med")].unsqueeze(1).to_broadcast([TC, B, D]),
               ALU.add).then_inc(S("kv_ctx"), 1)
            step(tt(Qg, Qc, gcum.unsqueeze(3).to_broadcast([P, NC, C, DH]), ALU.mult))
            po.wait_ge(S("att_raw"), C)
            step(tt(att, att, decay, ALU.mult))
            join()
            po.wait_ge(S("unit"), 2)
            for c in range(NC):
                if c:
                    po.wait_ge(S("state_ready"), c)
                if c >= NR:
                    po.wait_ge(S("o_mm"), c - NR + 1)
                tt(prod_s[:, :, c % NR].rearrange("p j t i -> p t i j"), Qg[:, c].unsqueeze(2).to_broadcast([P, C, DH, DH]),
                   state[:, c].unsqueeze(1).to_broadcast([P, C, DH, DH]), ALU.mult).then_inc(S("prods"), 1)
                po.wait_ge(S("u_ready"), c + 1)
                tt(prod_a[:, :, c % NR].rearrange("p j t i -> p t i j"), att[:, c].unsqueeze(2).to_broadcast([P, C, DH, C]),
                   U[:, c].rearrange("p j i -> p i j").unsqueeze(1).to_broadcast([P, C, DH, C]),
                   ALU.mult).then_inc(S("prods"), 1)

            def power(n, g):
                h = slice(g * HB, (g + 1) * HB)
                po.wait_ge(S("var"), half(n, g))
                tt(rstd[:, h], veps[:, h], mhalf[:, h], ALU.pow).then_inc(S("rstd"), 1)

            def residual(n, g, bias):
                h = slice(g * HB, (g + 1) * HB)
                po.wait_ge(S("normed"), normed(n - 1, (g + 1) * HB))
                tt(xres[:, h], xrow[:, (n - 1) % 2, h], bias.unsqueeze(1).to_broadcast([P, HB, D]),
                   ALU.add).then_inc(S("residual"), 1)

            po.wait_ge(S("late_in"), 16)
            step(ts(s3_th[:, 0:NF], W("theta"), 1.0, None, ALU.mult))
            step(ts(s3_th[:, NF:], W("theta"), TWO_PI / 4, None, ALU.add))
            join()
            then(ts(s3_n, s3_th, 1 / TWO_PI, ROUND, ALU.mult, ALU.add))
            then(ts(s3_n, s3_n, ROUND, None, ALU.subtract))
            then(ts(s3_sin, s3_n, 6.28125, None, ALU.mult))
            then(tt(s3_th, s3_th, s3_sin, ALU.subtract))
            then(ts(s3_sin, s3_n, TWO_PI - 6.28125, None, ALU.mult))
            then(tt(s3_th, s3_th, s3_sin, ALU.subtract))
            ts(s3_th, s3_th, PI_F, -PI_F, ALU.min, ALU.max).then_inc(S("theta"), 1)
            po.wait_ge(S("theta"), 1)
            then(ts(s3_bias, W("b1"), 0.1, None, ALU.mult))
            tt(s3_bias, s3_bias, s3_th[:, 0:NF], ALU.add).then_inc(S("theta"), 1)
            po.wait_ge(S("theta_sin"), 1)
            step(tt(s3_n[:, 0:NF], s3_sin[:, NF:], W("w_re"), ALU.mult))
            step(tt(s3_n[:, NF:], s3_sin[:, 0:NF], W("w_im"), ALU.mult))
            join()
            then(tt(s3_cf, s3_n[:, 0:NF], s3_n[:, NF:], ALU.add))
            then(tt(s3_cf, s3_cf, W("w_im"), ALU.mult))
            ts(s3_cf, s3_cf, 0.1, None, ALU.mult).then_inc(S("gate_factor"), 1)
            power(1, 0)
            power(1, 1)
            residual(2, 0, row_in[:, ROWS.index("bo0")])
            residual(2, 1, row_in[:, ROWS.index("bo0")])
            power(2, 0)
            power(2, 1)

            def reduce_angle(k):
                po.wait_ge(S("turns"), k + 1)
                tt(s3_ang[:, k % 2], s3_ang[:, k % 2], s3_t, ALU.subtract).then_inc(S("reduced"), 1)

            for g in range(2):
                residual(3, g, row_in[:, ROWS.index("b2")])
            for k in range(NF):
                reduce_angle(k)
            power(3, 0)
            power(3, 1)
            residual(4, 0, row_in[:, ROWS.index("b_out")])
            residual(4, 1, row_in[:, ROWS.index("b_out")])
            for n in range(NH):
                ts(diag_d[:, n], ident, W("d_skip")[:, n:n + 1], None, ALU.mult).then_inc(S("diag_d"), 1)
            po.wait_ge(S("normed"), normed(3))
            nc.gpsimd.memset(fade.rearrange("p n (b t) -> p (n b) t", t=T)[:, :, 0:1], 0.0).then_inc(S("fade_zero"), 1)
            po.wait_ge(S("dt_exp"), 2)
            then(ts(dtu[:, 1], dt_e[:, 1], 1.0, None, ALU.add))
            then(ts(dtu[:, 1], dtu[:, 1], 1.0, None, ALU.subtract))
            then(tt(dtu[:, 1], dt_e[:, 1], dtu[:, 1], ALU.subtract))
            po.wait_ge(S("dt_relu"), 2)
            po.wait_ge(S("dt_part"), 1)
            tt(dt[:, 1], dt[:, 1], dtu[:, 1], ALU.add).then_inc(S("dt_part"), 1)
            po.wait_ge(S("a_exp"), 1)
            ts(neg_a, neg_a, -1.0, None, ALU.mult).then_inc(S("neg_a"), 1)
            for k in range(NS * NH - 1):
                s = k // NH
                po.wait_ge(S("scan"), k + 1)
                po.wait_ge(S("c_wide"), s + 1)
                if k >= 2:
                    po.wait_ge(S("seen_used"), k - 1)
                tt(seen[:, k % 2], hist[:, k % 2], c_wide[:, s % 2], ALU.mult).then_inc(S("read_out"), 1)
            for g in range(2):
                power(4, g)
            for g in range(2):
                power(7, g)
            for g in range(2):
                residual(5, g, fold_bo[:])
            po.wait_ge(S("turned"), 4 * B)
            po.wait_ge(S("normed"), normed(7))
            then(tt(kv_lat[:], kv_lat[:], row_in[:, ROWS.index("g_lat")].unsqueeze(1).to_broadcast([P, B, D]), ALU.mult))
            tt(kv_lat[:], kv_lat[:], row_in[:, ROWS.index("be_lat")].unsqueeze(1).to_broadcast([P, B, D]),
               ALU.add).then_inc(S("kv_lat"), 1)
            po.wait_ge(S("normed"), normed(4))
            ts(omm[:, 0:1], W("mu_k"), -1.0, 1.0, ALU.mult, ALU.add).then_inc(S("one_minus_mu"), 1)
            ts(omm[:, 1:2], W("mu_r"), -1.0, 1.0, ALU.mult, ALU.add).then_inc(S("one_minus_mu"), 1)
            nc.gpsimd.memset(xpad[:, :, 0:1], 0.0).then_inc(S("xpad"), 1)
            for n in (5, 6):
                for g in range(2):
                    power(n, g)

        @block.scalar
        def _(ac):
            act = nc.scalar.activation

            def columns_out(n):
                for g in range(2):
                    ac.wait_ge(S("turned"), (n - 1) * B + HB * (g + 1))
                    act(xcol[:, g * HB:(g + 1) * HB], bank(6 + g).rearrange("p (b t) -> p b t", b=HB),
                        ACT.Copy).then_inc(S("xcol"), 1)

            for b in range(0, B, 2):
                ac.wait_ge(S("qkv_mm"), b + 1)
                act(qkvt[:, :, b], bank(b)[:, 0:3 * D + 2 * H].rearrange("p (n h) -> p n h", h=H), ACT.Copy).then_inc(S("qkv_even"), 1)
            ac.wait_ge(S("gates_turned"), 1)
            for n, dst in enumerate((gates[:, 0:T], gates[:, T:])):
                act(dst, bank(6)[:, n * T:(n + 1) * T], ACT.Sigmoid, bias=W("gate_bias")[:, n:n + 1]).then_inc(S("gates"), 1)
            for n in range(2):
                ac.wait_ge(S("kq_turned"), n + 1)
                act(square[:, n * T * DH:(n + 1) * T * DH].rearrange("p (t j) -> p j t", j=DH),
                    bank(2 * n, 2).rearrange("p (j t) -> p j t", j=DH), ACT.Square).then_inc(S("square"), 1)
            ac.wait_ge(S("square_sum"), 3)
            act(norm2, norm2, ACT.Sqrt).then_inc(S("norm_root"), 1)
            for dst, sem, k in ((fold_qk, "fold_qk", 0), (fold_vo, "fold_vo", 2)):
                for g in range(2):
                    ac.wait_ge(S(sem + "_mm"), 4 * (g + 1))
                    act(dst[:, 4 * g:4 * g + 4], bank(k + g).rearrange("p (h c) -> p h c", h=4), ACT.Copy).then_inc(S(sem), 1)
            ac.wait_ge(S("fold_bq_mm"), 1)
            act(fold_bq[:], bank(4)[:, 0:XH], ACT.Copy).then_inc(S("fold_bq"), 1)
            ac.wait_ge(S("late_in"), 16)
            act(pick[:], W("pick")[0:96].unsqueeze(2).to_broadcast([96, 2 * NS, P]), ACT.Copy).then_inc(S("pick"), 1)
            for g in range(2):
                ac.wait_ge(S("ctxT5_mm"), HB * (g + 1))
                act(kvT[:, g * HB:(g + 1) * HB, 0:TC], bank(g).rearrange("p (b t) -> p b t", b=HB)[:, :, 0:TC],
                    ACT.Identity, bias=W("be_med"), scale=W("g_med")).then_inc(S("kvT_ctx"), 1)
            ac.wait_ge(S("theta"), 1)
            act(s3_sin, s3_th, ACT.Sin).then_inc(S("theta_sin"), 1)
            for g in range(2):
                ac.wait_ge(S("o_mm"), NR * (g + 1))
                act(osb.rearrange("p (i t) -> p i t", i=DH)[:, :, g * 64:(g + 1) * 64],
                    bank(6 + g).rearrange("p (t i) -> p i t", i=DH), ACT.Copy).then_inc(S("osb"), 1)
            for g in range(2):
                ac.wait_ge(S("o_rows_mm"), 4 * (g + 1))
                act(ot.rearrange("p (n i) -> p i n", i=DH)[:, 4 * g:4 * g + 4],
                    bank(g).rearrange("p (i n) -> p i n", i=4), ACT.Copy).then_inc(S("o_rows"), 1)
            for g in range(2):
                ac.wait_ge(S("o_cols_mm"), HB * (g + 1))
                act(otT[:, g * 512:(g + 1) * 512], bank(2 + g), ACT.Copy).then_inc(S("o_cols"), 1)
            columns_out(1)
            for g in range(2):
                ac.wait_ge(S("q0_mm"), g + 1)
                act(s2_q[:, g * 512:(g + 1) * 512], bank(g), ACT.Identity, bias=W("bq0")).then_inc(S("q0"), 1)
            for g in range(2):
                e = s2_e[:, g * HB * NK:(g + 1) * HB * NK]
                ac.wait_ge(S("score0_shift"), g + 1)
                act(e, e, ACT.Exp, scale=float(DH) ** -0.5).then_inc(S("exp0"), 1)
            for g in range(2):
                ac.wait_ge(S("probT0_mm"), HB * (g + 1))
                act(s2_pT[0:NK, g * 512:(g + 1) * 512], bank(4 + g)[0:NK], ACT.Copy).then_inc(S("probT0"), 1)
            for g in range(2):
                ac.wait_ge(S("o0_mm"), HB * (g + 1))
                act(s2_oT[:, g * 512:(g + 1) * 512], bank(g), ACT.Identity, bias=W("bv0")).then_inc(S("o0"), 1)
            columns_out(2)

            def sine(k):
                ac.wait_ge(S("clamped"), k + 1)
                act(s3_ang[:, k % 2], s3_ang[:, k % 2], ACT.Sin).then_inc(S("sine"), 1)

            def hidden_out(k):
                if k >= 2:
                    ac.wait_ge(S("act3"), k - 1)
                for m in range(2):
                    f = 2 * (k % 2) + m
                    ac.wait_ge(S("hid_mm"), 2 * k + m + 1)
                    act(s3_ang[:, k % 2, m * 512:(m + 1) * 512], bank(2 * (k % 2) + m), ACT.Identity,
                        bias=s3_bias[:, f:f + 1], scale=0.1).then_inc(S("angle"), 1)
                for m in range(2):
                    f = 2 * (k % 2) + m
                    act(s3_hid[:, k % 2, m * 512:(m + 1) * 512], bank(2 * (k % 2) + m), ACT.Identity,
                        bias=W("b1")[:, f:f + 1]).then_inc(S("hid"), 1)

            hidden_out(0)
            for k in range(NF):
                if k + 1 < NF:
                    hidden_out(k + 1)
                sine(k)
            columns_out(3)
            for g in range(2):
                for n in range(NH):
                    ac.wait_ge(S("u_mm"), NH * g + n + 1)
                    act(u4[:, n, g * 512:(g + 1) * 512], bank(2 * g + n), ACT.Silu,
                        bias=W("b_in")[:, n:n + 1]).then_inc(S("u_in"), 1)
            for g in range(2):
                ac.wait_ge(S("xdbl_mm"), g + 1)
                act(bc_f[0:32, g * 512:(g + 1) * 512], bank(4 + g)[0:32], ACT.Identity,
                    bias=W("b_x")[0:32]).then_inc(S("xdbl"), 1)
            for n, k in enumerate((6, 0)):
                ac.wait_ge(S("dt_mm"), n + 1)
                act(dt_e[:, n], bank(k, 2), ACT.Abs, bias=W("b_dt")[:, n:n + 1]).then_inc(S("dt_abs"), 1)
                act(dt[:, n], bank(k, 2), ACT.Relu, bias=W("b_dt")[:, n:n + 1]).then_inc(S("dt_relu"), 1)
                ac.wait_ge(S("dt_abs"), n + 1)
                act(dt_e[:, n], dt_e[:, n], ACT.Exp, scale=-1.0).then_inc(S("dt_exp"), 1)
            act(neg_a.rearrange("p n s -> p (n s)"), W("a_log"), ACT.Exp).then_inc(S("a_exp"), 1)
            for n in range(NH):
                ac.wait_ge(S("dt_exp"), n + 1)
                act(dt_l[:, n], dt_e[:, n], ACT.Ln, bias=1.0).then_inc(S("dt_log"), 1)
            ac.wait_ge(S("fade_zero"), 1)
            ac.wait_ge(S("neg_a"), 1)

            def wide(s):
                ac.wait_ge(S("wide_mm"), 2 * s + 1)
                if s >= 2:
                    ac.wait_ge(S("drive"), NH * (s - 1))
                act(b_wide[:, s % 2], bank(4, 2), ACT.Copy).then_inc(S("b_wide"), 1)
                ac.wait_ge(S("wide_mm"), 2 * s + 2)
                if s >= 2:
                    ac.wait_ge(S("read_out"), NH * (s - 1))
                act(c_wide[:, s % 2], bank(6, 2), ACT.Copy).then_inc(S("c_wide"), 1)

            wide(0)
            for s in range(NS):
                if s == 0:
                    ac.wait_ge(S("dt"), NH)
                for n in range(NH):
                    k = s * NH + n
                    if k >= 3:
                        ac.wait_ge(S("scan"), k - 2)
                    act(fade[:, k % 3].rearrange("p (b t) -> p b t", t=T)[:, :, 1:],
                        dt[:, n].rearrange("p (b t) -> p b t", t=T)[:, :, 1:], ACT.Exp,
                        scale=neg_a[:, n, s:s + 1]).then_inc(S("fade"), 1)
                if s + 1 < NS:
                    wide(s + 1)
            ac.wait_ge(S("gz_in"), 2 * NH)
            for n in range(NH):
                act(gz[:, n], gz[:, n], ACT.Silu).then_inc(S("gz"), 1)
            for g in range(2):
                ac.wait_ge(S("turned"), 3 * B + HB * (g + 1))
                act(kvT[:, g * HB:(g + 1) * HB, TC:], bank(6 + g).rearrange("p (b t) -> p b t", b=HB), ACT.Identity,
                    bias=W("be_lat"), scale=W("g_lat")).then_inc(S("kvT_lat"), 1)
            for h in range(XH):
                ac.wait_ge(S("q5_mm"), h + 1)
                act(s5_q[:, h], bank(2 * (h % 2), 2), ACT.Identity, bias=fold_bq[:, h:h + 1]).then_inc(S("q5"), 1)
            for k in range(2 * B + 2):
                if k < 2 * B:
                    ac.wait_ge(S("sim_max"), k + 1)
                    if k >= 2:
                        ac.wait_ge(S("probT5_mm"), 8 * (k - 1))
                    for h in range(4):
                        act(s5_p[:, k % 2, h], bank(2 * (k % 2), 2).rearrange("p (h n) -> p h n", h=4)[:, h, 0:KV],
                            ACT.Exp, bias=s5_max[:, k % 2, h:h + 1], scale=float(D) ** -0.5,
                            accum_out=s5_den[:, k % 2, h:h + 1]).then_inc(S("exp5"), 1)
                if 1 <= k <= 2 * B:
                    j = k - 1
                    ac.wait_ge(S("probT5_mm"), 8 * (j + 1))
                    if j >= 2:
                        ac.wait_ge(S("z5_mm"), j - 1)
                    act(s5_pT[0:TC, j % 2, 0], bank(4)[0:TC], ACT.Copy).then_inc(S("probT5_ctx"), 1)
                if k >= 2:
                    j = k - 2
                    ac.wait_ge(S("z5_mm"), j + 1)
                    if j >= 2:
                        ac.wait_ge(S("y5_part"), j - 1)
                    act(s5_z[:, j % 2], bank(6), ACT.Copy).then_inc(S("z5"), 1)
            for g in range(2):
                ac.wait_ge(S("turned"), 4 * B + HB * (g + 1))
                act(xpad[:, g * HB:(g + 1) * HB, 1:], bank(4 + g).rearrange("p (b t) -> p b t", b=HB),
                    ACT.Copy).then_inc(S("xpad"), 1)
            for g in range(2):
                ac.wait_ge(S("k6_mm"), g + 1)
                act(kact[:, g * 512:(g + 1) * 512], bank(2 + g), ACT.Relu).then_inc(S("k_relu"), 1)
            for g in range(2):
                ac.wait_ge(S("r6_mm"), HB * (g + 1))
                act(gate6[:, g * 512:(g + 1) * 512], bank(g), ACT.Sigmoid).then_inc(S("recept"), 1)

        @block.tensor
        def _(pe):
            mm, turn = nc.tensor.matmul, nc.tensor.transpose
            xT = W("xT").rearrange("p (b t) -> p b t", b=B)

            def turn_rows(n, src, k=6):
                for b in range(B):
                    pe.wait_ge(S("normed"), normed(n, b + 1))
                    turn(bank(k, 2)[:, b * T:(b + 1) * T], src[:, b], ident).then_inc(S("turned"), 1)

            pe.wait_ge(S("first_in"), 16)
            for b in range(B):
                mm(bank(b)[:, 0:3 * D + 2 * H], xT[:, b], W("w_qkvgb"), start=True, stop=True).then_inc(S("qkv_mm"), 1)
            pe.wait_ge(S("qkv_even"), B // 2)
            pe.wait_ge(S("qkv_odd"), B // 2)
            for n in range(2):
                ins = turn(bank(6)[:, n * T:(n + 1) * T], qkvt[:, 3 * DH + n].rearrange("p b h -> p (b h)"), ident)
            ins.then_inc(S("gates_turned"), 1)
            for n, (k, sem) in enumerate(((1, "kq_turned"), (0, "kq_turned"), (2, "v_turned"))):
                for j in range(DH):
                    ins = turn(bank(2 * n, 2)[:, j * T:(j + 1) * T],
                               qkvt[:, k * DH + j].rearrange("p b h -> p (b h)"), ident)
                ins.then_inc(S(sem), 1)
            pe.wait_ge(S("fold_in"), 16)
            pe.wait_ge(S("unit"), 2)
            fq, fk = (W(n).rearrange("p (h c) -> p h c", h=XH) for n in ("wq1T", "wk1T"))
            fv, fo = (W(n).rearrange("p (h c) -> p h c", h=XH) for n in ("wv1T", "wo1"))
            for h in range(XH):
                mm(bank(0, 2)[:, h * D:(h + 1) * D], fq[:, h], fk[:, h], start=True, stop=True).then_inc(S("fold_qk_mm"), 1)
            for h in range(XH):
                mm(bank(2, 2)[:, h * D:(h + 1) * D], fv[:, h], fo[:, h], start=True, stop=True).then_inc(S("fold_vo_mm"), 1)
            pe.wait_ge(S("vector_step"), 1)
            for h in range(XH):
                ins = mm(bank(4)[:, h:h + 1], fk[:, h], W("bq1")[:, h:h + 1], start=True, stop=True)
            ins.then_inc(S("fold_bq_mm"), 1)
            for h in range(XH):
                ins = mm(bank(5)[:, 0:D], W("bv1")[:, h:h + 1].to_broadcast([P, P]), fo[:, h],
                         start=(h == 0), stop=(h == XH - 1))
            ins.then_inc(S("fold_bo_mm"), 1)
            pe.wait_ge(S("fold_qk"), 2)
            for b in range(B):
                pe.wait_ge(S("ctx_norm"), b + 1)
                turn(bank(0, 2)[:, b * T:b * T + TC], kv_ctx[0:TC, b], ident[0:TC, 0:TC]).then_inc(S("ctxT5_mm"), 1)
            pe.wait_ge(S("kvT_ctx"), 2)
            pe.wait_ge(S("early_in"), 16)
            cT = W("ctxT").rearrange("p (b t) -> p b t", b=B)
            for g in range(2):
                mm(bank(g)[:, 0:HB * TC], W("wk0"), W("ctxT")[:, g * HB * TC:(g + 1) * HB * TC],
                   start=True, stop=True).then_inc(S("key0_mm"), 1)
            pe.wait_ge(S("fold_vo"), 2)
            for g in range(2):
                for b in range(g * HB, (g + 1) * HB):
                    ins = mm(bank(2, 2)[0:NK, b * D:(b + 1) * D], cT[:, b, 0:NK], W("wv0"), start=True, stop=True)
                ins.then_inc(S("val0_mm"), 1)
            for c in range(0, NC, 2):
                at = c % NR * C * DH
                pe.wait_ge(S("prods"), 2 * (c + 2))
                for n, pr in enumerate((prod_s, prod_a)):
                    for j in range(C):
                        ins = mm(bank(6 + c // NR)[:, at:at + 2 * C * DH], ident,
                                 pr[:, j, c % NR:c % NR + 2].rearrange("p c t i -> p (c t i)"),
                                 start=(n == 0 and j == 0), stop=(n == 1 and j == C - 1))
                ins.then_inc(S("o_mm"), 2)
            pe.wait_ge(S("osb"), 2)
            pe.wait_ge(S("key0"), 2)
            for i in range(DH):
                turn(bank(0, 2)[:, i * P:(i + 1) * P], osb[:, i * T:(i + 1) * T], ident).then_inc(S("o_rows_mm"), 1)
            pe.wait_ge(S("o_rows"), 2)
            pe.wait_ge(S("val0"), 2)
            for b in range(B):
                turn(bank(2, 2)[:, b * T:(b + 1) * T], ot[:, b * D:(b + 1) * D], ident).then_inc(S("o_cols_mm"), 1)
            pe.wait_ge(S("fold_bq"), 1)
            pe.wait_ge(S("fold_bo"), 1)
            for b in range(B):
                if b % HB == 0:
                    pe.wait_ge(S("o_cols"), b // HB + 1)
                mm(bank(4, 2)[:, b * D:(b + 1) * D], otT[:, b * T:(b + 1) * T], W("w_out0"),
                   start=True, stop=True).then_inc(S("projected"), 1)
            turn_rows(1, xrow[:, 1])
            for g in range(2):
                pe.wait_ge(S("xcol"), 0 + g + 1)
                mm(bank(g), W("wq0"), xcol[:, g * HB:(g + 1) * HB], start=True, stop=True).then_inc(S("q0_mm"), 1)
            for b in range(B):
                if b % HB == 0:
                    pe.wait_ge(S("q0"), b // HB + 1)
                mm(bank(2, 2)[:, b * T:b * T + NK], s2_q[:, b * T:(b + 1) * T], key0[:, b],
                   start=True, stop=True).then_inc(S("score0"), 1)
            for b in range(B):
                if b % HB == 0:
                    pe.wait_ge(S("prob0"), b // HB + 1)
                turn(bank(4, 2)[0:NK, b * T:(b + 1) * T], s2_p[:, b * NK:(b + 1) * NK], ident).then_inc(S("probT0_mm"), 1)
            for b in range(B):
                if b % HB == 0:
                    pe.wait_ge(S("probT0"), b // HB + 1)
                mm(bank(0, 2)[:, b * T:(b + 1) * T], val0[0:NK, b], s2_pT[0:NK, b * T:(b + 1) * T],
                   start=True, stop=True).then_inc(S("o0_mm"), 1)
            for b in range(B):
                if b % HB == 0:
                    pe.wait_ge(S("o0"), b // HB + 1)
                mm(bank(2, 2)[:, b * D:(b + 1) * D], s2_oT[:, b * T:(b + 1) * T], W("wo0"),
                   start=True, stop=True).then_inc(S("projected"), 1)
            turn_rows(2, xrow[:, 0])
            w2 = W("w2").rearrange("p (f c) -> p f c", f=NF)
            def hidden(k):
                g = k // 2
                if k >= 2:
                    pe.wait_ge(S("hid"), 2 * (k - 1))
                pe.wait_ge(S("xcol"), 2 + g + 1)
                for m in range(2):
                    f = 2 * (k % 2) + m
                    mm(bank(2 * (k % 2) + m), W("w1")[:, f * P:(f + 1) * P], xcol[:, g * HB:(g + 1) * HB],
                       start=True, stop=True).then_inc(S("hid_mm"), 1)

            def project3(g):
                pe.wait_ge(S("act3"), 2 * (g + 1))
                for b in range(g * HB, (g + 1) * HB):
                    for f in range(NF):
                        ins = mm(bank(4, 2)[:, b * D:(b + 1) * D], s3_act[:, f, b * T:(b + 1) * T], w2[:, f],
                                 start=(f == 0), stop=(f == NF - 1))
                    ins.then_inc(S("projected"), 1)

            for k in range(NF):
                hidden(k)
            project3(0)
            project3(1)
            turn_rows(3, xrow[:, 1])
            def project4(n, g, k, sem):
                mm(bank(k), W("w_in")[:, n * P:(n + 1) * P], xcol[:, g * HB:(g + 1) * HB],
                   start=True, stop=True).then_inc(S(sem), 1)

            for g in range(2):
                pe.wait_ge(S("xcol"), 4 + g + 1)
                for n in range(NH):
                    project4(n, g, 2 * g + n, "u_mm")
            wx = W("w_x").rearrange("p (n s) -> p n s", n=NH)
            for g in range(2):
                pe.wait_ge(S("u_in"), NH * (g + 1))
                for n in range(NH):
                    ins = mm(bank(4 + g)[0:32], wx[:, n], u4[:, n, g * 512:(g + 1) * 512], start=(n == 0), stop=(n == NH - 1))
                ins.then_inc(S("xdbl_mm"), 1)
            wdt = W("w_dt").rearrange("p (n d) -> p n d", n=NH)
            for m, k in enumerate((6, 0)):
                for g in range(2):
                    for n in range(NH):
                        ins = mm(bank(k + g), wdt[:, n, m * P:(m + 1) * P], u4[:, n, g * 512:(g + 1) * 512],
                                 start=(n == 0), stop=(n == NH - 1))
                ins.then_inc(S("dt_mm"), 1)
            pe.wait_ge(S("xdbl"), 2)
            for n in range(NH):
                for g in range(2):
                    project4(NH + n, g, 2 + 2 * n + g, "z_mm")
            pe.wait_ge(S("diag_d"), NH)
            for n in range(NH):
                if n:
                    pe.wait_ge(S("gz_in"), 2)
                else:
                    pe.wait_ge(S("dt_relu"), 2)
                for g in range(2):
                    mm(bank(2 * n + g), diag_d[:, n], u4[:, n, g * 512:(g + 1) * 512], start=True, stop=False)

            def widen(s):
                for n, sem in enumerate(("b_wide", "c_wide")):
                    if s:
                        pe.wait_ge(S(sem), s)
                    for g in range(2):
                        ins = mm(bank(4 + 2 * n + g), pick[:, n * NS + s], bc_parts[0:96, g * 512:(g + 1) * 512],
                                 start=True, stop=True)
                    ins.then_inc(S("wide_mm"), 1)

            pe.wait_ge(S("bc_parts"), 2)
            pe.wait_ge(S("pick"), 1)
            pe.wait_ge(S("gz_in"), 2 * NH)
            widen(0)
            widen(1)
            for s in range(NS):
                if s + 2 < NS:
                    widen(s + 2)
                if s + 1 < NS:
                    for n in range(NH):
                        k = s * NH + n
                        pe.wait_ge(S("read_out"), k + 1)
                        for g in range(2):
                            ins = mm(bank(2 * n + g), ident, seen[:, k % 2, g * 512:(g + 1) * 512],
                                     start=False, stop=False)
                        ins.then_inc(S("seen_used"), 1)
            for g in range(2):
                for n in range(NH):
                    k = (NS - 1) * NH + n
                    if n:
                        pe.wait_ge(S("read_last"), g + 1)
                    else:
                        pe.wait_ge(S("read_out"), k + 1)
                    mm(bank(2 * n + g), ident, seen[:, k % 2, g * 512:(g + 1) * 512],
                       start=False, stop=True).then_inc(S("y_mm"), 1)
            wo = W("w_out").rearrange("p (n c) -> p n c", n=NH)
            for b in range(B):
                if b % HB == 0:
                    pe.wait_ge(S("y_gated"), NH * (b // HB + 1))
                for n in range(NH):
                    ins = mm(bank(4, 2)[:, b * D:(b + 1) * D], yg[:, n, b * T:(b + 1) * T], wo[:, n],
                             start=(n == 0), stop=(n == NH - 1))
                ins.then_inc(S("projected"), 1)
            turn_rows(7, kv_lat)
            for h in range(XH):
                if h >= 2:
                    pe.wait_ge(S("q5"), h - 1)
                for g in range(2):
                    pe.wait_ge(S("kvT_lat"), g + 1)
                    ins = mm(bank(2 * (h % 2) + g), fold_qk[:, h], kvT[:, g * HB:(g + 1) * HB, TC:], start=True, stop=True)
                ins.then_inc(S("q5_mm"), 1)
            pe.wait_ge(S("q5"), XH)

            def similar(k):
                b, g = k // 2, k % 2
                if k >= 2:
                    pe.wait_ge(S("exp5"), 4 * (k - 1))
                for h in range(4):
                    mm(bank(2 * (k % 2), 2)[:, h * 256:h * 256 + KV], s5_q[:, 4 * g + h, b * T:(b + 1) * T], kvT[:, b],
                       start=True, stop=True).then_inc(S("sim"), 1)

            similar(0)
            for k in range(2 * B + 2):
                if k + 1 < 2 * B:
                    similar(k + 1)
                if k >= 2:
                    j = k - 2
                    b, g = j // 2, j % 2
                    pe.wait_ge(S("z5"), j + 1)
                    if g == 0 and b:
                        pe.wait_ge(S("y5_out"), b)
                    for h in range(4):
                        ins = mm(bank(7)[:, (b % 4) * D:(b % 4 + 1) * D], s5_z[:, j % 2, h * T:(h + 1) * T],
                                 fold_vo[:, 4 * g + h], start=(g == 0 and h == 0), stop=(g == 1 and h == 3))
                    ins.then_inc(S("y5_part"), 1)
                if k < 2 * B:
                    pe.wait_ge(S("prob5"), k + 1)
                    if k:
                        pe.wait_ge(S("probT5_ctx"), k)
                        pe.wait_ge(S("probT5_lat"), k)
                    for h in range(4):
                        turn(bank(4)[0:TC, h * T:(h + 1) * T], s5_p[:, k % 2, h, 0:TC], ident).then_inc(S("probT5_mm"), 1)
                        turn(bank(5)[:, h * T:(h + 1) * T], s5_p[:, k % 2, h, TC:], ident).then_inc(S("probT5_mm"), 1)
                if 1 <= k <= 2 * B:
                    j = k - 1
                    b = j // 2
                    if j == 0:
                        pe.wait_ge(S("kv_lat"), 1)
                        pe.wait_ge(S("kv_ctx"), 1)
                    else:
                        pe.wait_ge(S("z5"), j)
                    pe.wait_ge(S("probT5_ctx"), j + 1)
                    mm(bank(6), kv_ctx[0:TC, b], s5_pT[0:TC, j % 2, 0], start=True, stop=False)
                    pe.wait_ge(S("probT5_lat"), j + 1)
                    mm(bank(6), kv_lat[:, b], s5_pT[:, j % 2, 1], start=False, stop=True).then_inc(S("z5_mm"), 1)
            turn_rows(5, xrow[:, 1], 4)
            for g in range(2):
                pe.wait_ge(S("mixed"), 2 * g + 1)
                mm(bank(2 + g), W("w_k"), mixed[:, 0, g * HB:(g + 1) * HB], start=True, stop=True).then_inc(S("k6_mm"), 1)
                pe.wait_ge(S("mixed"), 2 * g + 2)
                for b in range(g * HB, (g + 1) * HB):
                    mm(bank(0, 2)[:, b * D:(b + 1) * D], mixed[:, 1, b], W("w_r"), start=True, stop=True).then_inc(S("r6_mm"), 1)
            for b in range(B):
                if b % HB == 0:
                    pe.wait_ge(S("k_act"), b // HB + 1)
                mm(bank(4, 2)[:, b * D:(b + 1) * D], kact[:, b * T:(b + 1) * T], W("w_v"),
                   start=True, stop=True).then_inc(S("kv_mm"), 1)


_INS = ["first", "x", "early", "context", "fold", "late", "rows"]


def layout(i):
    i = {k: np.asarray(v) for k, v in i.items()}

    def col(v):
        return v.reshape(-1, P).T

    def blocks(w):
        return w.reshape(-1, P, w.shape[-1]).transpose(1, 0, 2).reshape(P, -1)

    def tall(w):
        out = np.zeros((P,) + w.shape[1:], w.dtype)
        out[:w.shape[0]] = w
        return out

    def heads_t(w):
        return w.reshape(D, XH, D).transpose(2, 1, 0).reshape(D, -1)

    ch, tok = np.arange(P), np.arange(P)
    mask = (ch[:, None] // DH == tok[None, :] % H).astype(np.float32)
    v = {
        "xT": i["x"].transpose(2, 0, 1).reshape(P, BT),
        "w_qkvgb": np.concatenate([i["L0_attn_Wqkv"].reshape(3, H, DH, D).transpose(3, 0, 2, 1).reshape(D, 3 * D), i["L0_attn_Wg"].T, i["L0_attn_Wb"].T], 1),
        "gate_bias": np.stack([np.tile(i["L0_attn_bg"], B), np.tile(i["L0_attn_bb"], B)], 1),
        "ident": np.eye(P, dtype=np.float32),
        "w_out0": i["L0_attn_Wout"].T,
        "wq0": i["L0_xattn_Wq"].T, "wk0": i["L0_xattn_Wk"].T, "wv0": i["L0_xattn_Wv"].T, "wo0": i["L0_xattn_Wo"].T,
        "bq0": col(i["L0_xattn_bq"]), "bk0": col(i["L0_xattn_bk"]), "bv0": col(i["L0_xattn_bv"]),
        "mask_k": mask[:, :NK], "mask_v": mask.T,
        "ctxT": i["ctx_1024"].transpose(2, 0, 1).reshape(P, B * TC),
        "wq1T": heads_t(i["L1_xattn_Wq"]),
        "wk1T": heads_t(i["L1_xattn_Wkv"][:, :XH * D]), "wv1T": heads_t(i["L1_xattn_Wkv"][:, XH * D:]),
        "wo1": blocks(i["L1_xattn_Wo"]), "bq1": col(i["L1_xattn_bq"]), "bv1": col(i["L1_xattn_bkv"][XH * D:]),
        "w1": i["L0_ffn_W1"], "b1": col(i["L0_ffn_b1"]), "theta": col(i["L0_ffn_quantum_phases"]),
        "w_re": col(i["L0_ffn_quantum_weights_real"]), "w_im": col(i["L0_ffn_quantum_weights_imag"]),
        "w2": blocks(i["L0_ffn_W2"]),
        "w_in": i["L1_attn_W_in"], "b_in": col(i["L1_attn_b_in"]), "w_x": blocks(i["L1_attn_W_x"]),
        "w_dt": blocks(i["L1_attn_W_dt"]), "b_dt": col(i["L1_attn_b_dt"]), "w_out": blocks(i["L1_attn_W_out"]),
        "a_log": blocks(i["L1_attn_A_log"]), "d_skip": col(i["L1_attn_D_param"]),
        "b_x": tall(i["L1_attn_b_x"][:, None]),
        "g_med": col(i["L1_xattn_gamma_media"]), "be_med": col(i["L1_xattn_beta_media"]),
        "g_lat": col(i["L1_xattn_gamma_lat"]), "be_lat": col(i["L1_xattn_beta_lat"]),
        "w_r": i["L1_ffn_W_r"].T, "w_k": i["L1_ffn_W_k"].T, "w_v": i["L1_ffn_W_v"].T,
        "mu_r": col(i["L1_ffn_mu_r"]), "mu_k": col(i["L1_ffn_mu_k"]),
        "pick": tall(np.tile(np.eye(2 * NS, dtype=np.float32), (3, 1))),
    }
    packs = {p: np.ascontiguousarray(np.concatenate([v[n] for n, _ in cols], 1)) for p, cols in PACKS.items()}
    packs["x"] = i["x"].transpose(1, 0, 2)
    packs["context"] = i["ctx_1024"].transpose(1, 0, 2)
    packs["rows"] = np.stack([i["L0_xattn_bo"], i["L0_ffn_b2"], i["L1_attn_b_out"], i["L1_xattn_bo"],
                              i["L1_xattn_gamma_media"], i["L1_xattn_beta_media"],
                              i["L1_xattn_gamma_lat"], i["L1_xattn_beta_lat"]])
    return packs


def kernel(**inputs):
    import concourse.bacc as bacc
    from concourse.bass_utils import run_bass_kernel_spmd

    nc = bacc.Bacc("TRN2", target_bir_lowering=False, num_devices=1)
    packs = layout(inputs)
    arrays, args = {}, []
    for name in _INS:
        a = np.ascontiguousarray(packs[name])
        arrays[f"in_{name}_dram"] = a
        args.append(nc.dram_tensor(f"in_{name}_dram", a.shape, mybir.dt.from_np(a.dtype), kind="ExternalInput").ap())
    args.append(nc.dram_tensor("out_0_dram", (B, T, D), F32, kind="ExternalOutput").ap())
    decoder(nc, *args)
    r = run_bass_kernel_spmd(nc, [arrays], core_ids=[0])
    return r.results[0]["out_0_dram"]
```

```python
from contextlib import ExitStack

import numpy as np
import concourse.bass as bass
from concourse import mybir

F32 = mybir.dt.float32
BF16 = mybir.dt.bfloat16
ALU = mybir.AluOpType
ACT = mybir.ActivationFunctionType
AX = mybir.AxisListType

P = 128
B, T, D = 8, 128, 128
BT = B * T
HB = B // 2
BANK = 512
H, DH = 16, 8
C = 8
NC = T // C
TC = 120
NM = TC // 16
NK = NM * 16
FF = 512
NF = FF // P
DI = 256
NH = DI // P
NS = 16
XH = 8
KV = TC + T
EPS = 1e-5
TWO_PI = float(2 * np.pi)
PI_F = float(np.nextafter(np.float32(np.pi), np.float32(0)))
ROUND = 1.5 * 2.0 ** 23

PACKS = {
    "first": [("w_qkvgb", 3 * D + 2 * H), ("gate_bias", 2), ("xT", BT), ("ident", P)],
    "early": [("w_out0", D), ("wq0", D), ("wk0", D), ("wv0", D), ("wo0", D), ("bq0", 1), ("bk0", 1),
              ("bv0", 1), ("mask_k", NK), ("mask_v", D), ("ctxT", B * TC)],
    "fold": [("wq1T", XH * D), ("wk1T", XH * D), ("wv1T", XH * D), ("wo1", XH * D), ("bq1", XH), ("bv1", XH)],
    "late": [("w1", FF), ("b1", NF), ("theta", NF), ("w_re", NF), ("w_im", NF), ("w2", NF * D), ("w_in", 2 * DI),
             ("b_in", 2 * NH), ("w_x", NH * 2 * NS), ("w_dt", NH * DI), ("b_dt", NH), ("w_out", NH * D),
             ("a_log", NH * NS), ("d_skip", NH), ("b_x", 1), ("g_lat", 1), ("be_lat", 1),
             ("w_r", D), ("w_k", D), ("w_v", D), ("mu_r", 1), ("mu_k", 1),
             ("pick", 2 * NS)],
}
ROWS = ["bo0", "b2", "b_out", "bo1", "g_med", "be_med", "g_lat", "be_lat"]


def columns(pack):
    at, out = 0, {}
    for name, n in PACKS[pack]:
        out[name] = (at, n)
        at += n
    return out, at


def decoder(nc, first, x, early, context, fold, late, rows, out):
    with ExitStack() as ctx:
        sems = {}

        def S(name):
            if name not in sems:
                sems[name] = ctx.enter_context(nc.semaphore(name))
            return sems[name]

        def sb(name, shape, dt=F32):
            return ctx.enter_context(nc.sbuf_tensor(name, shape, dt))

        where, tiles = {}, {}
        for pack in PACKS:
            cols, n = columns(pack)
            tiles[pack] = sb(f"{pack}_in", [P, n])
            for name, (at, w) in cols.items():
                where[name] = (pack, at, w)

        def W(name):
            pack, at, w = where[name]
            return tiles[pack][:, at:at + w]

        row_in = sb("rows_in", [P, len(ROWS), D])
        pick = sb("pick_wide", [3 * 2 * NS, 2 * NS, P], BF16)
        ident = W("ident")

        xrow = sb("xrow", [P, 2, B, D])
        xres = sb("xres", [P, B, D])
        xcol = sb("xcol", [P, B, T])
        key0 = sb("key0", [P, B, NK])
        val0 = sb("val0", [P, B, D])
        kvT = sb("kvT", [P, B, KV])
        kv_ctx = sb("kv_ctx", [P, B, D])
        kv_lat = sb("kv_lat", [P, B, D])
        fold_qk = sb("fold_qk", [P, XH, D])
        fold_vo = sb("fold_vo", [P, XH, D])
        fold_bq = sb("fold_bq", [P, XH])
        fold_bo = sb("fold_bo", [P, D])
        stats = sb("stats", [P, B, 6])
        mv = sb("mv", [P, B, 2])
        veps = sb("veps", [P, B])
        rstd = sb("rstd", [P, B])
        cstats = sb("cstats", [P, B, 6])
        cmv = sb("cmv", [P, B, 2])
        cveps = sb("cveps", [P, B])
        crstd = sb("crstd", [P, B])
        mhalf = sb("mhalf", [P, B])
        lat_rstd = sb("lat_rstd", [P, B])
        table = sb("table", [P, 1])
        arena = sb("arena", [P, 27000])
        ps = ctx.enter_context(nc.psum_tensor("ps", [P, 8 * BANK], F32))

        NORMS = [1, 2, 3, 4, 7, 5, 6]
        PARTS = [(0, HB), (HB, B - 1), (B - 1, B)]

        def normed(n, k=B):
            return NORMS.index(n) * B + k

        def halves(n, g):
            return 2 * (n - 1) + g + 1 + (len(PARTS) - 2) * (n > 5)

        class Arena:
            def __init__(self):
                self.at = 0

            def __call__(self, n):
                self.at += n
                assert self.at <= arena.shape[1], self.at
                return arena[:, self.at - n:self.at]

        def bank(k, n=1):
            return ps[:, k * BANK:(k + n) * BANK]

        def rows_of(ap):
            return ap.rearrange("p (b c) -> p b c", b=B)

        A = Arena()
        qkvt = A(B * (3 * D + 2 * H)).rearrange("p (n b h) -> p n b h", b=B, h=H)
        square = A(2 * T * DH)
        end = A.at
        A.at = 0
        sub_t = A(NC * 2 * DH * C)
        solved = A.at
        A.at = 0
        u_terms = A(2 * C * DH * (DH + 1)).rearrange("p (n t i j) -> p n t i j", n=2, t=C, i=DH)
        s_terms = A(2 * DH * DH * (C + 1)).rearrange("p (n i j t) -> p n i j t", n=2, i=DH, j=DH)
        A.at = max(A.at, solved)
        Kend = A(T * DH).rearrange("p (c t j) -> p c t j", t=C, j=DH)
        NP = 2
        sub_p = A(NP * 2 * DH * C)
        assert A.at <= end
        A.at = end
        norm2 = A(2 * T)
        inv = A(2 * T)
        K = A(T * DH).rearrange("p (t j) -> p t j", j=DH)
        Q = A(T * DH).rearrange("p (t j) -> p t j", j=DH)
        gates = A(2 * T)
        decay = A(T * C).rearrange("p (c t i) -> p c t i", t=C, i=C)
        bdecay = A(T * C).rearrange("p (c t i) -> p c t i", t=C, i=C)
        gcum = A(T).rearrange("p (c t) -> p c t", t=C)
        bgcum = A(T).rearrange("p (c t) -> p c t", t=C)
        low = A(T * C).rearrange("p (c t i) -> p c t i", t=C, i=C)
        att = A(T * C).rearrange("p (c t i) -> p c t i", t=C, i=C)
        X = A(T * 2 * DH).rearrange("p (c t n) -> p c t n", t=C, n=2 * DH)
        U = A(T * DH).rearrange("p (c t i) -> p c t i", t=C, i=DH)
        state = A(NC * DH * DH).rearrange("p (c i j) -> p c i j", i=DH, j=DH)
        Qg = A(T * DH).rearrange("p (c t j) -> p c t j", t=C, j=DH)
        NR = NC // 2
        gram = A.at
        prod_o = A(2 * NR * DH * C * DH)
        gram_k = arena[:, gram:gram + NC * DH * C * (C - 1) // 2]
        gram_q = arena[:, gram + NC * DH * C * (C - 1) // 2:gram + NC * DH * C * C]
        osb, ot = K.rearrange("p t j -> p (t j)"), Q.rearrange("p t j -> p (t j)")
        otT = low.rearrange("p c t i -> p (c t i)")

        alpha = gates[:, 0:T].rearrange("p (c t) -> p c t", t=C)
        beta = gates[:, T:2 * T].rearrange("p (c t) -> p c t", t=C)
        prods = prod_o.rearrange("p (n j c t i) -> p n j c t i", n=2, j=DH, c=NR, t=C)
        prod_s, prod_a = prods[:, 0], prods[:, 1]

        A = Arena()
        s2_q = A(BT)
        s2_max, s2_den, s2_rden = A(B * H), A(B * H), A(B * H)
        s2_e, s2_p = A(B * NK), A(B * NK)
        s2_pT, s2_oT = A(BT), A(BT)
        s3_ang = A(NF * BT).rearrange("p (n t) -> p n t", n=NF)
        s3_banks = (0, 2, 6, 4)
        s3_t = A(2 * BT).rearrange("p (n t) -> p n t", n=2)
        s3_act = A(NF * BT).rearrange("p (n t) -> p n t", n=NF)
        s3_th, s3_n, s3_sin, s3_cf, s3_bias = (sb(f"s3_{name}", [P, n * NF])[:] for name, n in
                                               (("th", 2), ("n", 2), ("sin", 2), ("cf", 1), ("bias", 1)))
        A = Arena()
        u4 = A(NH * BT).rearrange("p (n t) -> p n t", n=NH)
        gz = A(NH * BT).rearrange("p (n t) -> p n t", n=NH)
        dt = A(NH * BT).rearrange("p (n t) -> p n t", n=NH)
        dtu = A(NH * BT).rearrange("p (n t) -> p n t", n=NH)
        neg_a = A(NH * NS).rearrange("p (n s) -> p n s", n=NH)
        bc_f = A(BT)
        bc_r = A(BT)
        bc_mid = A(BT // 2).bitcast(BF16)
        bc_parts = A(BT // 2).bitcast(BF16)
        diag_d = A(NH * P).rearrange("p (n c) -> p n c", n=NH)
        fade = A(3 * BT).rearrange("p (n t) -> p n t", n=3)
        drive = A(3 * BT).rearrange("p (n t) -> p n t", n=3)
        hist = A(2 * BT).rearrange("p (n t) -> p n t", n=2)
        seen = A(2 * BT).rearrange("p (n t) -> p n t", n=2)
        c_wide = A(2 * BT).rearrange("p (n t) -> p n t", n=2)
        b_wide = A(2 * BT).rearrange("p (n t) -> p n t", n=2)
        yg = fade[:, 0:2]
        dt_e, dt_l = hist, seen
        A = Arena()
        s5_q = A(XH * BT).rearrange("p (h t) -> p h t", h=XH)
        s5_p = A(2 * 4 * KV).rearrange("p (n h k) -> p n h k", n=2, h=4)
        s5_pT = A(2 * 2 * 512).rearrange("p (n k i) -> p n k i", n=2, k=2)
        s5_z = A(2 * 512).rearrange("p (n i) -> p n i", n=2)
        s5_max = A(8).rearrange("p (n h) -> p n h", n=2)
        s5_den = A(8).rearrange("p (n h) -> p n h", n=2)
        s5_rden = A(8).rearrange("p (n h) -> p n h", n=2)
        xpad = A(B * (T + 1)).rearrange("p (b t) -> p b t", b=B)
        mixed = A(2 * BT).rearrange("p (n b t) -> p n b t", n=2, b=B)
        kact = A(BT)
        gate6 = A(BT)
        omm = A(2)

        def within_chunk(tt, c):
            return tt(prod_a[:, :, c % NR].rearrange("p j t i -> p t i j"), att[:, c].unsqueeze(2).to_broadcast([P, C, DH, C]),
                      U[:, c].rearrange("p j i -> p i j").unsqueeze(1).to_broadcast([P, C, DH, C]), ALU.mult)

        def substitute(tt, then, room, first_chunk, end, i):
            n, left, cs = end - first_chunk, C - 1 - i, slice(first_chunk, end)
            terms = room[:, 0:n * left * 2 * DH].rearrange("p (c t n) -> p c t n", c=n, t=left)
            then(tt(terms, low[:, cs, i + 1:, i:i + 1].to_broadcast([P, n, left, 2 * DH]),
                    X[:, cs, i:i + 1, :].to_broadcast([P, n, left, 2 * DH]), ALU.mult))
            return tt(X[:, cs, i + 1:, :], X[:, cs, i + 1:, :], terms, ALU.subtract)

        block = ctx.enter_context(nc.Block())

        @block.sync
        def _(sp):
            soon = 3 * D + 2 * H + 2 + BT // 2
            sp.dma_start(tiles["first"][:, 0:soon], first[:, 0:soon]).then_inc(S("first_in"), 16)
            sp.dma_start(tiles["first"][:, soon:], first[:, soon:]).then_inc(S("second_in"), 16)
            sp.dma_start(xres[:], x).then_inc(S("x_in"), 16)
            sp.dma_start(tiles["early"][:], early).then_inc(S("early_in"), 16)
            sp.dma_start(kv_ctx[0:TC], context).then_inc(S("ctx_in"), 16)
            sp.dma_start(tiles["fold"][:], fold).then_inc(S("fold_in"), 16)
            sp.dma_start(row_in[:], rows.partition_broadcast(P)).then_inc(S("rows_in"), 16)
            sp.dma_start(tiles["late"][:], late).then_inc(S("late_in"), 16)
            for b, end in PARTS:
                sp.wait_ge(S("normed"), normed(6, end))
                sp.dma_start(out[b:end].rearrange("b t c -> t b c"), xrow[:, 0, b:end]).then_inc(S("stored"), 16)
            sp.wait_ge(S("stored"), len(PARTS) * 16)

        @block.vector
        def _(ve):
            count = [0]

            def step(ins):
                count[0] += 1
                ins.then_inc(S("vector_step"), 1)

            def join():
                ve.wait_ge(S("vector_step"), count[0])

            def then(ins):
                step(ins)
                join()

            tt, stt, ts = nc.vector.tensor_tensor, nc.vector.scalar_tensor_tensor, nc.vector.tensor_scalar

            def add_residual(n, g, acc):
                h = slice(g * HB, (g + 1) * HB)
                if n == 1:
                    ve.wait_ge(S("x_in"), 16)
                else:
                    ve.wait_ge(S("residual"), 2 * (n - 2) + g + 1)
                ve.wait_ge(S("projected"), (n - 1) * B + (g + 1) * HB)
                then(tt(xrow[:, n % 2, h], acc.rearrange("p (b c) -> p b c", b=HB), xres[:, h], ALU.add))

            def norms(halves):
                last = None
                for n, g, src, dst, make in halves:
                    if make is not None:
                        make()
                    batches = range(g * HB, (g + 1) * HB)
                    statistics(batches, src)
                    if last:
                        norm_finish(*last)
                    ts(veps[:, g * HB:(g + 1) * HB], mv[:, g * HB:(g + 1) * HB, 1], EPS, None, ALU.add).then_inc(S("var"), 1)
                    last = (n, g, batches, src, dst)
                norm_finish(*last)

            def stage_norms(n, k):
                return [(n, g, xrow[:, n % 2], xrow[:, n % 2], lambda g=g: add_residual(n, g, bank(k + g)))
                        for g in range(2)]

            def statistics(batches, src):
                for b in batches:
                    step(nc.vector.bn_stats(stats[:, b], src[:, b]))
                join()
                for b in batches:
                    step(nc.vector.bn_aggr(mv[:, b], stats[:, b]))
                join()

            def norm_finish(n, part, batches, src, dst):
                ve.wait_ge(S("rstd"), halves(n, part))
                for b in batches:
                    ts(dst[:, b], src[:, b], mv[:, b, 0:1], rstd[:, b:b + 1],
                       ALU.subtract, ALU.mult).then_inc(S("normed"), 1)
                ve.wait_ge(S("normed"), normed(n, batches[-1] + 1))

            for b in range(1, B, 2):
                ve.wait_ge(S("qkv_mm"), b + 1)
                nc.vector.tensor_copy(qkvt[:, :, b], bank(b)[:, 0:3 * D + 2 * H].rearrange("p (n h) -> p n h", h=H)).then_inc(S("qkv_odd"), 1)
            for n in range(2):
                h = slice(n * T, (n + 1) * T)
                ve.wait_ge(S("square"), n + 1)
                nc.vector.tensor_reduce(norm2[:, h], square[:, n * T * DH:(n + 1) * T * DH].rearrange("p (t j) -> p t j", j=DH),
                                        AX.X, ALU.add).then_inc(S("square_sum"), 1)
                ve.wait_ge(S("square_sum"), n + 1)
                ts(norm2[:, h], norm2[:, h], 1e-24, None, ALU.max).then_inc(S("floored"), 1)
            for n, dst in ((0, K), (1, Q)):
                h = slice(n * T, (n + 1) * T)
                ve.wait_ge(S("norm_root"), n + 1)
                then(nc.vector.reciprocal(inv[:, h], norm2[:, h]))
                tt(dst, bank(2 * n, 2).rearrange("p (j t) -> p t j", j=DH),
                   inv[:, h].unsqueeze(2).to_broadcast([P, T, DH]), ALU.mult).then_inc(S("unit"), 1)
            ve.wait_ge(S("gates"), 2)
            ve.wait_ge(S("v_turned"), 1)
            tt(X[:, :, :, 0:DH], bank(4, 2).rearrange("p (j c t) -> p c t j", j=DH, t=C),
               beta.unsqueeze(3).to_broadcast([P, NC, C, DH]), ALU.mult).then_inc(S("beta_v"), 1)
            ve.wait_ge(S("unit"), 2)
            Kc = K.rearrange("p (c t) j -> p c t j", t=C)
            at, rows_k = 0, []
            for t in range(1, C):
                n = NC * t * DH
                rows_k.append(gram_k[:, at:at + n].rearrange("p (c i j) -> p c i j", i=t, j=DH))
                at += n
                step(tt(rows_k[-1], Kc[:, :, t:t + 1, :].to_broadcast([P, NC, t, DH]), Kc[:, :, 0:t, :], ALU.mult))
            join()
            ve.wait_ge(S("cleared"), 4)
            for t in range(1, C):
                step(nc.vector.tensor_reduce(low[:, :, t, 0:t], rows_k[t - 1], AX.X, ALU.add))
            ve.wait_ge(S("decayed"), 4)
            join()
            tt(low, low, bdecay, ALU.mult).then_inc(S("low_ready"), 1)
            ve.wait_ge(S("low_ready"), 1)
            ve.wait_ge(S("w_start"), 1)
            ve.wait_ge(S("beta_v"), 1)
            for i in range(C - 1):
                ins = substitute(tt, then, sub_t, 0, NC - NP, i)
                if i < C - 2:
                    then(ins)
            ins.then_inc(S("solved"), 1)
            ve.wait_ge(S("solved"), 1)
            ve.wait_ge(S("state_zero"), 1)
            ve.wait_ge(S("k_end"), 1)
            need = [0, 0]

            def half_step(g, ins):
                step(ins)
                need[g] = count[0]

            def half_join(g):
                ve.wait_ge(S("vector_step"), need[g])

            rows_i = [slice(0, DH // 2), slice(DH // 2, DH)]
            HI = DH // 2
            for c in range(NC):
                ut, st = u_terms[:, c % 2], s_terms[:, c % 2]
                if c == NC - NP:
                    ve.wait_ge(S("solved_last"), 1)
                if c:
                    for g, h in enumerate(rows_i):
                        ve.wait_ge(S("state_ready"), 2 * (c - 1) + g + 1)
                        half_step(g, tt(ut[:, :, h, 0:DH], X[:, c, :, DH:].unsqueeze(2).to_broadcast([P, C, HI, DH]),
                                        state[:, c, h].unsqueeze(1).to_broadcast([P, C, HI, DH]), ALU.mult))
                    ve.wait_ge(S("u0_laid"), c)
                    for g, h in enumerate(rows_i):
                        half_join(g)
                        nc.vector.tensor_reduce(U[:, c, :, h], ut[:, :, h], AX.X, ALU.add).then_inc(S("u_ready"), 1)
                else:
                    nc.vector.tensor_copy(U[:, c], X[:, c, :, 0:DH]).then_inc(S("u_ready"), 2)
                if c + 1 < NC:
                    for g, h in enumerate(rows_i):
                        ve.wait_ge(S("u_ready"), 2 * c + g + 1 if c else 2)
                        half_step(g, tt(st[:, h, :, 0:C],
                                        U[:, c, :, h].rearrange("p t i -> p i t").unsqueeze(2).to_broadcast([P, HI, DH, C]),
                                        Kend[:, c].rearrange("p t j -> p j t").unsqueeze(1).to_broadcast([P, HI, DH, C]),
                                        ALU.mult))
                    ve.wait_ge(S("s_laid"), c + 1)
                    for g, h in enumerate(rows_i):
                        half_join(g)
                        nc.vector.tensor_reduce(state[:, c + 1, h], st[:, h], AX.X, ALU.add).then_inc(S("state_ready"), 1)
            ve.wait_ge(S("att_ready"), 1)
            ve.wait_ge(S("u_ready"), 2 * NC)
            c = NC - 1
            parts = u_terms[:, (c + 1) % 2].rearrange("p t i j -> p (t i j)")[:, 0:2 * C * DH].rearrange("p (n t i) -> p n t i", n=2, t=C)
            ve.wait_ge(S("o_mm"), NR)
            step(within_chunk(tt, c))
            ve.wait_ge(S("prods"), 2 * c + 1)
            step(nc.vector.tensor_reduce(parts[:, 0], prod_s[:, :, c % NR].rearrange("p j t i -> p t i j"), AX.X, ALU.add))
            join()
            then(nc.vector.tensor_reduce(parts[:, 1], prod_a[:, :, c % NR].rearrange("p j t i -> p t i j"), AX.X, ALU.add))
            tt(osb.rearrange("p (i t) -> p t i", i=DH)[:, c * C:], parts[:, 0], parts[:, 1], ALU.add).then_inc(S("osb_last"), 1)
            for n in range(2):
                ve.wait_ge(S("key0_mm"), n + 1)
                stt(key0[:, n * HB:(n + 1) * HB],
                    bank(n)[:, 0:HB * TC].rearrange("p (b t) -> p b t", b=HB)[:, :, 0:NK], W("bk0"),
                    W("mask_k").unsqueeze(1).to_broadcast([P, HB, NK]), ALU.add, ALU.mult).then_inc(S("key0"), 1)
            ve.wait_ge(S("o_rows_mm"), 2 * 4)
            nc.vector.tensor_copy(ot.rearrange("p (n i) -> p i n", i=DH)[:, 4:],
                                  bank(7).rearrange("p (i n) -> p i n", i=4)).then_inc(S("o_rows_second"), 1)
            for n in range(2):
                ve.wait_ge(S("val0_mm"), n + 1)
                tt(val0[0:NK, n * HB:(n + 1) * HB], bank(2 + n)[0:NK].rearrange("p (b c) -> p b c", b=HB),
                   W("mask_v")[0:NK].unsqueeze(1).to_broadcast([NK, HB, D]), ALU.mult).then_inc(S("val0"), 1)
            ve.wait_ge(S("o_cols_mm"), 2 * HB)
            nc.vector.tensor_copy(otT[:, 512:], bank(5)).then_inc(S("o_cols_second"), 1)
            norms(stage_norms(1, 6))
            ve.wait_ge(S("ctx_in"), 16)
            cr = kv_ctx
            for b in range(B):
                step(nc.vector.bn_stats(cstats[0:TC, b], cr[0:TC, b]))
            join()
            for b in range(B):
                step(nc.vector.bn_aggr(cmv[0:TC, b], cstats[0:TC, b]))
            join()
            ts(cveps[0:TC], cmv[0:TC, :, 1], EPS, None, ALU.add).then_inc(S("ctx_var"), 1)

            def by_head(ap, g):
                return ap[:, g * HB:(g + 1) * HB].unsqueeze(2).to_broadcast([P, HB, NM, H])

            s2m, s2d, s2r = (ap.rearrange("p (b h) -> p b h", h=H) for ap in (s2_max, s2_den, s2_rden))
            s2e, s2p = (ap.rearrange("p (b m h) -> p b m h", b=B, h=H) for ap in (s2_e, s2_p))
            for g in range(2):
                h = slice(g * HB, (g + 1) * HB)
                ve.wait_ge(S("score0"), (g + 1) * HB)
                sc = bank(2 + g).rearrange("p (b n) -> p b n", b=HB)[:, :, 0:NK]
                then(nc.vector.tensor_reduce(s2m[:, h], sc.rearrange("p b (m h) -> p b h m", h=H), AX.X, ALU.max))
                tt(s2e[:, h], sc.rearrange("p b (m h) -> p b m h", h=H), by_head(s2m, g),
                   ALU.subtract).then_inc(S("score0_shift"), 1)
            for g in range(2):
                h = slice(g * HB, (g + 1) * HB)
                ve.wait_ge(S("exp0"), g + 1)
                then(nc.vector.tensor_reduce(s2d[:, h], s2e[:, h].rearrange("p b m h -> p b h m"), AX.X, ALU.add))
                then(nc.vector.reciprocal(s2r[:, h], s2d[:, h]))
                tt(s2p[:, h], s2e[:, h], by_head(s2r, g), ALU.mult).then_inc(S("prob0"), 1)
            ve.wait_ge(S("ctx_rstd"), 1)
            for b in range(B):
                ts(kv_ctx[0:TC, b], cr[0:TC, b], cmv[0:TC, b, 0:1], crstd[0:TC, b:b + 1],
                   ALU.subtract, ALU.mult).then_inc(S("ctx_norm"), 1)
            norms(stage_norms(2, 2))

            def turns_of(k):
                ve.wait_ge(S("angle"), 2 * (k + 1))
                if k >= 2:
                    ve.wait_ge(S("reduced"), k - 1)
                turns = s3_t[:, k % 2]
                then(ts(turns, s3_ang[:, k], 1 / TWO_PI, ROUND, ALU.mult, ALU.add))
                ts(turns, turns, ROUND, TWO_PI, ALU.subtract, ALU.mult).then_inc(S("turns"), 1)

            def clamp(k):
                ang = s3_ang[:, k]
                ve.wait_ge(S("reduced"), k + 1)
                ts(ang, ang, PI_F, -PI_F, ALU.min, ALU.max).then_inc(S("clamped"), 1)

            turns_of(0)
            turns_of(1)
            clamp(0)
            for k in range(NF):
                if k + 2 < NF:
                    turns_of(k + 2)
                elif k + 1 < NF:
                    clamp(k + 1)
                ve.wait_ge(S("sine"), k + 1)
                for m in range(2):
                    f = 2 * (k % 2) + m
                    ang = s3_ang[:, k, m * 512:(m + 1) * 512]
                    stt(ang, ang, s3_cf[:, f:f + 1], bank(s3_banks[k] + m), ALU.mult, ALU.add).then_inc(S("gated"), 1)
                if k + 2 < NF:
                    clamp(k + 1)
            for part in stage_norms(3, 0):
                norms([part])

            for g in range(2):
                h = slice(g * 512, (g + 1) * 512)
                ve.wait_ge(S("xdbl"), g + 1)
                then(nc.vector.tensor_copy(bc_parts[0:32, h], bc_f[0:32, h]))
                then(tt(bc_r[0:32, h], bc_f[0:32, h], bc_parts[0:32, h], ALU.subtract))
                then(nc.vector.tensor_copy(bc_mid[0:32, h], bc_r[0:32, h]))
                step(nc.vector.tensor_copy(bc_parts[32:64, h], bc_mid[0:32, h]))
                then(tt(bc_r[0:32, h], bc_r[0:32, h], bc_mid[0:32, h], ALU.subtract))
                nc.vector.tensor_copy(bc_parts[64:96, h], bc_r[0:32, h]).then_inc(S("bc_parts"), 1)
            for n in range(NH):
                ve.wait_ge(S("dt_exp"), n + 1)
                then(ts(dtu[:, n], dt_e[:, n], 1.0, None, ALU.add))
                ts(dtu[:, n], dtu[:, n], 1.0, None, ALU.subtract).then_inc(S("exp_kept"), 1)
                if n == 0:
                    ve.wait_ge(S("exp_kept"), 1)
                    then(tt(dtu[:, 0], dt_e[:, 0], dtu[:, 0], ALU.subtract))
                    ve.wait_ge(S("dt_relu"), 1)
                    step(tt(dt[:, 0], dt[:, 0], dtu[:, 0], ALU.add))
            for g in range(2):
                ve.wait_ge(S("z_mm"), g + 1)
                nc.vector.tensor_copy(gz[:, 0, g * 512:(g + 1) * 512], bank(2 + g)).then_inc(S("z_first"), 1)
            for n in range(NH):
                if n:
                    ve.wait_ge(S("exp_lost"), 1)
                    ve.wait_ge(S("dt_relu"), 2)
                    step(tt(dt[:, 1], dt[:, 1], dtu[:, 1], ALU.add))
                ve.wait_ge(S("dt_log"), n + 1)
                join()
                tt(dt[:, n], dt[:, n], dt_l[:, n], ALU.add).then_inc(S("dt"), 1)
                if n == 0:
                    ve.wait_ge(S("dt"), 1)
                    then(tt(dtu[:, 0], dt[:, 0], u4[:, 0], ALU.mult))
            def drive_of(k):
                s, n = k // NH, k % NH
                ve.wait_ge(S("b_wide"), s + 1)
                if k == 1:
                    ve.wait_ge(S("dtu_second"), 1)
                if k >= 3:
                    ve.wait_ge(S("scan"), k - 2)
                tt(drive[:, k % 3], dtu[:, n], b_wide[:, s % 2], ALU.mult).then_inc(S("drive"), 1)

            drive_of(0)
            for k in range(NS * NH):
                ve.wait_ge(S("fade"), k + 1)
                ve.wait_ge(S("drive"), k + 1)
                if k >= 2:
                    ve.wait_ge(S("read_out"), k - 1)
                else:
                    ve.wait_ge(S("dt"), k + 1)
                nc.vector.tensor_tensor_scan(hist[:, k % 2], fade[:, k % 3], drive[:, k % 3], 0.0,
                                             ALU.mult, ALU.add).then_inc(S("scan"), 1)
                if k == 0:
                    drive_of(1)
                if k + 2 < NS * NH:
                    drive_of(k + 2)
            ve.wait_ge(S("scan"), NS * NH)
            ve.wait_ge(S("seen_used"), NS * NH - 2)
            for g in range(2):
                h = slice(g * 512, (g + 1) * 512)
                tt(seen[:, 1, h], hist[:, 1, h], c_wide[:, (NS - 1) % 2, h], ALU.mult).then_inc(S("read_last"), 1)
            for g in range(2):
                for n in range(NH):
                    ve.wait_ge(S("y_mm"), NH * g + n + 1)
                    ve.wait_ge(S("gz"), n + 1)
                    y, z = (ap[:, n, g * 512:(g + 1) * 512] for ap in (yg, gz))
                    tt(y, bank(2 * n + g), z, ALU.mult).then_inc(S("y_gated"), 1)

            norms(stage_norms(4, 4))
            for g in range(2):
                ve.wait_ge(S("lat_rstd"), g + 1)
                for b in range(g * HB, (g + 1) * HB):
                    ts(kv_lat[:, b], xrow[:, 0, b], lat_rstd[:, b:b + 1], None, ALU.mult).then_inc(S("normed"), 1)

            def shift(k):
                sim = bank(2 * (k % 2), 2).rearrange("p (h n) -> p h n", h=4)[:, :, 0:KV]
                ve.wait_ge(S("sim"), 4 * (k + 1))
                mx = s5_max[:, k % 2]
                then(nc.vector.tensor_reduce(mx, sim, AX.X, ALU.max))
                ts(mx, mx, -float(D) ** -0.5, None, ALU.mult).then_inc(S("sim_max"), 1)

            def add5(b):
                ve.wait_ge(S("y5_part"), 2 * (b + 1))
                if b == 0:
                    ve.wait_ge(S("residual"), 8)
                tt(xrow[:, 1, b], bank(7)[:, (b % 4) * D:(b % 4 + 1) * D], xres[:, b], ALU.add).then_inc(S("y5_out"), 1)

            def stat5(b):
                ve.wait_ge(S("y5_out"), b + 1)
                then(nc.vector.bn_stats(stats[:, b], xrow[:, 1, b]))
                then(nc.vector.bn_aggr(mv[:, b], stats[:, b]))
                for first, last in PARTS:
                    if b == last - 1:
                        ts(veps[:, first:last], mv[:, first:last, 1], EPS, None, ALU.add).then_inc(S("var"), 1)

            def finish5(part):
                norm_finish(5, part, range(*PARTS[part]), xrow[:, 1], xrow[:, 1])

            def mix(part):
                h = slice(*PARTS[part])
                ve.wait_ge(S("one_minus_mu"), 2)
                ve.wait_ge(S("xpad"), part + 2)
                for n in range(2):
                    step(ts(mixed[:, n, h], xpad[:, h, 0:T], omm[:, n:n + 1], None, ALU.mult))
                join()
                for n, mu in enumerate(("mu_k", "mu_r")):
                    stt(mixed[:, n, h], xpad[:, h, 1:], W(mu), mixed[:, n, h], ALU.mult, ALU.add).then_inc(S("mixed"), 1)

            def gated_residual(part):
                first, last = PARTS[part]
                h = slice(first * T, last * T)
                ve.wait_ge(S("recept"), part + 1)
                ve.wait_ge(S("kv_mm"), last)
                then(tt(gate6[:, h], gate6[:, h], bank(2 * part + 1)[:, 0:(last - first) * T], ALU.mult))
                then(tt(xrow[:, 0, first:last], xrow[:, 1, first:last],
                        gate6[:, h].rearrange("p (b c) -> p b c", c=D), ALU.add))

            shift(0)
            for k in range(2 * B):
                ve.wait_ge(S("exp5"), 4 * (k + 1))
                then(nc.vector.reciprocal(s5_rden[:, k % 2], s5_den[:, k % 2]))
                pr = s5_p[:, k % 2]
                tt(pr, pr, s5_rden[:, k % 2].unsqueeze(2).to_broadcast([P, 4, KV]), ALU.mult).then_inc(S("prob5"), 1)
                if k >= 4 and k % 2 == 0:
                    add5(k // 2 - 2)
                if k + 1 < 2 * B:
                    shift(k + 1)
                if k >= 4 and k % 2 == 0:
                    stat5(k // 2 - 2)
                if k == 2 * HB + 4:
                    finish5(0)
                if k == 2 * B - 1:
                    add5(B - 2)
                ve.wait_ge(S("probT5_mm"), 8 * (k + 1))
                if k >= 2:
                    ve.wait_ge(S("z5_mm"), k - 1)
                nc.vector.tensor_copy(s5_pT[:, k % 2, 1], bank(5)).then_inc(S("probT5_lat"), 1)
            stat5(B - 2)
            mix(0)
            finish5(1)
            add5(B - 1)
            stat5(B - 1)
            finish5(2)
            mix(1)
            mix(2)
            for part, (first, last) in enumerate(PARTS):
                gated_residual(part)
                statistics(range(first, last), xrow[:, 0])
                if part:
                    norm_finish(6, part - 1, range(*PARTS[part - 1]), xrow[:, 0], xrow[:, 0])
                ts(veps[:, first:last], mv[:, first:last, 1], EPS, None, ALU.add).then_inc(S("var"), 1)
            norm_finish(6, part, range(first, last), xrow[:, 0], xrow[:, 0])

        @block.gpsimd
        def _(po):
            count = [0]

            def step(ins):
                count[0] += 1
                ins.then_inc(S("pool_step"), 1)

            def join():
                po.wait_ge(S("pool_step"), count[0])

            def then(ins):
                step(ins)
                join()

            tt, ts = nc.gpsimd.tensor_tensor, nc.gpsimd.tensor_scalar
            nc.gpsimd.memset(low, 0.0).then_inc(S("cleared"), 1)
            nc.gpsimd.memset(att, 0.0).then_inc(S("cleared"), 1)
            nc.gpsimd.memset(mhalf[:], -0.5).then_inc(S("cleared"), 1)
            nc.gpsimd.memset(decay, 0.0).then_inc(S("cleared"), 1)
            po.wait_ge(S("cleared"), 4)
            step(nc.gpsimd.memset(decay.rearrange("p c t i -> p c (t i)")[:, :, 0::C + 1], 1.0))
            nc.gpsimd.memset(state[:, 0], 0.0).then_inc(S("state_zero"), 1)
            join()
            po.wait_ge(S("cleared"), 4)
            po.wait_ge(S("gates"), 2)
            for t in range(1, C):
                ins = tt(decay[:, :, t, 0:t], decay[:, :, t - 1, 0:t],
                         alpha[:, :, t:t + 1].to_broadcast([P, NC, t]), ALU.mult)
                if t < C - 1:
                    then(ins)
            ins.then_inc(S("decayed"), 1)
            po.wait_ge(S("decayed"), 1)
            tt(gcum, decay[:, :, :, 0], alpha[:, :, 0:1].to_broadcast([P, NC, C]), ALU.mult).then_inc(S("decayed"), 1)
            po.wait_ge(S("decayed"), 2)
            then(tt(bgcum, gcum, beta, ALU.mult))
            ts(bgcum, bgcum, -1.0, None, ALU.mult).then_inc(S("decayed"), 1)
            tt(bdecay, decay, beta.unsqueeze(3).to_broadcast([P, NC, C, C]), ALU.mult).then_inc(S("decayed"), 1)
            po.wait_ge(S("decayed"), 4)
            po.wait_ge(S("unit"), 1)
            tt(X[:, :, :, DH:], K.rearrange("p (c t) j -> p c t j", t=C),
               bgcum.unsqueeze(3).to_broadcast([P, NC, C, DH]), ALU.mult).then_inc(S("w_start"), 1)
            po.wait_ge(S("unit"), 2)
            Kc = K.rearrange("p (c t) j -> p c t j", t=C)
            Qc = Q.rearrange("p (c t) j -> p c t j", t=C)
            at = 0
            for t in range(C):
                n = NC * (t + 1) * DH
                tt(gram_q[:, at:at + n].rearrange("p (c i j) -> p c i j", i=t + 1, j=DH),
                   Qc[:, :, t:t + 1, :].to_broadcast([P, NC, t + 1, DH]), Kc[:, :, 0:t + 1, :],
                   ALU.mult).then_inc(S("gram_q"), 1)
                at += n
            po.wait_ge(S("square_sum"), 2)
            po.wait_ge(S("v_turned"), 1)
            tt(Kend, Kc, decay[:, :, C - 1, :].unsqueeze(3).to_broadcast([P, NC, C, DH]), ALU.mult).then_inc(S("k_end"), 1)
            step(tt(Qg, Qc, gcum.unsqueeze(3).to_broadcast([P, NC, C, DH]), ALU.mult))
            po.wait_ge(S("low_ready"), 1)
            po.wait_ge(S("w_start"), 1)
            po.wait_ge(S("beta_v"), 1)
            for i in range(C - 1):
                ins = substitute(tt, then, sub_p, NC - NP, NC, i)
                if i < C - 2:
                    then(ins)
            ins.then_inc(S("solved_last"), 1)
            po.wait_ge(S("att_raw"), C)
            tt(att, att, decay, ALU.mult).then_inc(S("att_ready"), 1)
            po.wait_ge(S("att_ready"), 1)
            join()
            po.wait_ge(S("unit"), 2)
            po.wait_ge(S("solved"), 1)
            for c in range(NC):
                if c:
                    po.wait_ge(S("state_ready"), 2 * c)
                if c >= NR:
                    po.wait_ge(S("o_mm"), c - NR + 1)
                tt(prod_s[:, :, c % NR].rearrange("p j t i -> p t i j"), Qg[:, c].unsqueeze(2).to_broadcast([P, C, DH, DH]),
                   state[:, c].unsqueeze(1).to_broadcast([P, C, DH, DH]), ALU.mult).then_inc(S("prods"), 1)
                if c < NC - 1:
                    po.wait_ge(S("u_ready"), 2 * (c + 1))
                    within_chunk(tt, c).then_inc(S("prods"), 1)

            def power(n, g):
                h = slice(g * HB, (g + 1) * HB)
                po.wait_ge(S("var"), halves(n, g))
                tt(rstd[:, h], veps[:, h], mhalf[:, h], ALU.pow).then_inc(S("rstd"), 1)
            def residual(n, g, bias):
                h = slice(g * HB, (g + 1) * HB)
                po.wait_ge(S("normed"), normed(n - 1, (g + 1) * HB))
                tt(xres[:, h], xrow[:, (n - 1) % 2, h], bias.unsqueeze(1).to_broadcast([P, HB, D]),
                   ALU.add).then_inc(S("residual"), 1)

            po.wait_ge(S("late_in"), 16)
            step(ts(s3_th[:, 0:NF], W("theta"), 1.0, None, ALU.mult))
            step(ts(s3_th[:, NF:], W("theta"), TWO_PI / 4, None, ALU.add))
            join()
            then(ts(s3_n, s3_th, 1 / TWO_PI, ROUND, ALU.mult, ALU.add))
            then(ts(s3_n, s3_n, ROUND, None, ALU.subtract))
            then(ts(s3_sin, s3_n, 6.28125, None, ALU.mult))
            then(tt(s3_th, s3_th, s3_sin, ALU.subtract))
            then(ts(s3_sin, s3_n, TWO_PI - 6.28125, None, ALU.mult))
            then(tt(s3_th, s3_th, s3_sin, ALU.subtract))
            ts(s3_th, s3_th, PI_F, -PI_F, ALU.min, ALU.max).then_inc(S("theta"), 1)
            po.wait_ge(S("theta"), 1)
            then(ts(s3_bias, W("b1"), 0.1, None, ALU.mult))
            tt(s3_bias, s3_bias, s3_th[:, 0:NF], ALU.add).then_inc(S("theta"), 1)
            po.wait_ge(S("rows_in"), 16)
            po.wait_ge(S("fold_bo_sum"), 1)
            tt(fold_bo[:], fold_bo[:], row_in[:, ROWS.index("bo1")], ALU.add).then_inc(S("fold_bo"), 1)
            power(1, 0)
            power(1, 1)
            residual(2, 0, row_in[:, ROWS.index("bo0")])
            residual(2, 1, row_in[:, ROWS.index("bo0")])
            po.wait_ge(S("ctx_var"), 1)
            tt(crstd[0:TC], cveps[0:TC], mhalf[0:TC], ALU.pow).then_inc(S("ctx_rstd"), 1)
            po.wait_ge(S("theta_sin"), 1)
            step(tt(s3_n[:, 0:NF], s3_sin[:, NF:], W("w_re"), ALU.mult))
            step(tt(s3_n[:, NF:], s3_sin[:, 0:NF], W("w_im"), ALU.mult))
            join()
            then(tt(s3_cf, s3_n[:, 0:NF], s3_n[:, NF:], ALU.add))
            then(tt(s3_cf, s3_cf, W("w_im"), ALU.mult))
            ts(s3_cf, s3_cf, 0.1, None, ALU.mult).then_inc(S("gate_factor"), 1)
            power(2, 0)
            power(2, 1)

            def reduce_angle(k):
                po.wait_ge(S("turns"), k + 1)
                tt(s3_ang[:, k], s3_ang[:, k], s3_t[:, k % 2], ALU.subtract).then_inc(S("reduced"), 1)

            for g in range(2):
                residual(3, g, row_in[:, ROWS.index("b2")])
            for k in range(NF):
                reduce_angle(k)
            power(3, 0)
            power(3, 1)
            residual(4, 0, row_in[:, ROWS.index("b_out")])
            residual(4, 1, row_in[:, ROWS.index("b_out")])
            for n in range(NH):
                ts(diag_d[:, n], ident, W("d_skip")[:, n:n + 1], None, ALU.mult).then_inc(S("diag_d"), 1)
            po.wait_ge(S("normed"), normed(3))
            nc.gpsimd.memset(fade.rearrange("p n (b t) -> p (n b) t", t=T)[:, :, 0:1], 0.0).then_inc(S("fade_zero"), 1)
            po.wait_ge(S("ctx_norm"), B)
            po.wait_ge(S("rows_in"), 16)
            then(tt(kv_ctx[0:TC], kv_ctx[0:TC],
                    row_in[0:TC, ROWS.index("g_med")].unsqueeze(1).to_broadcast([TC, B, D]), ALU.mult))
            tt(kv_ctx[0:TC], kv_ctx[0:TC], row_in[0:TC, ROWS.index("be_med")].unsqueeze(1).to_broadcast([TC, B, D]),
               ALU.add).then_inc(S("kv_ctx"), 1)
            po.wait_ge(S("exp_kept"), 2)
            tt(dtu[:, 1], dt_e[:, 1], dtu[:, 1], ALU.subtract).then_inc(S("exp_lost"), 1)
            po.wait_ge(S("dt"), 2)
            tt(dtu[:, 1], dt[:, 1], u4[:, 1], ALU.mult).then_inc(S("dtu_second"), 1)
            for k in range(NS * NH - 1):
                s = k // NH
                po.wait_ge(S("scan"), k + 1)
                po.wait_ge(S("c_wide"), s + 1)
                if k >= 2:
                    po.wait_ge(S("seen_used"), k - 1)
                tt(seen[:, k % 2], hist[:, k % 2], c_wide[:, s % 2], ALU.mult).then_inc(S("read_out"), 1)
            for g in range(2):
                power(4, g)
                h = slice(g * HB, (g + 1) * HB)
                po.wait_ge(S("rstd"), halves(4, g))
                then(tt(lat_rstd[:, h], rstd[:, h], rstd[:, h], ALU.mult))
                then(tt(lat_rstd[:, h], lat_rstd[:, h], mv[:, h, 1], ALU.mult))
                then(ts(lat_rstd[:, h], lat_rstd[:, h], EPS, None, ALU.add))
                tt(lat_rstd[:, h], lat_rstd[:, h], mhalf[:, h], ALU.pow).then_inc(S("lat_rstd"), 1)
            for g in range(2):
                residual(5, g, fold_bo[:])
            po.wait_ge(S("turned"), 4 * B)
            po.wait_ge(S("normed"), normed(7))
            then(tt(kv_lat[:], kv_lat[:], row_in[:, ROWS.index("g_lat")].unsqueeze(1).to_broadcast([P, B, D]), ALU.mult))
            tt(kv_lat[:], kv_lat[:], row_in[:, ROWS.index("be_lat")].unsqueeze(1).to_broadcast([P, B, D]),
               ALU.add).then_inc(S("kv_lat"), 1)
            po.wait_ge(S("normed"), normed(4))
            ts(omm[:, 0:1], W("mu_k"), -1.0, 1.0, ALU.mult, ALU.add).then_inc(S("one_minus_mu"), 1)
            ts(omm[:, 1:2], W("mu_r"), -1.0, 1.0, ALU.mult, ALU.add).then_inc(S("one_minus_mu"), 1)
            nc.gpsimd.memset(xpad[:, :, 0:1], 0.0).then_inc(S("xpad"), 1)
            for n in (5, 6):
                for part, (first, last) in enumerate(PARTS):
                    po.wait_ge(S("var"), halves(n, part))
                    tt(rstd[:, first:last], veps[:, first:last], mhalf[:, first:last], ALU.pow).then_inc(S("rstd"), 1)

        @block.scalar
        def _(ac):
            act = nc.scalar.activation
            tables = [0]

            def table_of(function):
                if tables[0]:
                    ac.wait_ge(S("table"), tables[0])
                act(table[:], ident[:, 0:1], function).then_inc(S("table"), 1)
                tables[0] += 1

            def columns_out(n, g):
                ac.wait_ge(S("turned"), (n - 1) * B + HB * (g + 1))
                act(xcol[:, g * HB:(g + 1) * HB], bank(6 + g).rearrange("p (b t) -> p b t", b=HB),
                    ACT.Copy).then_inc(S("xcol"), 1)

            for b in range(0, B, 2):
                ac.wait_ge(S("qkv_mm"), b + 1)
                act(qkvt[:, :, b], bank(b)[:, 0:3 * D + 2 * H].rearrange("p (n h) -> p n h", h=H), ACT.Copy).then_inc(S("qkv_even"), 1)
            ac.wait_ge(S("gates_turned"), 1)
            for n, dst in enumerate((gates[:, 0:T], gates[:, T:])):
                act(dst, bank(6)[:, n * T:(n + 1) * T], ACT.Sigmoid, bias=W("gate_bias")[:, n:n + 1]).then_inc(S("gates"), 1)
            for n in range(2):
                ac.wait_ge(S("kq_turned"), n + 1)
                act(square[:, n * T * DH:(n + 1) * T * DH].rearrange("p (t j) -> p j t", j=DH),
                    bank(2 * n, 2).rearrange("p (j t) -> p j t", j=DH), ACT.Square).then_inc(S("square"), 1)
            for n in range(2):
                ac.wait_ge(S("floored"), n + 1)
                h = slice(n * T, (n + 1) * T)
                act(norm2[:, h], norm2[:, h], ACT.Sqrt).then_inc(S("norm_root"), 1)
            for g in range(2):
                ac.wait_ge(S("fold_qk_mm"), 4 * (g + 1))
                act(fold_qk[:, 4 * g:4 * g + 4], bank(g).rearrange("p (h c) -> p h c", h=4), ACT.Copy).then_inc(S("fold_qk"), 1)
            ac.wait_ge(S("fold_bo_mm"), 1)
            act(fold_bo[:], bank(5)[:, 0:D], ACT.Copy).then_inc(S("fold_bo_sum"), 1)
            ac.wait_ge(S("fold_bq_mm"), 1)
            act(fold_bq[:], bank(4)[:, 0:XH], ACT.Copy).then_inc(S("fold_bq"), 1)
            ac.wait_ge(S("late_in"), 16)
            act(pick[:], W("pick")[0:96].unsqueeze(2).to_broadcast([96, 2 * NS, P]), ACT.Copy).then_inc(S("pick"), 1)
            ac.wait_ge(S("cleared"), 4)
            at = 0
            for t in range(C):
                k, n = (6, at) if t < C - 1 else (7, 0)
                ac.wait_ge(S("att_mm"), 1 if t < C - 1 else 2)
                act(att[:, :, t, 0:t + 1], bank(k)[:, n:n + NC * (t + 1)].rearrange("p (c i) -> p c i", i=t + 1),
                    ACT.Copy).then_inc(S("att_raw"), 1)
                at += NC * (t + 1)
            def outputs_out(g):
                n = (NR - g) * C
                ac.wait_ge(S("o_mm"), NR * (g + 1) - g)
                act(osb.rearrange("p (i t) -> p i t", i=DH)[:, :, g * NR * C:g * NR * C + n],
                    bank(6 + g)[:, 0:n * DH].rearrange("p (t i) -> p i t", i=DH), ACT.Copy).then_inc(S("osb"), 1)

            ac.wait_ge(S("solved"), 1)
            for c in range(NC - 1):
                if c == NC - 2:
                    outputs_out(0)
                if c == NC - NP:
                    ac.wait_ge(S("solved_last"), 1)
                if c:
                    if c >= 3:
                        ac.wait_ge(S("u_ready"), 2 * (c - 1))
                    act(u_terms[:, c % 2, :, :, DH], X[:, c, :, 0:DH], ACT.Copy).then_inc(S("u0_laid"), 1)
                    ac.wait_ge(S("state_ready"), 2 * c)
                else:
                    ac.wait_ge(S("state_zero"), 1)
                act(s_terms[:, c % 2, :, :, C], state[:, c], ACT.Copy, scale=gcum[:, c, C - 1:C]).then_inc(S("s_laid"), 1)
            ac.wait_ge(S("u_ready"), 2 * (NC - 2))
            act(u_terms[:, (NC - 1) % 2, :, :, DH], X[:, NC - 1, :, 0:DH], ACT.Copy).then_inc(S("u0_laid"), 1)
            table_of(ACT.Exp)
            outputs_out(1)
            ac.wait_ge(S("o_rows_mm"), 4)
            act(ot.rearrange("p (n i) -> p i n", i=DH)[:, 0:4],
                bank(6).rearrange("p (i n) -> p i n", i=4), ACT.Copy).then_inc(S("o_rows"), 1)
            ac.wait_ge(S("o_cols_mm"), HB)
            act(otT[:, 0:512], bank(4), ACT.Copy).then_inc(S("o_cols"), 1)
            for g in range(2):
                columns_out(1, g)
                ac.wait_ge(S("q0_mm"), g + 1)
                act(s2_q[:, g * 512:(g + 1) * 512], bank(g), ACT.Identity, bias=W("bq0")).then_inc(S("q0"), 1)
            for g in range(2):
                e = s2_e[:, g * HB * NK:(g + 1) * HB * NK]
                ac.wait_ge(S("score0_shift"), g + 1)
                act(e, e, ACT.Exp, scale=float(DH) ** -0.5).then_inc(S("exp0"), 1)
            ac.wait_ge(S("theta"), 1)
            act(s3_sin, s3_th, ACT.Sin).then_inc(S("theta_sin"), 1)
            for g in range(2):
                ac.wait_ge(S("probT0_mm"), HB * (g + 1))
                act(s2_pT[0:NK, g * 512:(g + 1) * 512], bank(4 + g)[0:NK], ACT.Copy).then_inc(S("probT0"), 1)
            for g in range(2):
                ac.wait_ge(S("o0_mm"), HB * (g + 1))
                act(s2_oT[:, g * 512:(g + 1) * 512], bank(g), ACT.Identity, bias=W("bv0")).then_inc(S("o0"), 1)

            def angle(k, blocks=(0, 1)):
                for m in blocks:
                    f = 2 * (k % 2) + m
                    ac.wait_ge(S("hid_mm"), 2 * k + m + 1)
                    act(s3_ang[:, k, m * 512:(m + 1) * 512], bank(s3_banks[k] + m), ACT.Identity,
                        bias=s3_bias[:, f:f + 1], scale=0.1).then_inc(S("angle"), 1)

            def rectified(k):
                for m in range(2):
                    f = 2 * (k % 2) + m
                    ac.wait_ge(S("gated"), 2 * k + m + 1)
                    act(s3_act[:, f, k // 2 * 512:(k // 2 + 1) * 512], s3_ang[:, k, m * 512:(m + 1) * 512], ACT.Relu,
                        bias=W("b1")[:, f:f + 1]).then_inc(S("act3"), 1)

            columns_out(2, 0)
            angle(0, (0,))
            columns_out(2, 1)
            angle(0, (1,))
            angle(1)
            angle(2)
            for k in range(NF):
                ac.wait_ge(S("clamped"), k + 1)
                act(s3_ang[:, k], s3_ang[:, k], ACT.Sin).then_inc(S("sine"), 1)
                if k + 3 < NF:
                    angle(k + 3)
                rectified(k)
            table_of(ACT.Silu)
            columns_out(3, 0)
            for g in range(2):
                for n in range(NH):
                    if (g, n) == (0, 1):
                        columns_out(3, 1)
                    ac.wait_ge(S("u_mm"), NH * g + n + 1)
                    act(u4[:, n, g * 512:(g + 1) * 512], bank(2 * g + n), ACT.Silu,
                        bias=W("b_in")[:, n:n + 1]).then_inc(S("u_in"), 1)
            table_of(ACT.Exp)
            for g in range(2):
                ac.wait_ge(S("xdbl_mm"), g + 1)
                act(bc_f[0:32, g * 512:(g + 1) * 512], bank(4 + g)[0:32], ACT.Identity,
                    bias=W("b_x")[0:32]).then_inc(S("xdbl"), 1)
            for n, k in enumerate((6, 0)):
                ac.wait_ge(S("dt_mm"), n + 1)
                act(dt_e[:, n], bank(k, 2), ACT.Abs, bias=W("b_dt")[:, n:n + 1]).then_inc(S("dt_abs"), 1)
                act(dt[:, n], bank(k, 2), ACT.Relu, bias=W("b_dt")[:, n:n + 1]).then_inc(S("dt_relu"), 1)
                ac.wait_ge(S("dt_abs"), n + 1)
                act(dt_e[:, n], dt_e[:, n], ACT.Exp, scale=-1.0).then_inc(S("dt_exp"), 1)
            for n in range(NH):
                ac.wait_ge(S("dt_exp"), n + 1)
                act(dt_l[:, n], dt_e[:, n], ACT.Ln, bias=1.0).then_inc(S("dt_log"), 1)
            for g in range(2):
                ac.wait_ge(S("z_mm"), 2 + g + 1)
                act(gz[:, 1, g * 512:(g + 1) * 512], bank(4 + g), ACT.Copy).then_inc(S("z_second"), 1)
            na = neg_a.rearrange("p n s -> p (n s)")
            act(na, W("a_log"), ACT.Exp).then_inc(S("neg_a"), 1)
            ac.wait_ge(S("neg_a"), 1)
            act(na, na, ACT.Copy, scale=-1.0).then_inc(S("neg_a"), 1)
            ac.wait_ge(S("fade_zero"), 1)
            ac.wait_ge(S("neg_a"), 2)

            def wide(s):
                ac.wait_ge(S("wide_mm"), 2 * s + 1)
                if s >= 2:
                    ac.wait_ge(S("drive"), NH * (s - 1))
                act(b_wide[:, s % 2], bank(4, 2), ACT.Copy).then_inc(S("b_wide"), 1)
                ac.wait_ge(S("wide_mm"), 2 * s + 2)
                if s >= 2:
                    ac.wait_ge(S("read_out"), NH * (s - 1))
                act(c_wide[:, s % 2], bank(6, 2), ACT.Copy).then_inc(S("c_wide"), 1)

            wide(0)
            for s in range(NS):
                for n in range(NH):
                    k = s * NH + n
                    if s == 0:
                        ac.wait_ge(S("dt"), n + 1)
                    if k >= 3:
                        ac.wait_ge(S("scan"), k - 2)
                    act(fade[:, k % 3].rearrange("p (b t) -> p b t", t=T)[:, :, 1:],
                        dt[:, n].rearrange("p (b t) -> p b t", t=T)[:, :, 1:], ACT.Exp,
                        scale=neg_a[:, n, s:s + 1]).then_inc(S("fade"), 1)
                if s + 1 < NS:
                    wide(s + 1)
            ac.wait_ge(S("z_first"), 2)
            ac.wait_ge(S("z_second"), 2)
            for n in range(NH):
                act(gz[:, n], gz[:, n], ACT.Silu, bias=W("b_in")[:, NH + n:NH + n + 1]).then_inc(S("gz"), 1)
            for g in range(2):
                ac.wait_ge(S("ctxT5_mm"), HB * (g + 1))
                act(kvT[:, g * HB:(g + 1) * HB, 0:TC], bank(g).rearrange("p (b t) -> p b t", b=HB)[:, :, 0:TC],
                    ACT.Copy).then_inc(S("kvT_ctx"), 1)
            for g in range(2):
                ac.wait_ge(S("fold_vo_mm"), 4 * (g + 1))
                act(fold_vo[:, 4 * g:4 * g + 4], bank(2 + g).rearrange("p (h c) -> p h c", h=4), ACT.Copy).then_inc(S("fold_vo"), 1)

            def latents_out(g):
                ac.wait_ge(S("turned"), 3 * B + HB * (g + 1))
                act(kvT[:, g * HB:(g + 1) * HB, TC:], bank(6 + g).rearrange("p (b t) -> p b t", b=HB), ACT.Identity,
                    bias=W("be_lat"), scale=W("g_lat")).then_inc(S("kvT_lat"), 1)

            def queries_out(g, k):
                for h in range(XH):
                    ac.wait_ge(S("q5_mm"), g * XH + h + 1)
                    act(s5_q[:, h, g * 512:(g + 1) * 512], bank(k + h % 4), ACT.Identity,
                        bias=fold_bq[:, h:h + 1]).then_inc(S("q5"), 1)

            def exponentials(k):
                ac.wait_ge(S("sim_max"), k + 1)
                if k >= 2:
                    ac.wait_ge(S("probT5_mm"), 8 * (k - 1))
                for h in range(4):
                    act(s5_p[:, k % 2, h], bank(2 * (k % 2), 2).rearrange("p (h n) -> p h n", h=4)[:, h, 0:KV],
                        ACT.Exp, bias=s5_max[:, k % 2, h:h + 1], scale=float(D) ** -0.5,
                        accum_out=s5_den[:, k % 2, h:h + 1]).then_inc(S("exp5"), 1)

            def turned_out(j):
                ac.wait_ge(S("probT5_mm"), 8 * (j + 1))
                if j >= 2:
                    ac.wait_ge(S("z5_mm"), j - 1)
                act(s5_pT[0:TC, j % 2, 0], bank(4)[0:TC], ACT.Copy).then_inc(S("probT5_ctx"), 1)

            def mixed_out(j):
                ac.wait_ge(S("z5_mm"), j + 1)
                if j >= 2:
                    ac.wait_ge(S("y5_part"), j - 1)
                act(s5_z[:, j % 2], bank(6), ACT.Copy).then_inc(S("z5"), 1)

            table_of(ACT.Exp)
            latents_out(0)
            queries_out(0, 0)
            latents_out(1)
            exponentials(0)
            queries_out(1, 4)
            def columns6_out(part):
                first, last = PARTS[part]
                ac.wait_ge(S("turned"), 4 * B + last)
                act(xpad[:, first:last, 1:], bank(2 * part)[:, 0:(last - first) * T].rearrange("p (b t) -> p b t", t=T),
                    ACT.Copy).then_inc(S("xpad"), 1)

            def square6(part):
                first, last = PARTS[part]
                kg = kact[:, first * T:last * T]
                ac.wait_ge(S("k6_mm"), part + 1)
                act(kg, bank(2 * part + 1)[:, 0:(last - first) * T], ACT.Relu).then_inc(S("k_relu"), 1)
                ac.wait_ge(S("k_relu"), part + 1)
                act(kg, kg, ACT.Square).then_inc(S("k_act"), 1)

            def sigmoid6(part):
                first, last = PARTS[part]
                ac.wait_ge(S("r6_mm"), last)
                act(gate6[:, first * T:last * T], bank(2 * part)[:, 0:(last - first) * T], ACT.Sigmoid).then_inc(S("recept"), 1)

            for k in range(2 * B + 2):
                if 1 <= k < 2 * B:
                    exponentials(k)
                if k == 2 * B:
                    mixed_out(k - 2)
                if 1 <= k <= 2 * B:
                    turned_out(k - 1)
                if k >= 2 and k != 2 * B:
                    mixed_out(k - 2)
                if k == 2 * B - 1:
                    columns6_out(0)
            table_of(ACT.Sigmoid)
            square6(0)
            columns6_out(1)
            columns6_out(2)
            sigmoid6(0)
            for part in (1, 2):
                square6(part)
                sigmoid6(part)

        @block.tensor
        def _(pe):
            mm, turn = nc.tensor.matmul, nc.tensor.transpose
            xT = W("xT").rearrange("p (b t) -> p b t", b=B)

            def stay_awake(n, k):
                for _ in range(n):
                    mm(bank(k)[:, 0:256], ident, W("xT")[:, 0:256], start=True, stop=True)

            def turn_half(n, g):
                for b in range(g * HB, (g + 1) * HB):
                    pe.wait_ge(S("normed"), normed(n, b + 1))
                    turn(bank(6, 2)[:, b * T:(b + 1) * T], xrow[:, n % 2, b], ident).then_inc(S("turned"), 1)

            pe.wait_ge(S("first_in"), 16)
            for b in range(B):
                if b == HB:
                    pe.wait_ge(S("second_in"), 16)
                mm(bank(b)[:, 0:3 * D + 2 * H], xT[:, b], W("w_qkvgb"), start=True, stop=True).then_inc(S("qkv_mm"), 1)
            pe.wait_ge(S("qkv_even"), B // 2)
            pe.wait_ge(S("qkv_odd"), B // 2)
            for m in range(2):
                ins = turn(bank(6)[:, m * T:(m + 1) * T], qkvt[:, 3 * DH + m].rearrange("p b h -> p (b h)"), ident)
            ins.then_inc(S("gates_turned"), 1)
            for n, (k, sem) in enumerate(((1, "kq_turned"), (0, "kq_turned"), (2, "v_turned"))):
                for j in range(DH):
                    ins = turn(bank(2 * n, 2)[:, j * T:(j + 1) * T],
                               qkvt[:, k * DH + j].rearrange("p b h -> p (b h)"), ident)
                ins.then_inc(S(sem), 1)
            pe.wait_ge(S("fold_in"), 16)
            pe.wait_ge(S("unit"), 2)
            fq, fk = (W(n).rearrange("p (h c) -> p h c", h=XH) for n in ("wq1T", "wk1T"))
            fv, fo = (W(n).rearrange("p (h c) -> p h c", h=XH) for n in ("wv1T", "wo1"))
            for h in range(XH):
                mm(bank(0, 2)[:, h * D:(h + 1) * D], fq[:, h], fk[:, h], start=True, stop=True).then_inc(S("fold_qk_mm"), 1)
            pe.wait_ge(S("beta_v"), 1)
            for h in range(XH):
                ins = mm(bank(4)[:, h:h + 1], fk[:, h], W("bq1")[:, h:h + 1], start=True, stop=True)
            ins.then_inc(S("fold_bq_mm"), 1)
            for h in range(XH):
                ins = mm(bank(5)[:, 0:D], W("bv1")[:, h:h + 1].to_broadcast([P, P]), fo[:, h],
                         start=(h == 0), stop=(h == XH - 1))
            ins.then_inc(S("fold_bo_mm"), 1)
            pe.wait_ge(S("fold_qk"), 2)
            pe.wait_ge(S("early_in"), 16)
            cT = W("ctxT").rearrange("p (b t) -> p b t", b=B)
            for g in range(2):
                mm(bank(g)[:, 0:HB * TC], W("wk0"), W("ctxT")[:, g * HB * TC:(g + 1) * HB * TC],
                   start=True, stop=True).then_inc(S("key0_mm"), 1)
            for g in range(2):
                for b in range(g * HB, (g + 1) * HB):
                    ins = mm(bank(2, 2)[0:NK, b * D:(b + 1) * D], cT[:, b, 0:NK], W("wv0"), start=True, stop=True)
                ins.then_inc(S("val0_mm"), 1)
            pe.wait_ge(S("gates"), 2)
            cells = NC * C * (C - 1) // 2
            gram_j = gram_q.rearrange("p (n j) -> p n j", j=DH)
            for k, (at, end) in enumerate(((0, cells), (cells, cells + NC * C))):
                pe.wait_ge(S("gram_q"), C - 1 + k)
                for j in range(DH):
                    ins = mm(bank(6 + k)[:, 0:end - at], ident, gram_j[:, at:end, j], start=(j == 0), stop=(j == DH - 1))
                ins.then_inc(S("att_mm"), 1)
            pe.wait_ge(S("att_raw"), C)
            for c in range(0, NC - 1, 2):
                n_c = min(2, NC - 1 - c)
                at = c % NR * C * DH
                for n, pr in enumerate((prod_s, prod_a)):
                    pe.wait_ge(S("prods"), 2 * (c + n_c - 1) + n + 1)
                    for j in range(C):
                        ins = mm(bank(6 + c // NR)[:, at:at + n_c * C * DH], ident,
                                 pr[:, j, c % NR:c % NR + n_c].rearrange("p c t i -> p (c t i)"),
                                 start=(n == 0 and j == 0), stop=(n == 1 and j == C - 1))
                ins.then_inc(S("o_mm"), n_c)
            pe.wait_ge(S("osb"), 2)
            pe.wait_ge(S("osb_last"), 1)
            for i in range(DH):
                turn(bank(6, 2)[:, i * P:(i + 1) * P], osb[:, i * T:(i + 1) * T], ident).then_inc(S("o_rows_mm"), 1)
            pe.wait_ge(S("fold_bq"), 1)
            pe.wait_ge(S("fold_bo_sum"), 1)
            pe.wait_ge(S("o_rows"), 1)
            pe.wait_ge(S("o_rows_second"), 1)
            for b in range(B):
                turn(bank(4, 2)[:, b * T:(b + 1) * T], ot[:, b * D:(b + 1) * D], ident).then_inc(S("o_cols_mm"), 1)
            for b in range(B):
                if b % HB == 0:
                    pe.wait_ge(S("o_cols_second" if b else "o_cols"), 1)
                mm(bank(6, 2)[:, b * D:(b + 1) * D], otT[:, b * T:(b + 1) * T], W("w_out0"),
                   start=True, stop=True).then_inc(S("projected"), 1)
            stay_awake(8, 4)
            pe.wait_ge(S("key0"), 2)
            pe.wait_ge(S("val0"), 2)
            for g in range(2):
                turn_half(1, g)
                pe.wait_ge(S("xcol"), 0 + g + 1)
                mm(bank(g), W("wq0"), xcol[:, g * HB:(g + 1) * HB], start=True, stop=True).then_inc(S("q0_mm"), 1)
            for b in range(B):
                if b % HB == 0:
                    pe.wait_ge(S("q0"), b // HB + 1)
                mm(bank(2, 2)[:, b * T:b * T + NK], s2_q[:, b * T:(b + 1) * T], key0[:, b],
                   start=True, stop=True).then_inc(S("score0"), 1)
            stay_awake(6, 0)
            for b in range(B):
                if b % HB == 0:
                    pe.wait_ge(S("prob0"), b // HB + 1)
                turn(bank(4, 2)[0:NK, b * T:(b + 1) * T], s2_p[:, b * NK:(b + 1) * NK], ident).then_inc(S("probT0_mm"), 1)
            for b in range(B):
                if b % HB == 0:
                    pe.wait_ge(S("probT0"), b // HB + 1)
                mm(bank(0, 2)[:, b * T:(b + 1) * T], val0[0:NK, b], s2_pT[0:NK, b * T:(b + 1) * T],
                   start=True, stop=True).then_inc(S("o0_mm"), 1)
            for b in range(B):
                if b % HB == 0:
                    pe.wait_ge(S("o0"), b // HB + 1)
                mm(bank(2, 2)[:, b * D:(b + 1) * D], s2_oT[:, b * T:(b + 1) * T], W("wo0"),
                   start=True, stop=True).then_inc(S("projected"), 1)
            stay_awake(8, 4)
            w2 = W("w2").rearrange("p (f c) -> p f c", f=NF)
            def hidden(k, blocks=(0, 1)):
                g = k // 2
                pe.wait_ge(S("xcol"), 2 + g + 1)
                for m in blocks:
                    f = 2 * (k % 2) + m
                    mm(bank(s3_banks[k] + m), W("w1")[:, f * P:(f + 1) * P], xcol[:, g * HB:(g + 1) * HB],
                       start=True, stop=True).then_inc(S("hid_mm"), 1)

            def project3(g):
                pe.wait_ge(S("act3"), NF * (g + 1))
                for b in range(g * HB, (g + 1) * HB):
                    for f in range(NF):
                        ins = mm(bank(0, 2)[:, b * D:(b + 1) * D], s3_act[:, f, b * T:(b + 1) * T], w2[:, f],
                                 start=(f == 0), stop=(f == NF - 1))
                    ins.then_inc(S("projected"), 1)

            turn_half(2, 0)
            hidden(0, (0,))
            turn_half(2, 1)
            hidden(0, (1,))
            for k in range(1, NF):
                hidden(k)
            pe.wait_ge(S("gated"), 2)
            stay_awake(6, 0)
            project3(0)
            project3(1)
            stay_awake(6, 2)
            def project4(n, g, k, sem):
                mm(bank(k), W("w_in")[:, n * P:(n + 1) * P], xcol[:, g * HB:(g + 1) * HB],
                   start=True, stop=True).then_inc(S(sem), 1)

            turn_half(3, 0)
            for g in range(2):
                pe.wait_ge(S("xcol"), 4 + g + 1)
                for n in range(NH):
                    if (g, n) == (0, 1):
                        turn_half(3, 1)
                    project4(n, g, 2 * g + n, "u_mm")
            wx = W("w_x").rearrange("p (n s) -> p n s", n=NH)
            for g in range(2):
                pe.wait_ge(S("u_in"), NH * (g + 1))
                for n in range(NH):
                    ins = mm(bank(4 + g)[0:32], wx[:, n], u4[:, n, g * 512:(g + 1) * 512], start=(n == 0), stop=(n == NH - 1))
                ins.then_inc(S("xdbl_mm"), 1)
            wdt = W("w_dt").rearrange("p (n d) -> p n d", n=NH)
            for m, k in enumerate((6, 0)):
                for g in range(2):
                    for n in range(NH):
                        ins = mm(bank(k + g), wdt[:, n, m * P:(m + 1) * P], u4[:, n, g * 512:(g + 1) * 512],
                                 start=(n == 0), stop=(n == NH - 1))
                ins.then_inc(S("dt_mm"), 1)
            pe.wait_ge(S("xdbl"), 2)
            for n in range(NH):
                for g in range(2):
                    project4(NH + n, g, 2 + 2 * n + g, "z_mm")
            def widen(s):
                for n, sem in enumerate(("b_wide", "c_wide")):
                    if s:
                        pe.wait_ge(S(sem), s)
                    for g in range(2):
                        ins = mm(bank(4 + 2 * n + g), pick[:, n * NS + s], bc_parts[0:96, g * 512:(g + 1) * 512],
                                 start=True, stop=True)
                    ins.then_inc(S("wide_mm"), 1)

            pe.wait_ge(S("diag_d"), NH)
            for n in range(NH):
                if n:
                    pe.wait_ge(S("z_first"), 2)
                else:
                    pe.wait_ge(S("dt_relu"), 2)
                for g in range(2):
                    mm(bank(2 * n + g), diag_d[:, n], u4[:, n, g * 512:(g + 1) * 512], start=True, stop=False)
            pe.wait_ge(S("bc_parts"), 2)
            pe.wait_ge(S("pick"), 1)
            pe.wait_ge(S("z_second"), 2)
            widen(0)
            widen(1)
            for s in range(NS):
                if s + 2 < NS:
                    widen(s + 2)
                if s + 1 < NS:
                    for n in range(NH):
                        k = s * NH + n
                        pe.wait_ge(S("read_out"), k + 1)
                        for g in range(2):
                            ins = mm(bank(2 * n + g), ident, seen[:, k % 2, g * 512:(g + 1) * 512],
                                     start=False, stop=False)
                        ins.then_inc(S("seen_used"), 1)
            for g in range(2):
                for n in range(NH):
                    k = (NS - 1) * NH + n
                    if n:
                        pe.wait_ge(S("read_last"), g + 1)
                    else:
                        pe.wait_ge(S("read_out"), k + 1)
                    mm(bank(2 * n + g), ident, seen[:, k % 2, g * 512:(g + 1) * 512],
                       start=False, stop=True).then_inc(S("y_mm"), 1)
            wo = W("w_out").rearrange("p (n c) -> p n c", n=NH)
            for b in range(B):
                if b % HB == 0:
                    pe.wait_ge(S("y_gated"), NH * (b // HB + 1))
                for n in range(NH):
                    ins = mm(bank(4, 2)[:, b * D:(b + 1) * D], yg[:, n, b * T:(b + 1) * T], wo[:, n],
                             start=(n == 0), stop=(n == NH - 1))
                ins.then_inc(S("projected"), 1)
            pe.wait_ge(S("y_gated"), 2 * NH)
            pe.wait_ge(S("kv_ctx"), 1)
            for b in range(B):
                turn(bank(0, 2)[:, b * T:b * T + TC], kv_ctx[0:TC, b], ident[0:TC, 0:TC]).then_inc(S("ctxT5_mm"), 1)
            for h in range(XH):
                mm(bank(2, 2)[:, h * D:(h + 1) * D], fv[:, h], fo[:, h], start=True, stop=True).then_inc(S("fold_vo_mm"), 1)

            stay_awake(10, 6)

            def turn_latents(g):
                for b in range(g * HB, (g + 1) * HB):
                    pe.wait_ge(S("normed"), normed(7, b + 1))
                    turn(bank(6, 2)[:, b * T:(b + 1) * T], kv_lat[:, b], ident).then_inc(S("turned"), 1)

            def queries(g, k):
                pe.wait_ge(S("kvT_lat"), g + 1)
                for h in range(XH):
                    if h >= 4:
                        pe.wait_ge(S("q5"), g * XH + h - 3)
                    mm(bank(k + h % 4), fold_qk[:, h], kvT[:, g * HB:(g + 1) * HB, TC:],
                       start=True, stop=True).then_inc(S("q5_mm"), 1)

            turn_latents(0)
            pe.wait_ge(S("kvT_ctx"), 2)
            pe.wait_ge(S("fold_vo"), 2)
            queries(0, 0)
            turn_latents(1)

            def similar(k):
                b, g = k // 2, k % 2
                if k >= 2:
                    pe.wait_ge(S("exp5"), 4 * (k - 1))
                for h in range(4):
                    mm(bank(2 * (k % 2), 2)[:, h * 256:h * 256 + KV], s5_q[:, 4 * g + h, b * T:(b + 1) * T], kvT[:, b],
                       start=True, stop=True).then_inc(S("sim"), 1)

            def turn6(part):
                first, last = PARTS[part]
                for b in range(first, last):
                    pe.wait_ge(S("normed"), normed(5, b + 1))
                    turn(bank(2 * part)[:, (b - first) * T:(b - first + 1) * T], xrow[:, 1, b], ident).then_inc(S("turned"), 1)

            def mix6(part):
                first, last = PARTS[part]
                pe.wait_ge(S("mixed"), 2 * part + 1)
                mm(bank(2 * part + 1)[:, 0:(last - first) * T], W("w_k"), mixed[:, 0, first:last],
                   start=True, stop=True).then_inc(S("k6_mm"), 1)
                pe.wait_ge(S("mixed"), 2 * part + 2)
                for b in range(first, last):
                    mm(bank(2 * part)[:, (b - first) * D:(b - first + 1) * D], mixed[:, 1, b], W("w_r"),
                       start=True, stop=True).then_inc(S("r6_mm"), 1)

            def out6(part):
                first, last = PARTS[part]
                pe.wait_ge(S("k_act"), part + 1)
                for b in range(first, last):
                    mm(bank(2 * part + 1)[:, (b - first) * D:(b - first + 1) * D], kact[:, b * T:(b + 1) * T], W("w_v"),
                       start=True, stop=True).then_inc(S("kv_mm"), 1)

            def turn_probabilities(k):
                pe.wait_ge(S("prob5"), k + 1)
                if k:
                    pe.wait_ge(S("probT5_ctx"), k)
                    pe.wait_ge(S("probT5_lat"), k)
                for h in range(4):
                    turn(bank(4)[0:TC, h * T:(h + 1) * T], s5_p[:, k % 2, h, 0:TC], ident).then_inc(S("probT5_mm"), 1)
                    turn(bank(5)[:, h * T:(h + 1) * T], s5_p[:, k % 2, h, TC:], ident).then_inc(S("probT5_mm"), 1)

            def mix_context(j):
                b = j // 2
                if j == 0:
                    pe.wait_ge(S("kv_lat"), 1)
                    pe.wait_ge(S("kv_ctx"), 1)
                else:
                    pe.wait_ge(S("z5"), j)
                pe.wait_ge(S("probT5_ctx"), j + 1)
                mm(bank(6), kv_ctx[0:TC, b], s5_pT[0:TC, j % 2, 0], start=True, stop=False)
                pe.wait_ge(S("probT5_lat"), j + 1)
                mm(bank(6), kv_lat[:, b], s5_pT[:, j % 2, 1], start=False, stop=True).then_inc(S("z5_mm"), 1)

            pe.wait_ge(S("q5"), XH)
            similar(0)
            similar(1)
            queries(1, 4)
            pe.wait_ge(S("q5"), 2 * XH)
            for k in range(2 * B + 2):
                if 1 <= k < 2 * B - 1:
                    similar(k + 1)
                if k >= 2:
                    j = k - 2
                    b, g = j // 2, j % 2
                    pe.wait_ge(S("z5"), j + 1)
                    if g == 0 and b:
                        pe.wait_ge(S("y5_out"), b)
                    for h in range(4):
                        ins = mm(bank(7)[:, (b % 4) * D:(b % 4 + 1) * D], s5_z[:, j % 2, h * T:(h + 1) * T],
                                 fold_vo[:, 4 * g + h], start=(g == 0 and h == 0), stop=(g == 1 and h == 3))
                    ins.then_inc(S("y5_part"), 1)
                if k == 2 * B - 1:
                    mix_context(k - 1)
                if k < 2 * B:
                    turn_probabilities(k)
                if 1 <= k <= 2 * B and k != 2 * B - 1:
                    mix_context(k - 1)
                if k == 2 * B - 2:
                    turn6(0)
            mix6(0)
            turn6(1)
            out6(0)
            turn6(2)
            for part in (1, 2):
                mix6(part)
                out6(part)


_INS = ["first", "x", "early", "context", "fold", "late", "rows"]


def layout(i):
    i = {k: np.asarray(v) for k, v in i.items()}

    def col(v):
        return v.reshape(-1, P).T

    def blocks(w):
        return w.reshape(-1, P, w.shape[-1]).transpose(1, 0, 2).reshape(P, -1)

    def tall(w):
        out = np.zeros((P,) + w.shape[1:], w.dtype)
        out[:w.shape[0]] = w
        return out

    def heads_t(w):
        return w.reshape(D, XH, D).transpose(2, 1, 0).reshape(D, -1)

    ch, tok = np.arange(P), np.arange(P)
    mask = (ch[:, None] // DH == tok[None, :] % H).astype(np.float32)
    v = {
        "xT": i["x"].transpose(2, 0, 1).reshape(P, BT),
        "w_qkvgb": np.concatenate([i["L0_attn_Wqkv"].reshape(3, H, DH, D).transpose(3, 0, 2, 1).reshape(D, 3 * D), i["L0_attn_Wg"].T, i["L0_attn_Wb"].T], 1),
        "gate_bias": np.stack([np.tile(i["L0_attn_bg"], B), np.tile(i["L0_attn_bb"], B)], 1),
        "ident": np.eye(P, dtype=np.float32),
        "w_out0": i["L0_attn_Wout"].T,
        "wq0": i["L0_xattn_Wq"].T, "wk0": i["L0_xattn_Wk"].T, "wv0": i["L0_xattn_Wv"].T, "wo0": i["L0_xattn_Wo"].T,
        "bq0": col(i["L0_xattn_bq"]), "bk0": col(i["L0_xattn_bk"]), "bv0": col(i["L0_xattn_bv"]),
        "mask_k": mask[:, :NK], "mask_v": mask.T,
        "ctxT": i["ctx_1024"].transpose(2, 0, 1).reshape(P, B * TC),
        "wq1T": heads_t(i["L1_xattn_Wq"]),
        "wk1T": heads_t(i["L1_xattn_Wkv"][:, :XH * D]), "wv1T": heads_t(i["L1_xattn_Wkv"][:, XH * D:]),
        "wo1": blocks(i["L1_xattn_Wo"]), "bq1": col(i["L1_xattn_bq"]), "bv1": col(i["L1_xattn_bkv"][XH * D:]),
        "w1": i["L0_ffn_W1"], "b1": col(i["L0_ffn_b1"]), "theta": col(i["L0_ffn_quantum_phases"]),
        "w_re": col(i["L0_ffn_quantum_weights_real"]), "w_im": col(i["L0_ffn_quantum_weights_imag"]),
        "w2": blocks(i["L0_ffn_W2"]),
        "w_in": i["L1_attn_W_in"], "b_in": col(i["L1_attn_b_in"]), "w_x": blocks(i["L1_attn_W_x"]),
        "w_dt": blocks(i["L1_attn_W_dt"]), "b_dt": col(i["L1_attn_b_dt"]), "w_out": blocks(i["L1_attn_W_out"]),
        "a_log": blocks(i["L1_attn_A_log"]), "d_skip": col(i["L1_attn_D_param"]),
        "b_x": tall(i["L1_attn_b_x"][:, None]),
        "g_lat": col(i["L1_xattn_gamma_lat"]), "be_lat": col(i["L1_xattn_beta_lat"]),
        "w_r": i["L1_ffn_W_r"].T, "w_k": i["L1_ffn_W_k"].T, "w_v": i["L1_ffn_W_v"].T,
        "mu_r": col(i["L1_ffn_mu_r"]), "mu_k": col(i["L1_ffn_mu_k"]),
        "pick": tall(np.tile(np.eye(2 * NS, dtype=np.float32), (3, 1))),
    }
    packs = {p: np.ascontiguousarray(np.concatenate([v[n] for n, _ in cols], 1)) for p, cols in PACKS.items()}
    packs["x"] = i["x"].transpose(1, 0, 2)
    packs["context"] = i["ctx_1024"].transpose(1, 0, 2)
    packs["rows"] = np.stack([i["L0_xattn_bo"], i["L0_ffn_b2"], i["L1_attn_b_out"], i["L1_xattn_bo"],
                              i["L1_xattn_gamma_media"], i["L1_xattn_beta_media"],
                              i["L1_xattn_gamma_lat"], i["L1_xattn_beta_lat"]])
    return packs


def kernel(**inputs):
    import concourse.bacc as bacc
    from concourse.bass_utils import run_bass_kernel_spmd

    nc = bacc.Bacc("TRN2", target_bir_lowering=False, num_devices=1)
    packs = layout(inputs)
    arrays, args = {}, []
    for name in _INS:
        a = np.ascontiguousarray(packs[name])
        arrays[f"in_{name}_dram"] = a
        args.append(nc.dram_tensor(f"in_{name}_dram", a.shape, mybir.dt.from_np(a.dtype), kind="ExternalInput").ap())
    args.append(nc.dram_tensor("out_0_dram", (B, T, D), F32, kind="ExternalOutput").ap())
    decoder(nc, *args)
    r = run_bass_kernel_spmd(nc, [arrays], core_ids=[0])
    return r.results[0]["out_0_dram"]
```
